# Optimizing a Trainium2 kernel written in Bass

```python
import numpy as np
import jax
import jax.numpy as jnp

def _softmax(x, axis=-1):
    return jax.nn.softmax(x, axis=axis)

def _gelu(x):
    return jax.nn.gelu(x, approximate=True)

def _silu(x):
    return jax.nn.silu(x)

def _sigmoid(x):
    return jax.nn.sigmoid(x)

def _layernorm(x, axis=-1, eps=1e-05):
    m = jnp.mean(x, axis=axis, keepdims=True)
    v = jnp.var(x, axis=axis, keepdims=True)
    return (x - m) / jnp.sqrt(v + eps)

def _scatter_add(tgt, idx, src, axis=0):
    return tgt.at[idx].add(src)

def _segment_sum(src, seg, n):
    return jax.ops.segment_sum(src, seg, n)
kernel_name = 'mk_seq_preln_d1_jaxref_r4_b9e82a'

def setup_inputs(seed: int=0):
    np.random.seed(seed)
    _w = jnp.asarray

    def _L0_attn_setup():
        import jax, jax.numpy as jnp
        import numpy as np
        BSZ, SEQ, DZ = (4, 512, 256)
        C, R = (16, 64)
        SCALE = 0.03125
        REG_H = 1.0
        key = jax.random.key(seed)
        k1, k2, k3 = jax.random.split(key, 3)
        qz = jax.random.normal(k1, (BSZ, SEQ, DZ), dtype=jnp.float32)
        ternary_factor_u = jax.random.normal(k2, (C * R, DZ), dtype=jnp.float32) * 0.02
        ternary_factor_v = jax.random.normal(k3, (C * R, DZ), dtype=jnp.float32) * 0.02
        return {'qz': qz, 'ternary_factor_u': ternary_factor_u, 'ternary_factor_v': ternary_factor_v}
    _L0_attn_in = _L0_attn_setup()

    def _L0_ffn_setup():
        import jax, jax.numpy as jnp
        import numpy as np
        D = 256
        H = 16
        FF = 1024
        E = 8
        K = 2
        EH = 256
        B, S = (2, 512)
        EPS = 1e-05

        def rmsnorm(x, w):
            v = jnp.mean(jnp.square(x), axis=-1, keepdims=True)
            return x * jax.lax.rsqrt(v + EPS) * w

        def _dense_path(x, wq, wk, wv, wo, w1, w2, w3, attn_norm_w, ff_norm_w):
            b, s, d = x.shape
            hd = d // H
            q = (x @ wq).reshape(b, s, H, hd)
            k = (x @ wk).reshape(b, s, H, hd)
            v = (x @ wv).reshape(b, s, H, hd)
            scores = jnp.einsum('bqhd,bkhd->bhqk', q, k) / np.sqrt(hd).astype(np.float32)
            causal = jnp.tril(jnp.ones((s, s), bool))
            scores = jnp.where(causal, scores, jnp.finfo(scores.dtype).min)
            attn = jax.nn.softmax(scores, axis=-1)
            o = jnp.einsum('bhqk,bkhd->bqhd', attn, v).reshape(b, s, d)
            h = x + rmsnorm(o @ wo, attn_norm_w)
            ffn = jax.nn.silu(h @ w1) * (h @ w3) @ w2
            return h + rmsnorm(ffn, ff_norm_w)

        def _sparse_path(x, router_w, ew1, ew2, ew3, moe_norm_w):
            b, s, d = x.shape
            xt = x.reshape(-1, d)
            probs = jax.nn.softmax(xt @ router_w, axis=-1)
            topw, topi = jax.lax.top_k(probs, K)
            g = jax.nn.silu(jnp.einsum('td,edh->eth', xt, ew1)) * jnp.einsum('td,edh->eth', xt, ew3)
            eo = jnp.einsum('eth,ehd->ted', g, ew2)
            sel = jnp.take_along_axis(eo, topi[:, :, None], axis=1)
            moe_out = jnp.sum(topw[:, :, None] * sel, axis=1).reshape(b, s, d)
            return rmsnorm(moe_out, moe_norm_w)
        key = jax.random.key(seed)
        ks = jax.random.split(key, 16)
        s = 0.02
        return {'x': jax.random.normal(ks[0], (B, S, D), jnp.float32), 'wq': jax.random.normal(ks[1], (D, D), jnp.float32) * s, 'wk': jax.random.normal(ks[2], (D, D), jnp.float32) * s, 'wv': jax.random.normal(ks[3], (D, D), jnp.float32) * s, 'wo': jax.random.normal(ks[4], (D, D), jnp.float32) * s, 'w1': jax.random.normal(ks[5], (D, FF), jnp.float32) * s, 'w2': jax.random.normal(ks[6], (FF, D), jnp.float32) * s, 'w3': jax.random.normal(ks[7], (D, FF), jnp.float32) * s, 'attn_norm_w': jnp.ones((D,), jnp.float32), 'ff_norm_w': jnp.ones((D,), jnp.float32), 'moe_norm_w': jnp.ones((D,), jnp.float32), 'router_w': jax.random.normal(ks[8], (D, E), jnp.float32) * s, 'ew1': jax.random.normal(ks[9], (E, D, EH), jnp.float32) * s, 'ew2': jax.random.normal(ks[10], (E, EH, D), jnp.float32) * s, 'ew3': jax.random.normal(ks[11], (E, D, EH), jnp.float32) * s}
    _L0_ffn_in = _L0_ffn_setup()
    _d = {'L0_attn_qz': _L0_attn_in['qz'], 'L0_attn_ternary_factor_u': _L0_attn_in['ternary_factor_u'], 'L0_attn_ternary_factor_v': _L0_attn_in['ternary_factor_v'], 'L0_ffn_wq': _L0_ffn_in['wq'], 'L0_ffn_wk': _L0_ffn_in['wk'], 'L0_ffn_wv': _L0_ffn_in['wv'], 'L0_ffn_wo': _L0_ffn_in['wo'], 'L0_ffn_w1': _L0_ffn_in['w1'], 'L0_ffn_w2': _L0_ffn_in['w2'], 'L0_ffn_w3': _L0_ffn_in['w3'], 'L0_ffn_attn_norm_w': _L0_ffn_in['attn_norm_w'], 'L0_ffn_ff_norm_w': _L0_ffn_in['ff_norm_w'], 'L0_ffn_moe_norm_w': _L0_ffn_in['moe_norm_w'], 'L0_ffn_router_w': _L0_ffn_in['router_w'], 'L0_ffn_ew1': _L0_ffn_in['ew1'], 'L0_ffn_ew2': _L0_ffn_in['ew2'], 'L0_ffn_ew3': _L0_ffn_in['ew3']}
    _x0 = _d['L0_attn_qz']
    _d['L0_attn_qz'] = jax.random.normal(jax.random.fold_in(jax.random.key(seed), 1), (4, 1024, 256), dtype=_x0.dtype)
    del _x0
    return _d

def reference(L0_attn_qz, L0_attn_ternary_factor_u, L0_attn_ternary_factor_v, L0_ffn_wq, L0_ffn_wk, L0_ffn_wv, L0_ffn_wo, L0_ffn_w1, L0_ffn_w2, L0_ffn_w3, L0_ffn_attn_norm_w, L0_ffn_ff_norm_w, L0_ffn_moe_norm_w, L0_ffn_router_w, L0_ffn_ew1, L0_ffn_ew2, L0_ffn_ew3):

    def _L0_attn_ref(qz, ternary_factor_u, ternary_factor_v):
        import jax, jax.numpy as jnp
        import numpy as np
        BSZ, SEQ, DZ = (4, 512, 256)
        C, R = (16, 64)
        SCALE = 0.03125
        REG_H = 1.0
        bsz, seq_len, _ = qz.shape
        qz_u = qz @ ternary_factor_u.T * SCALE
        qz_v = qz @ ternary_factor_v.T * SCALE
        qz_u = qz_u.reshape(bsz, seq_len, C, R).transpose(0, 2, 1, 3)
        qz_v = qz_v.reshape(bsz, seq_len, C, R).transpose(0, 2, 1, 3)
        message_F = jnp.einsum('bcsr,bctr->bcst', qz_u, qz_v)
        qh = jax.nn.sigmoid(message_F / REG_H)
        qh_v1 = jnp.einsum('bcst,bctr->bcsr', qh, qz_v)
        qh_v2 = jnp.einsum('bcst,bcsr->bctr', qh, qz_u)
        qh_v1 = qh_v1.transpose(0, 2, 1, 3).reshape(bsz, seq_len, C * R)
        qh_v2 = qh_v2.transpose(0, 2, 1, 3).reshape(bsz, seq_len, C * R)
        message_G = (qh_v1 @ ternary_factor_u + qh_v2 @ ternary_factor_v) * SCALE
        return message_G

    def _L0_ffn_ref(x, wq, wk, wv, wo, w1, w2, w3, attn_norm_w, ff_norm_w, moe_norm_w, router_w, ew1, ew2, ew3):
        import jax, jax.numpy as jnp
        import numpy as np
        D = 256
        H = 16
        FF = 1024
        E = 8
        K = 2
        EH = 256
        B, S = (2, 512)
        EPS = 1e-05

        def rmsnorm(x, w):
            v = jnp.mean(jnp.square(x), axis=-1, keepdims=True)
            return x * jax.lax.rsqrt(v + EPS) * w

        def _dense_path(x, wq, wk, wv, wo, w1, w2, w3, attn_norm_w, ff_norm_w):
            b, s, d = x.shape
            hd = d // H
            q = (x @ wq).reshape(b, s, H, hd)
            k = (x @ wk).reshape(b, s, H, hd)
            v = (x @ wv).reshape(b, s, H, hd)
            scores = jnp.einsum('bqhd,bkhd->bhqk', q, k) / np.sqrt(hd).astype(np.float32)
            causal = jnp.tril(jnp.ones((s, s), bool))
            scores = jnp.where(causal, scores, jnp.finfo(scores.dtype).min)
            attn = jax.nn.softmax(scores, axis=-1)
            o = jnp.einsum('bhqk,bkhd->bqhd', attn, v).reshape(b, s, d)
            h = x + rmsnorm(o @ wo, attn_norm_w)
            ffn = jax.nn.silu(h @ w1) * (h @ w3) @ w2
            return h + rmsnorm(ffn, ff_norm_w)

        def _sparse_path(x, router_w, ew1, ew2, ew3, moe_norm_w):
            b, s, d = x.shape
            xt = x.reshape(-1, d)
            probs = jax.nn.softmax(xt @ router_w, axis=-1)
            topw, topi = jax.lax.top_k(probs, K)
            g = jax.nn.silu(jnp.einsum('td,edh->eth', xt, ew1)) * jnp.einsum('td,edh->eth', xt, ew3)
            eo = jnp.einsum('eth,ehd->ted', g, ew2)
            sel = jnp.take_along_axis(eo, topi[:, :, None], axis=1)
            moe_out = jnp.sum(topw[:, :, None] * sel, axis=1).reshape(b, s, d)
            return rmsnorm(moe_out, moe_norm_w)
        dense_out = _dense_path(x, wq, wk, wv, wo, w1, w2, w3, attn_norm_w, ff_norm_w)
        sparse_out = _sparse_path(x, router_w, ew1, ew2, ew3, moe_norm_w)
        return dense_out + sparse_out
    x = L0_attn_qz
    x = x + _L0_attn_ref(_layernorm(x, axis=-1), L0_attn_ternary_factor_u, L0_attn_ternary_factor_v)
    x = x + _L0_ffn_ref(_layernorm(x, axis=-1), L0_ffn_wq, L0_ffn_wk, L0_ffn_wv, L0_ffn_wo, L0_ffn_w1, L0_ffn_w2, L0_ffn_w3, L0_ffn_attn_norm_w, L0_ffn_ff_norm_w, L0_ffn_moe_norm_w, L0_ffn_router_w, L0_ffn_ew1, L0_ffn_ew2, L0_ffn_ew3)
    return x

_drawn_inputs = setup_inputs


def setup_inputs(seed=0):
    import zlib

    import numpy as np

    out = dict(_drawn_inputs(seed))
    spreads = {'L0_ffn_attn_norm_w': (1.0, 0.2),
     'L0_ffn_ff_norm_w': (1.0, 0.2),
     'L0_ffn_moe_norm_w': (1.0, 0.2)}
    factors = {}
    for name, (base, spread) in spreads.items():
        noise = np.random.default_rng([zlib.crc32(name.encode()), seed]).standard_normal(out[name].shape)
        drawn = base * np.exp(spread * noise) if base else spread * noise
        out[name] = jnp.asarray(drawn.astype(out[name].dtype))
    for name, factor in factors.items():
        out[name] = (out[name] * factor).astype(out[name].dtype)
    return out
```

```python
from contextlib import ExitStack

import numpy as np

import concourse.bass as bass
from concourse import mybir

F32 = mybir.dt.float32
F32R = mybir.dt.float32r
ALU = mybir.AluOpType
ACT = mybir.ActivationFunctionType
AX = mybir.AxisListType

P = 128
D = 256
KT = D // P
EPS = 1e-5
CHUNK = 512


def stage_identity(nc, ident):
    with ExitStack() as ctx:
        cleared = ctx.enter_context(nc.semaphore("ident_cleared"))
        block = ctx.enter_context(nc.Block())

        @block.gpsimd
        def _(pool):
            nc.gpsimd.memset(ident[:, :], 0.0).then_inc(cleared, 1)
            pool.wait_ge(cleared, 1)
            nc.gpsimd.affine_select(out=ident[:, :], in_=ident[:, :], compare_op=ALU.not_equal, fill=1.0, base=0,
                                    pattern=[[-1, P]], channel_multiplier=1)


def stage_layernorm(nc, name, src, zh, zl, z_keep, ident, ntok):
    tiles = ntok // P
    with ExitStack() as ctx:
        rows = ctx.enter_context(nc.sbuf_tensor(name + "_rows", [P, tiles, D], F32))
        stats = ctx.enter_context(nc.sbuf_tensor(name + "_stats", [P, tiles, 6], F32))
        mean_var = ctx.enter_context(nc.sbuf_tensor(name + "_mean_var", [P, tiles, 2], F32))
        var_eps = ctx.enter_context(nc.sbuf_tensor(name + "_var_eps", [P, tiles], F32))
        std = ctx.enter_context(nc.sbuf_tensor(name + "_std", [P, tiles], F32))
        rstd = ctx.enter_context(nc.sbuf_tensor(name + "_rstd", [P, tiles], F32))
        slots = 4 if z_keep is None else tiles
        z = ctx.enter_context(nc.sbuf_tensor(name + "_z", [P, slots, D], F32))
        turned = ctx.enter_context(nc.psum_tensor(name + "_turned", [P, 2, CHUNK], F32))
        parts = 4
        rows_in = [ctx.enter_context(nc.semaphore(f"{name}_rows_in{c}")) for c in range(parts)]
        stats_done = ctx.enter_context(nc.semaphore(name + "_stats_done"))
        std_done = ctx.enter_context(nc.semaphore(name + "_std_done"))
        z_done = ctx.enter_context(nc.semaphore(name + "_z_done"))
        z_kept = ctx.enter_context(nc.semaphore(name + "_z_kept"))
        turned_done = ctx.enter_context(nc.semaphore(name + "_turned_done"))
        zh_done = ctx.enter_context(nc.semaphore(name + "_zh_done"))
        zl_done = ctx.enter_context(nc.semaphore(name + "_zl_done"))
        block = ctx.enter_context(nc.Block())
        src_t = src.rearrange("(t p) d -> p t d", p=P)
        per = tiles // parts

        @block.sync
        def _(sp):
            for c in range(parts):
                sp.dma_start(rows[:, c * per:(c + 1) * per, :],
                             src_t[:, c * per:(c + 1) * per, :]).then_inc(rows_in[c], 16)
            if z_keep is not None:
                keep_t = z_keep.rearrange("(t p) d -> p t d", p=P)
                for c in range(parts):
                    sp.wait_ge(z_done, (c + 1) * per)
                    sp.dma_start(keep_t[:, c * per:(c + 1) * per, :], z[:, c * per:(c + 1) * per, :]
                                 ).then_inc(z_kept, 16)
                sp.wait_ge(z_kept, 16 * parts)

        def z_slot(t):
            return z[:, t % slots, :]

        @block.vector
        def _(dve):
            for t in range(tiles):
                if t % per == 0:
                    dve.wait_ge(rows_in[t // per], 16)
                nc.vector.bn_stats(stats[:, t, :], rows[:, t, :]).then_inc(stats_done, 1)
            for t in range(tiles):
                dve.wait_ge(stats_done, t + 1)
                nc.vector.bn_aggr(mean_var[:, t, :], stats[:, t, :]).then_inc(stats_done, 1)
            dve.wait_ge(stats_done, 2 * tiles)
            nc.vector.tensor_scalar(var_eps[:, :], mean_var[:, :, 1], EPS, None, ALU.add).then_inc(stats_done, 1)
            dve.wait_ge(std_done, 1)
            nc.vector.reciprocal(rstd[:, :], std[:, :]).then_inc(std_done, 1)
            dve.wait_ge(std_done, 2)

            def low_part(g):
                dve.wait_ge(zh_done, g + 1)
                col = 2 * g * P
                nc.vector.tensor_tensor(zl[:, :, col:col + 2 * P],
                                        turned[:, g % 2, :].rearrange("p (k c) -> p k c", k=KT),
                                        zh[:, :, col:col + 2 * P].bitcast(F32),
                                        ALU.subtract).then_inc(zl_done, 1)

            for g in range(tiles // 2):
                for t in (2 * g, 2 * g + 1):
                    if z_keep is None and g >= 2:
                        dve.wait_ge(turned_done, g - 1)
                    nc.vector.tensor_scalar(z_slot(t), rows[:, t, :], mean_var[:, t, 0:1], rstd[:, t:t + 1],
                                            ALU.subtract, ALU.mult).then_inc(z_done, 1)
                if g >= 1:
                    low_part(g - 1)
            low_part(tiles // 2 - 1)

        @block.tensor
        def _(pe):
            for g in range(tiles // 2):
                pe.wait_ge(z_done, 2 * g + 2)
                if g >= 2:
                    pe.wait_ge(zl_done, g - 1)
                for j in range(2):
                    for k in range(KT):
                        last = nc.tensor.transpose(turned[:, g % 2, k * 2 * P + j * P:k * 2 * P + (j + 1) * P],
                                                   z_slot(2 * g + j)[:, k * P:(k + 1) * P], ident[:, :])
                last.then_inc(turned_done, 1)

        @block.scalar
        def _(act):
            act.wait_ge(stats_done, 2 * tiles + 1)
            nc.scalar.activation(std[:, :], var_eps[:, :], ACT.Sqrt).then_inc(std_done, 1)
            for g in range(tiles // 2):
                act.wait_ge(turned_done, g + 1)
                col = 2 * g * P
                nc.scalar.activation(zh[:, :, col:col + 2 * P],
                                     turned[:, g % 2, :].rearrange("p (k c) -> p k c", k=KT),
                                     ACT.Copy).then_inc(zh_done, 1)


def stage_factors(nc, u, v, ident, packed, pairs):
    with ExitStack() as ctx:
        nat = [ctx.enter_context(nc.sbuf_tensor(f"factor{i}", [P, pairs, D], F32)) for i in range(2)]
        rec = ctx.enter_context(nc.sbuf_tensor("factor_records", [P, pairs, 8, D], F32R))
        turned = ctx.enter_context(nc.psum_tensor("factor_turned", [P, 2, CHUNK], F32))
        factors_in = ctx.enter_context(nc.semaphore("factors_in"))
        nat_high = ctx.enter_context(nc.semaphore("nat_high"))
        nat_low = ctx.enter_context(nc.semaphore("nat_low"))
        turned_done = ctx.enter_context(nc.semaphore("factor_turned_done"))
        turned_high = ctx.enter_context(nc.semaphore("factor_turned_high"))
        turned_low = ctx.enter_context(nc.semaphore("factor_turned_low"))
        stored = ctx.enter_context(nc.semaphore("factors_stored"))
        block = ctx.enter_context(nc.Block())

        @block.sync
        def _(sp):
            for i, f in enumerate((u, v)):
                sp.dma_start(nat[i][:, :, :], f.rearrange("(c p) d -> p c d", p=P)).then_inc(factors_in, 16)
            for c in range(pairs):
                sp.wait_ge(nat_low, c + 1)
                sp.wait_ge(turned_low, c + 1)
                sp.dma_start(packed[c], rec[:, c, :, :].rearrange("p r d -> p (r d)").bitcast(F32)).then_inc(stored, 16)
            sp.wait_ge(stored, 16 * pairs)

        @block.tensor
        def _(pe):
            pe.wait_ge(factors_in, 32)
            for c in range(pairs):
                if c >= 2:
                    pe.wait_ge(turned_low, c - 1)
                for i in range(2):
                    for k in range(KT):
                        last = nc.tensor.transpose(turned[:, c % 2, i * D + k * P:i * D + (k + 1) * P],
                                                   nat[i][:, c, k * P:(k + 1) * P], ident[:, :])
                last.then_inc(turned_done, 1)

        @block.scalar
        def _(act):
            act.wait_ge(factors_in, 32)
            for c in range(pairs):
                for i in range(2):
                    last = nc.scalar.activation(rec[:, c, 4 + 2 * i, :], nat[i][:, c, :], ACT.Copy)
                    last.then_inc(nat_high, 1)
                act.wait_ge(turned_done, c + 1)
                nc.scalar.activation(rec[:, c, 0:3:2, :], turned[:, c % 2, :].rearrange("p (i d) -> p i d", i=2),
                                     ACT.Copy).then_inc(turned_high, 1)

        @block.vector
        def _(dve):
            dve.wait_ge(factors_in, 32)
            for c in range(pairs):
                dve.wait_ge(nat_high, 2 * c + 2)
                nc.vector.tensor_tensor(rec[:, c, 5, :], nat[0][:, c, :], rec[:, c, 4, :].bitcast(F32), ALU.subtract)
                nc.vector.tensor_tensor(rec[:, c, 7, :], nat[1][:, c, :], rec[:, c, 6, :].bitcast(F32),
                                        ALU.subtract).then_inc(nat_low, 1)
                dve.wait_ge(turned_high, c + 1)
                nc.vector.tensor_tensor(rec[:, c, 1:4:2, :], turned[:, c % 2, :].rearrange("p (i d) -> p i d", i=2),
                                        rec[:, c, 0:3:2, :].bitcast(F32), ALU.subtract).then_inc(turned_low, 1)


def stage_pairs(nc, x, x1, zh, zl, packed, ident, batches, seq, pairs):
    SCALE = 0.03125
    R = 64
    STEPS = 32
    BLK = seq // P
    TURNS = batches * pairs
    JOBS = 12
    NEW = 8
    with ExitStack() as ctx:
        def sb(n, shape, dt):
            return ctx.enter_context(nc.sbuf_tensor(n, shape, dt))

        def sem(n):
            return ctx.enter_context(nc.semaphore(n))

        w = [sb(f"w{i}", [P, 8, D], F32R) for i in range(2)]
        proj = sb("proj", [P, 2, seq], F32)
        u_low = sb("u_low", [P, seq], F32R)
        u_stack = [sb(f"u_stack{i}", [P, 2, seq], F32R) for i in range(2)]
        v_high = [sb(f"v_high{i}", [P, 2, seq], F32R) for i in range(2)]
        v_low = [sb(f"v_low{i}", [P, 2, seq], F32R) for i in range(2)]
        nat = [sb(f"nat{i}", [P, 2, BLK, P], F32) for i in range(2)]
        probs = sb("probs", [P, 2, 2, CHUNK], F32)
        msg_high = sb("msg_high", [P, 2, seq], F32R)
        msg_low = sb("msg_low", [P, 2, seq], F32R)
        total = sb("total", [P, BLK, D], F32)
        f_ps = ctx.enter_context(nc.psum_tensor("f_ps", [P, 2, 2, CHUNK], F32))
        acc = ctx.enter_context(nc.psum_tensor("acc", [P, 2, CHUNK], F32))
        misc = ctx.enter_context(nc.psum_tensor("misc", [P, 2, CHUNK], F32))

        w_in = sem("w_in")
        x_in = sem("x_in")
        x1_out = sem("x1_out")
        waited = sem("waited")
        f_ready = sem("f_ready")
        probs_ready = sem("probs_ready")
        acc_ready = sem("acc_ready")
        msg_high_ready = sem("msg_high_ready")
        msg_low_ready = sem("msg_low_ready")
        misc_ready = sem("misc_ready")
        misc_read = sem("misc_read")
        primed = sem("primed")
        split_high = sem("split_high")
        split_done = sem("split_done")
        u_low_moved = sem("u_low_moved")
        v_moved = sem("v_moved")
        block = ctx.enter_context(nc.Block())

        x_b = x.rearrange("(b t p) d -> b p t d", p=P, t=BLK)
        x1_b = x1.rearrange("(b t p) d -> b p t d", p=P, t=BLK)

        G_AT = {1: 0, 3: 1, 5: 2, 7: 3}
        P_AT = {11: 0, 13: 1, 15: 2, 17: 3}
        N_AT = {19: 0, 21: 1, 23: 2, 31: 3}

        @block.sync
        def _(sp):
            def load_w(slot, turn):
                sp.dma_start(w[slot][:, :, :].rearrange("p r d -> p (r d)").bitcast(F32),
                             packed[turn % pairs] if isinstance(turn, int) else
                             packed[bass.ds(turn % pairs, 1)].rearrange("o p n -> (o p) n")).then_inc(w_in, 16)

            def stacks(slot, turn):
                sp.wait_ge(split_done, turn * 2 + 1)
                sp.dma_start(u_stack[slot][R:P, 0, :].bitcast(F32), u_low[0:R, :].bitcast(F32)).then_inc(u_low_moved, 16)
                sp.dma_start(u_stack[slot][0:R, 1, :].bitcast(F32), u_low[R:P, :].bitcast(F32)).then_inc(u_low_moved, 16)
                sp.wait_ge(split_done, turn * 2 + 2)
                for part in (v_high, v_low):
                    sp.dma_start(part[slot][R:P, 0, :].bitcast(F32),
                                 part[slot][0:R, 0, :].bitcast(F32)).then_inc(v_moved, 16)
                    sp.dma_start(part[slot][0:R, 1, :].bitcast(F32),
                                 part[slot][R:P, 1, :].bitcast(F32)).then_inc(v_moved, 16)

            load_w(0, 0)
            load_w(1, 1)
            stacks(0, 0)
            with sp.Fori(0, TURNS, 2) as t0:
                for par in range(2):
                    turn = t0 + par
                    sp.wait_ge(misc_read, turn * JOBS + NEW + 4)
                    load_w(1 - par, turn + 1)
                    stacks(1 - par, turn + 1)
            sp.wait_ge(u_low_moved, 32 * (TURNS + 1))
            sp.wait_ge(v_moved, 64 * (TURNS + 1))

        @block.gpsimd
        def _(pool):
            nc.gpsimd.memset(msg_high[:, :, :].bitcast(F32), 0.0).then_inc(primed, 1)
            nc.gpsimd.memset(msg_low[:, :, :].bitcast(F32), 0.0).then_inc(msg_low_ready, 1)
            with pool.Fori(0, batches, 1) as b:
                pool.dma_start(total[:, :, :], x_b[bass.ds(b, 1)].rearrange("o p t d -> (o p) t d")).then_inc(x_in, 16)
                pool.wait_ge(misc_read, (b * pairs + pairs) * JOBS + NEW + 4)
                pool.sem_inc(waited, 1)
                pool.dma_start(x1_b[bass.ds(b, 1)].rearrange("o p t d -> (o p) t d"), total[:, :, :]).then_inc(x1_out, 16)
                pool.wait_ge(x1_out, b * 16 + 16)

        @block.tensor
        def _(pe):
            def f_step(par, s):
                kind, blk, chunk = s // 16, s % 16 // 2, s % 2
                rows = slice(blk * P, (blk + 1) * P)
                cols = slice(chunk * CHUNK, (chunk + 1) * CHUNK)
                for h in range(2):
                    for n, part in enumerate((v_high[par], v_low[par])):
                        lhs, rhs = u_stack[par][:, h, rows], part[:, h, cols]
                        if kind == 1:
                            lhs, rhs = part[:, h, rows], u_stack[par][:, h, cols]
                        last = nc.tensor.matmul(f_ps[:, s % 2, h, :], lhs, rhs, start=(n == 0), stop=(n == 1))
                last.then_inc(f_ready, 1)

            def msg_step(par, s, turn):
                kind, blk, chunk = s // 16, s % 16 // 2, s % 2
                pe.wait_ge(probs_ready, turn * STEPS + s + 1)
                if blk == 0:
                    pe.wait_ge(msg_low_ready, 1 + turn * 4 + (0 if kind == 0 else chunk + 1))
                for h in range(2):
                    last = nc.tensor.matmul(acc[h * R:(h + 1) * R, chunk, :], nat[par][:, kind, blk, h * R:(h + 1) * R],
                                            probs[:, s % 2, h, :], start=(blk == 0), stop=(blk == BLK - 1))
                if blk == BLK - 1:
                    last.then_inc(acc_ready, 1)

            def g_job(slot, g, count):
                pe.wait_ge(misc_read, count - 1)
                for j in range(2):
                    tok = slice((2 * g + j) * P, (2 * g + j + 1) * P)
                    n = 0
                    for kind, f in ((0, 6), (1, 4)):
                        for lhs, rhs in ((msg_high, f), (msg_high, f + 1), (msg_low, f)):
                            last = nc.tensor.matmul(misc[:, g % 2, j * D:(j + 1) * D], lhs[:, kind, tok],
                                                    w[slot][:, rhs, :], start=(n == 0), stop=(n == 5))
                            n += 1
                last.then_inc(misc_ready, 1)

            def p_job(slot, p, turn, count):
                which, chunk = p // 2, p % 2
                if count is not None:
                    pe.wait_ge(misc_read, count - 1)
                n = 0
                for k in range(KT):
                    for a, z in ((0, zh), (0, zl), (1, zh)):
                        lhs = w[slot][:, 2 * which + a, k * P:(k + 1) * P]
                        if isinstance(turn, int):
                            rhs = z[:, k, chunk * CHUNK:(chunk + 1) * CHUNK]
                        else:
                            rhs = z[:, k, bass.ds((turn // pairs) % batches * seq + chunk * CHUNK, CHUNK)]
                        last = nc.tensor.matmul(misc[:, p % 2, :], lhs, rhs, start=(n == 0), stop=(n == 5))
                        n += 1
                last.then_inc(misc_ready, 1)

            def n_job(q, count):
                which, half = q // 2, q % 2
                pe.wait_ge(misc_read, count - 1)
                for j in range(4):
                    blk = 4 * half + j
                    last = nc.tensor.transpose(misc[:, q % 2, j * P:(j + 1) * P],
                                               proj[:, which, blk * P:(blk + 1) * P], ident[:, :])
                last.then_inc(misc_ready, 1)

            def new_jobs_first():
                for p in range(4):
                    p_job(0, p, 0, p if p >= 2 else None)
                for q in range(4):
                    if q == 0:
                        pe.wait_ge(misc_read, 4)
                    n_job(q, 4 + q)

            pe.wait_ge(w_in, 32)
            new_jobs_first()
            pe.wait_ge(primed, 1)
            with pe.Fori(0, TURNS, 2) as t0:
                for par in range(2):
                    turn = t0 + par
                    base = turn * JOBS + NEW
                    pe.wait_ge(u_low_moved, turn * 32 + 32)
                    pe.wait_ge(v_moved, turn * 64 + 64)
                    for s in range(STEPS):
                        f_step(par, s)
                        if s == 1:
                            pe.wait_ge(misc_read, turn * JOBS + NEW)
                        if s >= 1:
                            msg_step(par, s - 1, turn)
                        if s in G_AT:
                            if s == 1:
                                pe.wait_ge(msg_low_ready, 1 + turn * 4)
                            g_job(1 - par, G_AT[s], base + G_AT[s])
                        if s in P_AT:
                            if P_AT[s] == 0:
                                pe.wait_ge(w_in, turn * 16 + 48)
                            p_job(1 - par, P_AT[s], turn + 1, base + 4 + P_AT[s])
                        if s in N_AT:
                            if N_AT[s] == 0:
                                pe.wait_ge(misc_read, base + 8)
                            n_job(N_AT[s], base + 8 + N_AT[s])
                    msg_step(par, STEPS - 1, turn)
            pe.wait_ge(msg_low_ready, 1 + TURNS * 4)
            for g in range(4):
                g_job(1, g, TURNS * JOBS + NEW + g)

        @block.scalar
        def _(act):
            def msg_split(c, turn):
                act.wait_ge(acc_ready, turn * 4 + c + 1)
                kind, chunk = c // 2, c % 2
                nc.scalar.activation(msg_high[:, kind, chunk * CHUNK:(chunk + 1) * CHUNK], acc[:, chunk, :],
                                     ACT.Copy, scale=SCALE).then_inc(msg_high_ready, 1)

            act.wait_ge(primed, 1)
            with act.Fori(0, TURNS, 2) as t0:
                for par in range(2):
                    turn = t0 + par
                    for s in range(STEPS):
                        act.wait_ge(f_ready, turn * STEPS + s + 1)
                        nc.scalar.activation(probs[:, s % 2, :, :], f_ps[:, s % 2, :, :],
                                             ACT.Sigmoid).then_inc(probs_ready, 1)
                        if s == 15:
                            act.wait_ge(misc_read, turn * JOBS + NEW + 4)
                            msg_split(0, turn)
                        if s == 16:
                            msg_split(1, turn)
                    msg_split(2, turn)
                    msg_split(3, turn)

        @block.vector
        def _(dve):
            def low(c, turn):
                dve.wait_ge(msg_high_ready, turn * 4 + c + 1)
                kind, chunk = c // 2, c % 2
                cols = slice(chunk * CHUNK, (chunk + 1) * CHUNK)
                nc.vector.scalar_tensor_tensor(msg_low[:, kind, cols], acc[:, chunk, :], SCALE,
                                               msg_high[:, kind, cols].bitcast(F32), ALU.mult,
                                               ALU.subtract).then_inc(msg_low_ready, 1)

            def keep_proj(p, count):
                which, chunk = p // 2, p % 2
                dve.wait_ge(misc_ready, count + 1)
                nc.vector.tensor_scalar(proj[:, which, chunk * CHUNK:(chunk + 1) * CHUNK], misc[:, p % 2, :], SCALE,
                                        None, ALU.mult).then_inc(misc_read, 1)

            def split(slot, which, turn, count):
                dve.wait_ge(misc_read, count)
                high = (u_stack, v_high)[which][slot]
                if which == 0 and not isinstance(turn, int):
                    dve.wait_ge(u_low_moved, turn * 32)
                for h in range(2):
                    rows = slice(h * R, (h + 1) * R)
                    nc.vector.tensor_copy(high[rows, h, :], proj[rows, which, :]).then_inc(split_high, 1)
                dve.wait_ge(split_high, turn * 4 + 2 * which + 2)
                for h in range(2):
                    rows = slice(h * R, (h + 1) * R)
                    dst = u_low[rows, :] if which == 0 else v_low[slot][rows, h, :]
                    last = nc.vector.tensor_tensor(dst, proj[rows, which, :], high[rows, h, :].bitcast(F32),
                                                   ALU.subtract)
                last.then_inc(split_done, 1)

            def keep_nat(slot, q, count):
                which, half = q // 2, q % 2
                dve.wait_ge(misc_ready, count + 1)
                nc.vector.tensor_copy(nat[slot][:, which, 4 * half:4 * half + 4, :],
                                      misc[:, q % 2, :].rearrange("p (j r) -> p j r", j=4)).then_inc(misc_read, 1)

            def add_g(g, count):
                dve.wait_ge(misc_ready, count + 1)
                part = total[:, 2 * g:2 * g + 2, :]
                nc.vector.tensor_tensor(part, misc[:, g % 2, :].rearrange("p (j d) -> p j d", j=2), part,
                                        ALU.add).then_inc(misc_read, 1)

            for p in range(4):
                keep_proj(p, p)
                if p % 2 == 1:
                    split(0, p // 2, 0, p + 1)
            for q in range(4):
                keep_nat(0, q, 4 + q)
            dve.wait_ge(x_in, 16)
            with dve.Fori(0, TURNS, 2) as t0:
                for par in range(2):
                    turn = t0 + par
                    base = turn * JOBS + NEW
                    if par == 1:
                        dve.wait_ge(x_in, (turn + pairs - 1) // pairs * 16)
                    for g in range(4):
                        add_g(g, base + g)
                    keep_proj(0, base + 4)
                    keep_proj(1, base + 5)
                    split(1 - par, 0, turn + 1, base + 6)
                    low(0, turn)
                    keep_proj(2, base + 6)
                    low(1, turn)
                    keep_proj(3, base + 7)
                    split(1 - par, 1, turn + 1, base + 8)
                    for q in range(3):
                        keep_nat(1 - par, q, base + 8 + q)
                    low(2, turn)
                    keep_nat(1 - par, 3, base + 11)
                    low(3, turn)
            for g in range(4):
                add_g(g, TURNS * JOBS + NEW + g)


HEADS = 16
HD = 16
BIG = -1.0e37


def split_weights(nc, dve, act_or_none, src, high, low, sem, count):
    pass


def stage_qkv(nc, zh, zl, wq, wk, wv, qk_high, qk_low, v_aug, ident, ntok):
    CH = ntok // CHUNK
    with ExitStack() as ctx:
        def sb(n, shape, dt):
            return ctx.enter_context(nc.sbuf_tensor("qkv_" + n, shape, dt))

        def sem(n):
            return ctx.enter_context(nc.semaphore("qkv_" + n))

        raw = sb("raw", [P, 3, KT, D], F32)
        w_high = sb("w_high", [P, 3, KT, D], F32R)
        w_low = sb("w_low", [P, 3, KT, D], F32R)
        high = [sb(f"high{i}", [P, 4, CHUNK], F32R) for i in range(2)]
        low = [sb(f"low{i}", [P, 4, CHUNK], F32R) for i in range(2)]
        v_t = sb("v_t", [P, 2, CHUNK], F32)
        v_rows = [sb(f"v_rows{i}", [P, 4, HEADS, 2 * HD], F32) for i in range(2)]
        ps = ctx.enter_context(nc.psum_tensor("qkv_ps", [P, 6, CHUNK], F32))
        v_ps = ctx.enter_context(nc.psum_tensor("qkv_v_ps", [P, 2, CHUNK], F32))
        w_in, w_rounded, w_split, ones_set = sem("w_in"), sem("w_rounded"), sem("w_split"), sem("ones_set")
        proj_ready, high_ready, low_ready = sem("proj_ready"), sem("high_ready"), sem("low_ready")
        turned, v_ready, stored = sem("turned"), sem("v_ready"), sem("stored")
        block = ctx.enter_context(nc.Block())

        @block.sync
        def _(sp):
            sp.sem_inc(stored, 16)
            for i, w in enumerate((wq, wk, wv)):
                sp.dma_start(raw[:, i, :, :], w.rearrange("(k p) n -> p k n", p=P)).then_inc(w_in, 16)
            with sp.Fori(0, CH // 2, 1) as half:
                c0 = half * 2
                for par in range(2):
                    c = c0 + par
                    sp.wait_ge(low_ready, 1 + c * 4 + 4)
                    for dst, src in ((qk_high, high[par]), (qk_low, low[par])):
                        sp.dma_start(dst.rearrange("(j p) n -> p j n", p=P)[:, :, bass.ds(c * CHUNK, CHUNK)],
                                     src[:, :, :].bitcast(F32)).then_inc(stored, 16)
                    sp.wait_ge(v_ready, 1 + c * 2 + 2)
                    sp.dma_start(v_aug.rearrange("(t p) n -> p t n", p=P)[:, bass.ds(c * 4, 4), :],
                                 v_rows[par][:, :, :, :].rearrange("p t h e -> p t (h e)")).then_inc(stored, 16)
            sp.wait_ge(stored, 16 + 48 * CH)

        @block.gpsimd
        def _(pool):
            for i in range(2):
                nc.gpsimd.memset(v_rows[i][:, :, :, HD:], 1.0).then_inc(ones_set, 1)

        @block.tensor
        def _(pe):
            pe.sem_inc(turned, 1)
            pe.wait_ge(w_split, 3)
            with pe.Fori(0, CH, 1) as c:
                pe.wait_ge(high_ready, 1 + c * 6)
                pe.wait_ge(low_ready, 1 + c * 4)
                for j, (which, ct) in enumerate(((2, 0), (2, 1), (0, 0), (0, 1), (1, 0), (1, 1))):
                    n = 0
                    for k in range(KT):
                        for w, z in ((w_high, zh), (w_high, zl), (w_low, zh)):
                            last = nc.tensor.matmul(ps[:, j, :], w[:, which, k, ct * P:(ct + 1) * P],
                                                    z[:, k, bass.ds(c * CHUNK, CHUNK)], start=(n == 0), stop=(n == 5))
                            n += 1
                    last.then_inc(proj_ready, 1)
                pe.wait_ge(high_ready, 1 + c * 6 + 2)
                pe.wait_ge(v_ready, 1 + c * 2)
                for ct in range(2):
                    for j in range(4):
                        last = nc.tensor.transpose(v_ps[:, ct, j * P:(j + 1) * P], v_t[:, ct, j * P:(j + 1) * P],
                                                   ident[:, :])
                    last.then_inc(turned, 1)

        @block.scalar
        def _(act):
            act.sem_inc(high_ready, 1)
            act.wait_ge(w_in, 48)
            for i in range(3):
                nc.scalar.activation(w_high[:, i, :, :], raw[:, i, :, :], ACT.Copy).then_inc(w_rounded, 1)
            with act.Fori(0, CH // 2, 1) as half:
                c0 = half * 2
                for par in range(2):
                    c = c0 + par
                    act.wait_ge(turned, 1 + c * 2)
                    for j in range(2):
                        act.wait_ge(proj_ready, c * 6 + j + 1)
                        nc.scalar.activation(v_t[:, j, :], ps[:, j, :], ACT.Copy).then_inc(high_ready, 1)
                    act.wait_ge(stored, 16 + c0 * 48)
                    for j in range(4):
                        act.wait_ge(proj_ready, c * 6 + j + 3)
                        nc.scalar.activation(high[par][:, j, :], ps[:, j + 2, :], ACT.Copy,
                                             scale=(HD ** -0.5 if j < 2 else 1.0)).then_inc(high_ready, 1)

        @block.vector
        def _(dve):
            for counted in (low_ready, v_ready):
                dve.sem_inc(counted, 1)
            for i in range(3):
                dve.wait_ge(w_rounded, i + 1)
                nc.vector.tensor_tensor(w_low[:, i, :, :], raw[:, i, :, :], w_high[:, i, :, :].bitcast(F32),
                                        ALU.subtract).then_inc(w_split, 1)
            dve.wait_ge(ones_set, 2)
            with dve.Fori(0, CH // 2, 1) as half:
                c0 = half * 2
                for par in range(2):
                    c = c0 + par
                    dve.wait_ge(stored, 16 + c0 * 48)
                    for j in range(4):
                        dve.wait_ge(high_ready, 1 + c * 6 + j + 3)
                        nc.vector.scalar_tensor_tensor(low[par][:, j, :], ps[:, j + 2, :],
                                                       (HD ** -0.5 if j < 2 else 1.0), high[par][:, j, :].bitcast(F32),
                                                       ALU.mult, ALU.subtract).then_inc(low_ready, 1)
                    for ct in range(2):
                        dve.wait_ge(turned, 1 + c * 2 + ct + 1)
                        nc.vector.tensor_copy(v_rows[par][:, :, ct * 8:ct * 8 + 8, 0:HD],
                                              v_ps[:, ct, :].rearrange("p (t h e) -> p t h e", t=4, h=8)
                                              ).then_inc(v_ready, 1)


def stage_attention(nc, qk_high, qk_low, v_aug, o_raw, ident, batches, seq):
    HQ = HEADS // 4
    TURNS = batches * HQ
    SLOTS = 4
    NB = seq // P
    GROUPS = [(kb, c) for kb in range(NB) for c in range(2) if c * 4 + 3 >= kb]
    DIAG = [g for g, (kb, c) in enumerate(GROUPS) if kb // 4 == c]
    UNITS = [(qb, c, h) for qb in range(NB) for c in range(qb // 4 + 1) for h in range(4)]
    NU = len(UNITS)
    NG = len(GROUPS)
    AHEAD = 2
    PER = NU // NG
    EARLY = 3
    with ExitStack() as ctx:
        def sb(n, shape, dt):
            return ctx.enter_context(nc.sbuf_tensor("att_" + n, shape, dt))

        def sem(n):
            return ctx.enter_context(nc.semaphore("att_" + n))

        k_stack = [sb(f"k_stack{i}", [P, 2, seq], F32R) for i in range(SLOTS)]
        q_stack = [sb(f"q_stack{i}", [P, 4, seq], F32R) for i in range(SLOTS)]
        v_win = [sb(f"v_win{i}", [P, NB, 4 * 2 * HD], F32) for i in range(SLOTS)]
        probs = sb("probs", [P, AHEAD + 1, 4, CHUNK], F32)
        mask = sb("mask", [P, CHUNK], F32)
        unused = sb("unused", [P, 2, CHUNK], F32)
        top = sb("top", [P, 2, 4, NB], F32)
        top2 = sb("top2", [P, 2, 4, NB // 2], F32)
        top_t = sb("top_t", [4 * NB, P], F32R)
        st = ctx.enter_context(nc.psum_tensor("att_st", [P, 2, 2, CHUNK], F32))
        s_ps = ctx.enter_context(nc.psum_tensor("att_s", [P, 2, CHUNK], F32))
        o_ps = ctx.enter_context(nc.psum_tensor("att_o", [P, 2, CHUNK], F32))
        set_up, mask_set = sem("set_up"), sem("mask_set")
        qk_in, v_in, top_in = ([sem(f"{n}{i}") for i in range(SLOTS)] for n in ("qk_in", "v_in", "top_in"))
        st_ready, exp_ready, sel_ready = sem("st_ready"), sem("exp_ready"), sem("sel_ready")
        s_ready, max_done, combined = sem("s_ready"), sem("max_done"), sem("combined")
        o_ready, o_kept = sem("o_ready"), sem("o_kept")
        waited, waited_max = sem("waited"), sem("waited_max")
        block = ctx.enter_context(nc.Block())

        O_READY0, O_KEPT0 = 4, 2

        @block.sync
        def _(sp):
            def load(slot, turn):
                b, hq = turn // HQ, turn % HQ
                if isinstance(turn, int):
                    b = b % batches

                    def rows(d, base):
                        return d[base + hq * 64:base + hq * 64 + 64, b * seq:(b + 1) * seq]
                    v_src = v_aug[b * seq:(b + 1) * seq, hq * P:(hq + 1) * P]
                else:
                    b = b % batches
                    def rows(d, base):
                        return d[bass.ds(hq * 64 + base, 64), bass.ds(b * seq, seq)]
                    v_src = v_aug[bass.ds(b * seq, seq), bass.ds(hq * P, P)]
                for quad, kd, qd in ((0, qk_high, qk_high), (1, qk_low, qk_high), (2, qk_high, qk_low)):
                    at = 32 * quad
                    sp.dma_start(k_stack[slot][at:at + 32, :, :].bitcast(F32),
                                 rows(kd, D).rearrange("(pr r) n -> r pr n", r=32)).then_inc(qk_in[slot], 16)
                    for sub in range(2):
                        sp.dma_start(q_stack[slot][at + 16 * sub:at + 16 * sub + 16, sub:4:2, :].bitcast(F32),
                                     rows(qd, 0).rearrange("(pr s r) n -> s r pr n", s=2, r=16)[sub]
                                     ).then_inc(qk_in[slot], 16)
                sp.dma_start(v_win[slot][:, :, :], v_src.rearrange("(t p) n -> p t n", p=P)).then_inc(v_in[slot], 16)

            def tops(slot, turn):
                sp.wait_ge(max_done, turn * (NU + 1) + NU + 1)
                sp.dma_start(q_stack[slot][96:97, :, :].rearrange("o h (b q) -> o (h b) q", q=P).bitcast(F32),
                             top_t[:, :].bitcast(F32)).then_inc(top_in[slot], 16)

            sp.wait_ge(set_up, 2 * SLOTS)
            load(0, 0)
            load(1, 1)
            tops(0, 0)
            with sp.Fori(0, TURNS // SLOTS, 1) as lap:
                for par in range(SLOTS):
                    turn = lap * SLOTS + par
                    sp.wait_ge(o_ready, O_READY0 + turn * 2 - 2)
                    load((par + 2) % SLOTS, turn + 2)
                    tops((par + 1) % SLOTS, turn + 1)
            for slot in range(SLOTS):
                loads = (TURNS + 2 - slot + SLOTS - 1) // SLOTS
                sp.wait_ge(qk_in[slot], 144 * loads)
                sp.wait_ge(v_in[slot], 16 * loads)
                sp.wait_ge(top_in[slot], 16 * ((TURNS + 1 - slot + SLOTS - 1) // SLOTS))

        @block.gpsimd
        def _(pool):
            nc.gpsimd.memset(mask[:, :], 0.0).then_inc(mask_set, 1)
            pool.wait_ge(mask_set, 1)
            nc.gpsimd.affine_select(out=mask[:, CHUNK - P:], in_=mask[:, CHUNK - P:], compare_op=ALU.is_ge, fill=BIG,
                                    base=0, pattern=[[-1, P]], channel_multiplier=1).then_inc(mask_set, 1)
            with pool.Fori(0, TURNS, 1) as turn:
                for g in DIAG:
                    kb = GROUPS[g][0]
                    pool.wait_ge(exp_ready, turn * (2 * NG) + 2 * g + 2)
                    pool.sem_inc(waited, 1)
                    part = probs[:, g % (AHEAD + 1), :, kb % 4 * P:kb % 4 * P + P]
                    nc.gpsimd.affine_select(out=part, in_=part, compare_op=ALU.is_ge, fill=0.0, base=0,
                                            pattern=[[0, 4], [1, P]], channel_multiplier=-1).then_inc(sel_ready, 1)

        @block.tensor
        def _(pe):
            def s_unit(slot, u, turn):
                qb, c, h = UNITS[u]
                n = CHUNK if qb // 4 > c else max(2, qb % 4 + 1) * P
                bank = (slot + u) % 2
                if not (isinstance(turn, int) and turn == 0 and u < 2):
                    pe.wait_ge(max_done, turn * (NU + 1) + u - 1)
                nc.tensor.matmul(s_ps[:, bank, 0:n], q_stack[slot][0:96, h, qb * P:(qb + 1) * P],
                                 k_stack[slot][0:96, h // 2, c * CHUNK:c * CHUNK + n],
                                 start=True, stop=True).then_inc(s_ready, 1)

            def top_unit(slot, turn):
                pe.wait_ge(combined, turn + 1)
                pe.wait_ge(max_done, turn * (NU + 1) + NU - 1)
                nc.tensor.transpose(s_ps[0:4 * NB, (slot + NU) % 2, 0:P],
                                    top[:, slot % 2, :, :].rearrange("p h b -> p (h b)"),
                                    ident[:, :]).then_inc(s_ready, 1)

            def st_unit(slot, g, pr, turn):
                kb, c = GROUPS[g]
                u = 2 * g + pr
                if not (isinstance(turn, int) and turn == 0 and u < 2):
                    pe.wait_ge(exp_ready, turn * (2 * NG) + u - 1)
                lo = min(kb % 4, 2) * P if kb // 4 == c else 0
                for h in range(2):
                    last = nc.tensor.matmul(st[:, u % 2, h, lo:CHUNK], k_stack[slot][0:97, pr, kb * P:(kb + 1) * P],
                                            q_stack[slot][0:97, 2 * pr + h, c * CHUNK + lo:(c + 1) * CHUNK],
                                            start=True, stop=True)
                last.then_inc(st_ready, 1)

            def pv(slot, g, turn):
                kb, c = GROUPS[g]
                if g in DIAG:
                    pe.wait_ge(sel_ready, turn * len(DIAG) + DIAG.index(g) + 1)
                else:
                    pe.wait_ge(exp_ready, turn * (2 * NG) + 2 * g + 2)
                if kb == 0:
                    pe.wait_ge(o_kept, O_KEPT0 + turn * 2 + c - 1)
                lo = kb % 4 * P if kb // 4 == c else 0
                end = kb == 4 * c + 3
                for h in range(4):
                    last = nc.tensor.matmul(o_ps[32 * h:32 * h + 32, c, lo:CHUNK], v_win[slot][:, kb, 32 * h:32 * h + 32],
                                            probs[:, g % (AHEAD + 1), h, lo:CHUNK], start=(kb == 0), stop=end)
                if end:
                    last.then_inc(o_ready, 1)

            pe.sem_inc(o_ready, O_READY0)
            pe.wait_ge(qk_in[0], 144)
            for u in range(NU):
                s_unit(0, u, 0)
            top_unit(0, 0)
            pe.wait_ge(qk_in[1], 144)
            for u in range(PER * EARLY):
                s_unit(1, u, 1)
            pe.wait_ge(top_in[0], 16)
            for g in range(AHEAD):
                for pr in range(2):
                    st_unit(0, g, pr, 0)
            with pe.Fori(0, TURNS // SLOTS, 1) as lap:
                for par in range(SLOTS):
                    turn = lap * SLOTS + par
                    one, two = (par + 1) % SLOTS, (par + 2) % SLOTS
                    pe.wait_ge(v_in[par], lap * 16 + 16)
                    for g in range(NG):
                        if g < NG - EARLY:
                            todo = [(one, PER * (g + EARLY) + i, turn + 1) for i in range(PER)]
                        else:
                            todo = [(two, PER * (g + EARLY - NG) + i, turn + 2) for i in range(PER)]
                        first = g == NG - EARLY
                        if first:
                            pe.wait_ge(qk_in[two], (lap + (par + 2) // SLOTS) * 144 + 144)
                        ahead = (par, g + AHEAD, turn) if g + AHEAD < NG else (one, g + AHEAD - NG, turn + 1)
                        if g + AHEAD == NG:
                            pe.wait_ge(top_in[one], (lap + (par + 1) // SLOTS) * 16 + 16)
                        if not first:
                            s_unit(*todo[0])
                        st_unit(ahead[0], ahead[1], 0, ahead[2])
                        if not first:
                            s_unit(*todo[1])
                        st_unit(ahead[0], ahead[1], 1, ahead[2])
                        if first:
                            top_unit(one, turn + 1)
                            s_unit(*todo[0])
                            s_unit(*todo[1])
                        s_unit(*todo[2])
                        pv(par, g, turn)
                        s_unit(*todo[3])

        @block.scalar
        def _(act):
            def exps(g, turn):
                kb, c = GROUPS[g]
                lo = kb % 4 * P if kb // 4 == c else 0
                for pr in range(2):
                    u = 2 * g + pr
                    act.wait_ge(st_ready, turn * (2 * NG) + u + 1)
                    nc.scalar.activation(probs[:, g % (AHEAD + 1), 2 * pr:2 * pr + 2, lo:CHUNK], st[:, u % 2, :, lo:CHUNK],
                                         ACT.Exp).then_inc(exp_ready, 1)

            def keep(c, turn):
                act.wait_ge(o_ready, O_READY0 + turn * 2 + c + 1)
                nc.scalar.activation(o_raw[:, bass.ds(turn, 1), c * CHUNK:(c + 1) * CHUNK],
                                     o_ps[:, c, :].rearrange("p (o n) -> p o n", o=1), ACT.Copy).then_inc(o_kept, 1)

            act.sem_inc(o_kept, O_KEPT0)
            for g in range(AHEAD):
                exps(g, 0)
            with act.Fori(0, TURNS, 1) as turn:
                for g in range(NG):
                    if g + AHEAD < NG:
                        exps(g + AHEAD, turn)
                    else:
                        exps(g + AHEAD - NG, turn + 1)
                    if GROUPS[g] == (4, 1):
                        keep(0, turn)
                keep(1, turn)

        @block.vector
        def _(dve):
            def maxima(par, turn, units):
                for u in units:
                    qb, c, h = UNITS[u]
                    bank = (par + u) % 2
                    dve.wait_ge(s_ready, turn * (NU + 1) + u + 1)
                    if qb // 4 == c:
                        dve.sem_inc(waited_max, 1)
                    n = CHUNK if qb // 4 > c else (qb % 4 + 1) * P
                    acc = top[:, par, h, qb:qb + 1] if c == 0 else top2[:, par, h, qb - 4:qb - 3]
                    if qb // 4 > c:
                        nc.vector.reduce_max(acc, s_ps[:, bank, 0:n], AX.X).then_inc(max_done, 1)
                    else:
                        nc.vector.tensor_tensor_reduce(out=unused[:, bank, 0:n], in0=s_ps[:, bank, 0:n],
                                                       in1=mask[:, CHUNK - n:], scale=1.0, scalar=BIG, op0=ALU.add,
                                                       op1=ALU.max, accum_out=acc).then_inc(max_done, 1)

            def negate(par, turn, before):
                dve.wait_ge(max_done, turn * (NU + 1) + NU)
                nc.vector.tensor_tensor(top[:, par, :, NB // 2:], top[:, par, :, NB // 2:], top2[:, par, :, :],
                                        ALU.max).then_inc(combined, 1)
                dve.wait_ge(s_ready, turn * (NU + 1) + NU + 1)
                if before is not None:
                    dve.wait_ge(*before)
                nc.vector.tensor_scalar(top_t[:, :], s_ps[0:4 * NB, (par + NU) % 2, 0:P], -1.0, None,
                                        ALU.mult).then_inc(max_done, 1)

            for i in range(SLOTS):
                nc.vector.memset(q_stack[i][:, :, :].bitcast(F32), 0.0).then_inc(set_up, 1)
                nc.vector.memset(k_stack[i][96:97, :, :].bitcast(F32), 1.0).then_inc(set_up, 1)
            dve.wait_ge(mask_set, 2)
            maxima(0, 0, range(NU))
            negate(0, 0, None)
            maxima(1, 1, range(PER * EARLY))
            with dve.Fori(0, TURNS // SLOTS, 1) as lap:
                for par in range(SLOTS):
                    turn = lap * SLOTS + par
                    maxima((par + 1) % 2, turn + 1, range(PER * EARLY, NU))
                    negate((par + 1) % 2, turn + 1, (top_in[par], lap * 16 + 16))
                    maxima(par % 2, turn + 2, range(PER * EARLY))


EXPERTS = 8


def stage_router(nc, zh, zl, router, weights, ident, ntok):
    T = ntok // P
    CH = ntok // CHUNK
    E = EXPERTS
    with ExitStack() as ctx:
        def sb(n, shape, dt=F32):
            return ctx.enter_context(nc.sbuf_tensor("router_" + n, shape, dt))

        def sem(n):
            return ctx.enter_context(nc.semaphore("router_" + n))

        raw = sb("raw", [P, KT, E])
        w_high = sb("w_high", [P, KT, E], F32R)
        w_low = sb("w_low", [P, KT, E], F32R)
        logits_t = sb("logits_t", [E, ntok])
        top = sb("top", [P, T, 1])
        less = sb("less", [P, T, E])
        expo = sb("expo", [P, T, E])
        total = sb("total", [P, T, 1])
        share = sb("share", [P, T, 1])
        prob = sb("prob", [P, T, E])
        rank = sb("rank", [P, T, E])
        beats = sb("beats", [P, T, E])
        ps = ctx.enter_context(nc.psum_tensor("router_ps", [P, 2, CHUNK], F32))
        lg = ctx.enter_context(nc.psum_tensor("router_lg", [P, T, E], F32))
        w_in, logits_ready, kept = sem("w_in"), sem("logits_ready"), sem("kept")
        turned, step, less_ready, expo_ready = sem("turned"), sem("step"), sem("less_ready"), sem("expo_ready")
        block = ctx.enter_context(nc.Block())

        @block.sync
        def _(sp):
            sp.dma_start(raw[:, :, :], router.rearrange("(k p) e -> p k e", p=P)).then_inc(w_in, 16)

        @block.tensor
        def _(pe):
            pe.wait_ge(step, 2)
            for c in range(CH):
                if c >= 2:
                    pe.wait_ge(kept, c - 1)
                n = 0
                for k in range(KT):
                    for w, z in ((w_high, zh), (w_high, zl), (w_low, zh)):
                        last = nc.tensor.matmul(ps[0:E, c % 2, :], w[:, k, :], z[:, k, c * CHUNK:(c + 1) * CHUNK],
                                                start=(n == 0), stop=(n == 5))
                        n += 1
                last.then_inc(logits_ready, 1)
            pe.wait_ge(kept, CH)
            for t in range(T):
                last = nc.tensor.transpose(lg[:, t, :], logits_t[:, t * P:(t + 1) * P], ident[0:E, 0:E])
            last.then_inc(turned, 1)

        @block.scalar
        def _(act):
            for c in range(CH):
                act.wait_ge(logits_ready, c + 1)
                nc.scalar.activation(logits_t[:, c * CHUNK:(c + 1) * CHUNK], ps[0:E, c % 2, :],
                                     ACT.Copy).then_inc(kept, 1)
            act.wait_ge(less_ready, 1)
            nc.scalar.activation(expo[:, :, :], less[:, :, :], ACT.Exp).then_inc(expo_ready, 1)

        @block.vector
        def _(dve):
            count = [0]

            def link(ins):
                count[0] += 1
                ins.then_inc(step, 1)
                dve.wait_ge(step, count[0])

            def wide(ap):
                return ap.broadcast_to([P, T, E])

            dve.wait_ge(w_in, 16)
            link(nc.vector.tensor_copy(w_high[:, :, :], raw[:, :, :]))
            link(nc.vector.tensor_tensor(w_low[:, :, :], raw[:, :, :], w_high[:, :, :].bitcast(F32), ALU.subtract))
            dve.wait_ge(turned, 1)
            link(nc.vector.tensor_reduce(top[:, :, :].rearrange("p t o -> p (t o)"), lg[:, :, :], AX.X, ALU.max))
            nc.vector.tensor_tensor(less[:, :, :], lg[:, :, :], wide(top[:, :, :]), ALU.subtract).then_inc(less_ready, 1)
            link(nc.vector.memset(rank[:, :, :], 0.0))
            dve.wait_ge(expo_ready, 1)
            link(nc.vector.tensor_reduce(total[:, :, :].rearrange("p t o -> p (t o)"), expo[:, :, :], AX.X, ALU.add))
            link(nc.vector.reciprocal(share[:, :, :], total[:, :, :]))
            link(nc.vector.tensor_tensor(prob[:, :, :], expo[:, :, :], wide(share[:, :, :]), ALU.mult))
            for j in range(E):
                if j + 1 < E:
                    link(nc.vector.tensor_tensor(beats[:, :, j + 1:], prob[:, :, j:j + 1].broadcast_to([P, T, E - j - 1]),
                                                 prob[:, :, j + 1:], ALU.is_ge))
                link(nc.vector.tensor_tensor(beats[:, :, 0:j + 1], prob[:, :, j:j + 1].broadcast_to([P, T, j + 1]),
                                             prob[:, :, 0:j + 1], ALU.is_gt))
                link(nc.vector.tensor_tensor(rank[:, :, :], rank[:, :, :], beats[:, :, :], ALU.add))
            link(nc.vector.tensor_scalar(beats[:, :, :], rank[:, :, :], 2.0, None, ALU.is_lt))
            link(nc.vector.tensor_tensor(weights[:, :, :], prob[:, :, :], beats[:, :, :], ALU.mult))


def stage_experts(nc, zh, zl, ew1, ew2, ew3, weights, moe, ntok):
    TURN_CHUNKS = 2
    CH = ntok // CHUNK
    INNER = CH // TURN_CHUNKS
    TILES = CHUNK // P
    with ExitStack() as ctx:
        def sb(n, shape, dt=F32):
            return ctx.enter_context(nc.sbuf_tensor("moe_" + n, shape, dt))

        def sem(n):
            return ctx.enter_context(nc.semaphore("moe_" + n))

        raw = sb("raw", [P, 3, KT, D])
        w_high = [sb(f"w_high{i}", [P, 3, KT, D], F32R) for i in range(2)]
        w_low = [sb(f"w_low{i}", [P, 3, KT, D], F32R) for i in range(2)]
        silu = sb("silu", [P, 2, CHUNK])
        gate = sb("gate", [P, 2, CHUNK])
        g_high = sb("g_high", [P, 4, CHUNK], F32R)
        g_low = sb("g_low", [P, 4, CHUNK], F32R)
        up = ctx.enter_context(nc.psum_tensor("moe_up", [P, 2, 2, CHUNK], F32))
        down = ctx.enter_context(nc.psum_tensor("moe_down", [P, 2, TILES, D], F32))
        raw_in, w_rounded, w_ready = sem("raw_in"), sem("w_rounded"), sem("w_ready")
        up_ready, silu_done, gate_done = sem("up_ready"), sem("silu_done"), sem("gate_done")
        high_done, low_done, down_ready, added = sem("high_done"), sem("low_done"), sem("down_ready"), sem("added")
        cleared, waited, waited_pe = sem("cleared"), sem("waited"), sem("waited_pe")
        block = ctx.enter_context(nc.Block())
        sources = (ew1, ew3, ew2)

        @block.sync
        def _(sp):
            def load(e):
                for i, w in enumerate(sources):
                    src = w[e] if isinstance(e, int) else w[bass.ds(e, 1)].rearrange("o d n -> (o d) n")
                    sp.dma_start(raw[:, i, :, :], src.rearrange("(k p) n -> p k n", p=P)).then_inc(raw_in, 16)

            load(0)
            with sp.Fori(0, EXPERTS - 1, 1) as e:
                sp.wait_ge(w_ready, e + 1)
                load(e + 1)

        @block.gpsimd
        def _(pool):
            def split(slot, e):
                pool.wait_ge(raw_in, e * 48 + 48)
                pool.sem_inc(waited, 1)
                nc.gpsimd.tensor_copy(w_high[slot][:, :, :, :], raw[:, :, :, :]).then_inc(w_rounded, 1)
                pool.wait_ge(w_rounded, e + 1)
                nc.gpsimd.tensor_tensor(w_low[slot][:, :, :, :], raw[:, :, :, :], w_high[slot][:, :, :, :].bitcast(F32),
                                        ALU.subtract).then_inc(w_ready, 1)

            split(0, 0)
            split(1, 1)
            with pool.Fori(0, EXPERTS // 2 - 1, 1) as half:
                for par in range(2):
                    pool.wait_ge(down_ready, (half * 2 + par + 1) * (2 * INNER))
                    split(par, half * 2 + par + 2)

        @block.tensor
        def _(pe):
            with pe.Fori(0, EXPERTS // 2, 1) as half:
                for par in range(2):
                    pe.wait_ge(w_ready, half * 2 + par + 1)
                    pe.sem_inc(waited_pe, 1)
                    with pe.Fori(0, INNER, 1) as inner:
                        turn = (half * 2 + par) * INNER + inner
                        for j in range(4):
                            c, f = j // 2, j % 2
                            if j >= 2:
                                pe.wait_ge(gate_done, turn * 4 + j - 1)
                            for which in range(2):
                                n = 0
                                for k in range(KT):
                                    for w, z in ((w_high, zh), (w_high, zl), (w_low, zh)):
                                        last = nc.tensor.matmul(
                                            up[:, j % 2, which, :], w[par][:, which, k, f * P:(f + 1) * P],
                                            z[:, k, bass.ds(inner * (2 * CHUNK) + c * CHUNK, CHUNK)],
                                            start=(n == 0), stop=(n == 5))
                                        n += 1
                            last.then_inc(up_ready, 1)
                        for c in range(2):
                            pe.wait_ge(low_done, 1 + turn * 4 + 2 * c + 2)
                            if c == 0:
                                pe.wait_ge(added, 1 + turn * 8)
                            for i in range(TILES):
                                n = 0
                                for f in range(2):
                                    for g, w in ((g_high, w_high), (g_high, w_low), (g_low, w_high)):
                                        last = nc.tensor.matmul(down[:, c, i, :], g[:, 2 * c + f, i * P:(i + 1) * P],
                                                                w[par][:, 2, f, :], start=(n == 0), stop=(n == 5))
                                        n += 1
                            last.then_inc(down_ready, 1)

        @block.scalar
        def _(act):
            with act.Fori(0, EXPERTS * INNER, 1) as turn:
                def high(j):
                    act.wait_ge(gate_done, turn * 4 + j + 1)
                    nc.scalar.activation(g_high[:, j, :], gate[:, j % 2, :], ACT.Copy).then_inc(high_done, 1)

                for j in range(4):
                    act.wait_ge(up_ready, turn * 4 + j + 1)
                    nc.scalar.activation(silu[:, j % 2, :], up[:, j % 2, 0, :], ACT.Silu).then_inc(silu_done, 1)
                    if j >= 1:
                        high(j - 1)
                high(3)

        @block.vector
        def _(dve):
            for counted in (low_done, added):
                dve.sem_inc(counted, 1)
            nc.vector.memset(moe[:, :, :], 0.0).then_inc(cleared, 1)
            dve.wait_ge(cleared, 1)
            with dve.Fori(0, EXPERTS, 1) as e:
                with dve.Fori(0, INNER, 1) as inner:
                    turn = e * INNER + inner

                    def low(j):
                        dve.wait_ge(high_done, turn * 4 + j + 1)
                        nc.vector.tensor_tensor(g_low[:, j, :], gate[:, j % 2, :], g_high[:, j, :].bitcast(F32),
                                                ALU.subtract).then_inc(low_done, 1)

                    for j in range(4):
                        dve.wait_ge(low_done, 1 + turn * 4 + max(j - 1, 0))
                        dve.wait_ge(silu_done, turn * 4 + j + 1)
                        nc.vector.tensor_tensor(gate[:, j % 2, :], up[:, j % 2, 1, :], silu[:, j % 2, :],
                                                ALU.mult).then_inc(gate_done, 1)
                        if j >= 1:
                            low(j - 1)
                    low(3)
                    dve.wait_ge(added, 1 + turn * 8)
                    for c in range(2):
                        dve.wait_ge(down_ready, turn * 2 + c + 1)
                        for i in range(TILES):
                            tile = inner * (2 * TILES) + c * TILES + i
                            part = moe[:, bass.ds(tile, 1), :].rearrange("p o d -> p (o d)")
                            by = weights[:, bass.ds(tile, 1), bass.ds(e, 1)].rearrange("p o e -> p (o e)")
                            nc.vector.scalar_tensor_tensor(part, down[:, c, i, :], by, part, ALU.mult,
                                                           ALU.add).then_inc(added, 1)


def stage_norm_add(nc, name, rows, norm_w, extras, out, ntok):
    T = ntok // P
    G = 4
    with ExitStack() as ctx:
        def sb(n, shape, dt=F32):
            return ctx.enter_context(nc.sbuf_tensor(name + "_" + n, shape, dt))

        def sem(n):
            return ctx.enter_context(nc.semaphore(name + "_" + n))

        squares = sb("squares", [P, 2, D])
        mean_sq = sb("mean_sq", [P, T])
        ms_eps = sb("ms_eps", [P, T])
        rms = sb("rms", [P, T])
        inv = sb("inv", [P, T])
        w_row = sb("w_row", [P, D])
        extra_in = [sb(f"extra{i}", [P, 2, G, D]) for i in range(len(extras))]
        res = sb("res", [P, 2, G, D])
        w_in, summed, eps_added, rms_done, inv_done = (sem(n) for n in ("w_in", "summed", "eps_added", "rms_done", "inv_done"))
        scaled, finished = sem("scaled"), sem("finished")
        loaded = [sem(f"loaded{i}") for i in range(2)]
        stored = [sem(f"stored{i}") for i in range(2)]
        block = ctx.enter_context(nc.Block())
        out_t = out.rearrange("(t p) d -> p t d", p=P)
        n_in = len(extras)

        @block.sync
        def _(sp):
            sp.dma_start(w_row[:, :], norm_w.rearrange("(o d) -> o d", o=1).broadcast_to([P, D])).then_inc(w_in, 16)
            for c in range(T // G):
                if c >= 2:
                    sp.wait_ge(finished, (c - 1) * G)
                for i, x in enumerate(extras):
                    sp.dma_start(extra_in[i][:, c % 2, :, :],
                                 x.rearrange("(t p) d -> p t d", p=P)[:, c * G:(c + 1) * G, :]
                                 ).then_inc(loaded[c % 2], 16)
                if c >= 1:
                    sp.wait_ge(finished, c * G)
                    sp.dma_start(out_t[:, (c - 1) * G:c * G, :], res[:, (c - 1) % 2, :, :]).then_inc(stored[(c - 1) % 2], 16)
            c = T // G
            sp.wait_ge(finished, c * G)
            sp.dma_start(out_t[:, (c - 1) * G:c * G, :], res[:, (c - 1) % 2, :, :]).then_inc(stored[(c - 1) % 2], 16)
            for i in range(2):
                sp.wait_ge(stored[i], 16 * (T // G // 2))

        @block.scalar
        def _(act):
            for t in range(T):
                if t >= 2:
                    act.wait_ge(summed, t - 1)
                nc.scalar.activation(squares[:, t % 2, :], rows[:, t, :], ACT.Square,
                                     accum_out=mean_sq[:, t:t + 1]).then_inc(summed, 1)
            act.wait_ge(eps_added, 1)
            nc.scalar.activation(rms[:, :], ms_eps[:, :], ACT.Sqrt).then_inc(rms_done, 1)

        @block.vector
        def _(dve):
            dve.wait_ge(summed, T)
            nc.vector.tensor_scalar(ms_eps[:, :], mean_sq[:, :], 1.0 / D, EPS, ALU.mult, ALU.add).then_inc(eps_added, 1)
            dve.wait_ge(rms_done, 1)
            nc.vector.reciprocal(inv[:, :], rms[:, :]).then_inc(inv_done, 1)
            dve.wait_ge(inv_done, 1)
            dve.wait_ge(w_in, 16)
            for t in range(T):
                c, i = t // G, t % G
                if i == 0:
                    if c >= 2:
                        dve.wait_ge(stored[c % 2], 16 * (c // 2))
                    dve.wait_ge(loaded[c % 2], 16 * n_in * (c // 2 + 1))
                nc.vector.scalar_tensor_tensor(res[:, c % 2, i, :], rows[:, t, :], inv[:, t:t + 1], w_row[:, :],
                                               ALU.mult, ALU.mult).then_inc(scaled, 1)
                dve.wait_ge(scaled, (n_in) * t + 1)
                for n in range(n_in):
                    last = nc.vector.tensor_tensor(res[:, c % 2, i, :], res[:, c % 2, i, :],
                                                   extra_in[n][:, c % 2, i, :], ALU.add)
                    if n + 1 < n_in:
                        last.then_inc(scaled, 1)
                        dve.wait_ge(scaled, n_in * t + n + 2)
                last.then_inc(finished, 1)


def stage_attention_out(nc, o_raw, z_rows, wo, norm_w, hh, hl, h_out, ident, batches, seq):
    ntok = batches * seq
    T = ntok // P
    HQ = HEADS // 4
    with ExitStack() as ctx:
        def sb(n, shape, dt=F32):
            return ctx.enter_context(nc.sbuf_tensor("ao_" + n, shape, dt))

        def sem(n):
            return ctx.enter_context(nc.semaphore("ao_" + n))

        raw = sb("raw", [P, KT, D])
        w_high = sb("w_high", [P, KT, D], F32R)
        w_low = sb("w_low", [P, KT, D], F32R)
        w_row = sb("w_row", [P, D])
        share = sb("share", [P, 2, HEADS, 1])
        o_rows = sb("o_rows", [P, 2, D])
        o_high = sb("o_high", [P, 2, KT, P], F32R)
        o_low = sb("o_low", [P, 2, KT, P], F32R)
        squares = sb("squares", [P, 2, D])
        sums = sb("sums", [P, 2, 1])
        ms = sb("ms", [P, 2, 1])
        rms = sb("rms", [P, 2, 1])
        inv = sb("inv", [P, 2, 1])
        scaled = sb("scaled", [P, 2, D])
        h = sb("h", [P, 4, D])
        t1 = ctx.enter_context(nc.psum_tensor("ao_t1", [P, 2, CHUNK], F32))
        t2 = ctx.enter_context(nc.psum_tensor("ao_t2", [P, 2, CHUNK], F32))
        prod = ctx.enter_context(nc.psum_tensor("ao_prod", [P, 2, CHUNK], F32))
        t3 = ctx.enter_context(nc.psum_tensor("ao_t3", [P, 2, CHUNK], F32))
        w_in, w_rounded, w_split = sem("w_in"), sem("w_rounded"), sem("w_split")
        t1_ready, share_done, rows_done, t2_ready = sem("t1_ready"), sem("share_done"), sem("rows_done"), sem("t2_ready")
        o_high_done, o_low_done, prod_ready = sem("o_high_done"), sem("o_low_done"), sem("prod_ready")
        sums_done, ms_done, rms_done, inv_done = sem("sums_done"), sem("ms_done"), sem("rms_done"), sem("inv_done")
        scaled_done, h_done, t3_ready = sem("scaled_done"), sem("h_done"), sem("t3_ready")
        h_high_done, h_low_done = sem("h_high_done"), sem("h_low_done")
        stored = [sem(f"stored{i}") for i in range(4)]
        z_in = [sem(f"z_in{i}") for i in range(2)]
        z = sb("z", [P, 2, 4, D])
        block = ctx.enter_context(nc.Block())

        @block.sync
        def _(sp):
            def load_z(c):
                sp.dma_start(z[:, c % 2, :, :], z_rows.rearrange("(t p) d -> p t d", p=P)[:, 4 * c:4 * c + 4, :]
                             ).then_inc(z_in[c % 2], 16)

            sp.dma_start(raw[:, :, :], wo.rearrange("(k p) n -> p k n", p=P)).then_inc(w_in, 16)
            sp.dma_start(w_row[:, :], norm_w.rearrange("(o d) -> o d", o=1).broadcast_to([P, D])).then_inc(w_in, 16)
            load_z(0)
            load_z(1)
            for t in range(T):
                sp.wait_ge(h_done, t + 1)
                if t % 4 == 3 and t + 4 < T - 1:
                    load_z(t // 4 + 2)
                sp.dma_start(h_out[t * P:(t + 1) * P, :], h[:, t % 4, :]).then_inc(stored[t % 4], 16)
            for i in range(4):
                sp.wait_ge(stored[i], 16 * (T // 4))

        @block.tensor
        def _(pe):
            def turn_heads(t):
                if t >= 2:
                    pe.wait_ge(rows_done, t - 1)
                at = t * P % seq
                for hq in range(HQ):
                    last = nc.tensor.transpose(t1[:, t % 2, hq * P:(hq + 1) * P],
                                               o_raw[:, t * P // seq * HQ + hq, at:at + P], ident[:, :])
                last.then_inc(t1_ready, 1)

            def turn_rows(t):
                pe.wait_ge(rows_done, t + 1)
                if t >= 2:
                    pe.wait_ge(o_low_done, t - 1)
                for k in range(KT):
                    last = nc.tensor.transpose(t2[:, t % 2, k * P:(k + 1) * P], o_rows[:, t % 2, k * P:(k + 1) * P],
                                               ident[:, :])
                last.then_inc(t2_ready, 1)

            def product(t):
                pe.wait_ge(o_low_done, t + 1)
                if t >= 2:
                    pe.wait_ge(scaled_done, t - 1)
                n = 0
                for k in range(KT):
                    for o, w in ((o_high, w_high), (o_high, w_low), (o_low, w_high)):
                        last = nc.tensor.matmul(prod[:, t % 2, 0:D], o[:, t % 2, k, :], w[:, k, :],
                                                start=(n == 0), stop=(n == 5))
                        n += 1
                last.then_inc(prod_ready, 1)

            def turn_h(t):
                pe.wait_ge(h_done, t + 1)
                if t >= 2:
                    pe.wait_ge(h_low_done, t - 1)
                for k in range(KT):
                    last = nc.tensor.transpose(t3[:, t % 2, k * P:(k + 1) * P], h[:, t % 4, k * P:(k + 1) * P],
                                               ident[:, :])
                last.then_inc(t3_ready, 1)

            pe.wait_ge(w_split, 1)
            for t in range(T + 3):
                if t < T:
                    turn_heads(t)
                if 0 <= t - 1 < T:
                    turn_rows(t - 1)
                if 0 <= t - 2 < T:
                    product(t - 2)
                if 0 <= t - 3 < T:
                    turn_h(t - 3)

        @block.scalar
        def _(act):
            act.wait_ge(w_in, 32)
            nc.scalar.activation(w_high[:, :, :], raw[:, :, :], ACT.Copy).then_inc(w_rounded, 1)
            for t in range(T + 3):
                if 0 <= t - 1 < T:
                    u = t - 1
                    act.wait_ge(t2_ready, u + 1)
                    if u >= 2:
                        act.wait_ge(prod_ready, u - 1)
                    nc.scalar.activation(o_high[:, u % 2, :, :], t2[:, u % 2, 0:D].rearrange("p (k c) -> p k c", k=KT),
                                         ACT.Copy).then_inc(o_high_done, 1)
                if 0 <= t - 2 < T:
                    u = t - 2
                    act.wait_ge(prod_ready, u + 1)
                    if u >= 2:
                        act.wait_ge(ms_done, u - 1)
                        act.wait_ge(sums_done, u - 1)
                    nc.scalar.activation(squares[:, u % 2, :], prod[:, u % 2, 0:D], ACT.Square,
                                         accum_out=sums[:, u % 2, :]).then_inc(sums_done, 1)
                    act.wait_ge(ms_done, u + 1)
                    if u >= 2:
                        act.wait_ge(inv_done, u - 1)
                    nc.scalar.activation(rms[:, u % 2, :], ms[:, u % 2, :], ACT.Sqrt).then_inc(rms_done, 1)
                if 0 <= t - 3 < T:
                    u = t - 3
                    act.wait_ge(t3_ready, u + 1)
                    nc.scalar.activation(hh[:, :, u * P:(u + 1) * P],
                                         t3[:, u % 2, 0:D].rearrange("p (k c) -> p k c", k=KT),
                                         ACT.Copy).then_inc(h_high_done, 1)

        @block.vector
        def _(dve):
            dve.wait_ge(w_rounded, 1)
            nc.vector.tensor_tensor(w_low[:, :, :], raw[:, :, :], w_high[:, :, :].bitcast(F32),
                                    ALU.subtract).then_inc(w_split, 1)
            for t in range(T + 3):
                if t < T:
                    dve.wait_ge(t1_ready, t + 1)
                    heads = t1[:, t % 2, :].rearrange("p (h e) -> p h e", e=2 * HD)
                    nc.vector.reciprocal(share[:, t % 2, :, :], heads[:, :, HD:HD + 1]).then_inc(share_done, 1)
                    dve.wait_ge(share_done, t + 1)
                    if t >= 2:
                        dve.wait_ge(t2_ready, t - 1)
                    nc.vector.tensor_tensor(o_rows[:, t % 2, :].rearrange("p (h e) -> p h e", e=HD), heads[:, :, 0:HD],
                                            share[:, t % 2, :, :].broadcast_to([P, HEADS, HD]),
                                            ALU.mult).then_inc(rows_done, 1)
                if 0 <= t - 1 < T:
                    u = t - 1
                    dve.wait_ge(o_high_done, u + 1)
                    nc.vector.tensor_tensor(o_low[:, u % 2, :, :], t2[:, u % 2, 0:D].rearrange("p (k c) -> p k c", k=KT),
                                            o_high[:, u % 2, :, :].bitcast(F32), ALU.subtract).then_inc(o_low_done, 1)
                if 0 <= t - 2 < T:
                    u = t - 2
                    dve.wait_ge(sums_done, u + 1)
                    nc.vector.tensor_scalar(ms[:, u % 2, :], sums[:, u % 2, :], 1.0 / D, EPS, ALU.mult,
                                            ALU.add).then_inc(ms_done, 1)
                    dve.wait_ge(rms_done, u + 1)
                    nc.vector.reciprocal(inv[:, u % 2, :], rms[:, u % 2, :]).then_inc(inv_done, 1)
                    dve.wait_ge(inv_done, u + 1)
                    nc.vector.scalar_tensor_tensor(scaled[:, u % 2, :], prod[:, u % 2, 0:D], inv[:, u % 2, :],
                                                   w_row[:, :], ALU.mult, ALU.mult).then_inc(scaled_done, 1)
                    dve.wait_ge(scaled_done, u + 1)
                    if u >= 4:
                        dve.wait_ge(stored[u % 4], 16 * (u // 4))
                        dve.wait_ge(t3_ready, u - 3)
                    if u % 4 == 0:
                        dve.wait_ge(z_in[u // 4 % 2], 16 * (u // 8 + 1))
                    nc.vector.tensor_tensor(h[:, u % 4, :], scaled[:, u % 2, :], z[:, u // 4 % 2, u % 4, :], ALU.add).then_inc(h_done, 1)
                if 0 <= t - 3 < T:
                    u = t - 3
                    dve.wait_ge(h_high_done, u + 1)
                    nc.vector.tensor_tensor(hl[:, :, u * P:(u + 1) * P],
                                            t3[:, u % 2, 0:D].rearrange("p (k c) -> p k c", k=KT),
                                            hh[:, :, u * P:(u + 1) * P].bitcast(F32), ALU.subtract).then_inc(h_low_done, 1)


def stage_ffn(nc, hh, hl, w1, w2, w3, ffn, ntok):
    CH = ntok // CHUNK
    FT = w1.shape[1] // P
    TILES = CHUNK // P
    with ExitStack() as ctx:
        def sb(n, shape, dt=F32):
            return ctx.enter_context(nc.sbuf_tensor("ffn_" + n, shape, dt))

        def sem(n):
            return ctx.enter_context(nc.semaphore("ffn_" + n))

        SIZE = KT * FT * P
        raw = sb("raw", [P, SIZE])
        w_high = sb("w_high", [P, 3, SIZE], F32R)
        w_low = sb("w_low", [P, 3, SIZE], F32R)
        silu = sb("silu", [P, 2, CHUNK])
        gate = sb("gate", [P, 2, CHUNK])
        g_high = sb("g_high", [P, 2, CHUNK], F32R)
        g_low = sb("g_low", [P, 2, CHUNK], F32R)
        up = ctx.enter_context(nc.psum_tensor("ffn_up", [P, 2, 2, CHUNK], F32))
        down = ctx.enter_context(nc.psum_tensor("ffn_down", [P, TILES, CHUNK], F32))
        raw_in, w_rounded, w_ready = sem("raw_in"), sem("w_rounded"), sem("w_ready")
        up_ready, silu_done, gate_done = sem("up_ready"), sem("silu_done"), sem("gate_done")
        high_done, low_done, down_ready, kept = sem("high_done"), sem("low_done"), sem("down_ready"), sem("kept")
        block = ctx.enter_context(nc.Block())

        @block.sync
        def _(sp):
            for i, w in enumerate((w1, w3, w2)):
                if i:
                    sp.wait_ge(w_ready, i)
                n = w.shape[1]
                sp.dma_start(raw[:, :].rearrange("p (k n) -> p k n", n=n), w.rearrange("(k p) n -> p k n", p=P)
                             ).then_inc(raw_in, 16)

        def upw(w, which, k, f):
            at = k * FT * P + f * P
            return w[:, which, at:at + P]

        @block.tensor
        def _(pe):
            def up_job(f, c):
                if f >= 2:
                    pe.wait_ge(gate_done, 1 + c * FT + f - 1)
                elif f == 0:
                    pe.wait_ge(gate_done, 1 + c * FT)
                for which in range(2):
                    n = 0
                    for k in range(KT):
                        for w, z in ((w_high, hh), (w_high, hl), (w_low, hh)):
                            last = nc.tensor.matmul(up[:, f % 2, which, :], upw(w, which, k, f),
                                                    z[:, k, bass.ds(c * CHUNK, CHUNK)], start=(n == 0), stop=(n == 5))
                            n += 1
                last.then_inc(up_ready, 1)

            def down_job(f, c):
                pe.wait_ge(low_done, 1 + c * FT + f + 1)
                if f == 0:
                    pe.wait_ge(kept, 1 + c)
                for i in range(TILES):
                    for n, (g, w) in enumerate(((g_high, w_high), (g_high, w_low), (g_low, w_high))):
                        last = nc.tensor.matmul(down[:, i, 0:D], g[:, f % 2, i * P:(i + 1) * P],
                                                w[:, 2, f * D:(f + 1) * D], start=(f == 0 and n == 0),
                                                stop=(f == FT - 1 and n == 2))
                last.then_inc(down_ready, 1)

            pe.sem_inc(down_ready, 1)
            pe.wait_ge(w_ready, 3)
            with pe.Fori(0, CH, 1) as c:
                for f in range(FT):
                    up_job(f, c)
                    if f >= 1:
                        down_job(f - 1, c)
                down_job(FT - 1, c)

        @block.scalar
        def _(act):
            for i in range(3):
                act.wait_ge(raw_in, 16 * i + 16)
                nc.scalar.activation(w_high[:, i, :], raw[:, :], ACT.Copy).then_inc(w_rounded, 1)
            with act.Fori(0, CH, 1) as c:
                def high(f):
                    act.wait_ge(gate_done, 1 + c * FT + f + 1)
                    if f >= 2:
                        act.wait_ge(down_ready, 1 + c * FT + f - 1)
                    else:
                        act.wait_ge(down_ready, 1 + c * FT)
                    nc.scalar.activation(g_high[:, f % 2, :], gate[:, f % 2, :], ACT.Copy).then_inc(high_done, 1)

                for f in range(FT):
                    act.wait_ge(up_ready, c * FT + f + 1)
                    nc.scalar.activation(silu[:, f % 2, :], up[:, f % 2, 0, :], ACT.Silu).then_inc(silu_done, 1)
                    if f >= 1:
                        high(f - 1)
                high(FT - 1)

        @block.vector
        def _(dve):
            for counted in (gate_done, kept, low_done):
                dve.sem_inc(counted, 1)
            for i in range(3):
                dve.wait_ge(w_rounded, i + 1)
                nc.vector.tensor_tensor(w_low[:, i, :], raw[:, :], w_high[:, i, :].bitcast(F32),
                                        ALU.subtract).then_inc(w_ready, 1)
            with dve.Fori(0, CH, 1) as c:
                def low(f):
                    dve.wait_ge(high_done, c * FT + f + 1)
                    nc.vector.tensor_tensor(g_low[:, f % 2, :], gate[:, f % 2, :], g_high[:, f % 2, :].bitcast(F32),
                                            ALU.subtract).then_inc(low_done, 1)

                for f in range(FT):
                    dve.wait_ge(low_done, 1 + c * FT + max(f - 1, 0))
                    dve.wait_ge(silu_done, c * FT + f + 1)
                    nc.vector.tensor_tensor(gate[:, f % 2, :], up[:, f % 2, 1, :], silu[:, f % 2, :],
                                            ALU.mult).then_inc(gate_done, 1)
                    if f >= 1:
                        low(f - 1)
                low(FT - 1)
                dve.wait_ge(down_ready, 1 + c * FT + FT)
                nc.vector.tensor_copy(ffn[:, bass.ds(c * TILES, TILES), :], down[:, :, 0:D]).then_inc(kept, 1)


def seq_preln(nc, x, u, v, wq, wk, wv, wo, w1, w2, w3, attn_w, ff_w, moe_w, router, ew1, ew2, ew3, out):
    batches, seq, _ = x.shape
    ntok = batches * seq
    pairs = u.shape[0] // P
    x = x.rearrange("b s d -> (b s) d")
    out = out.rearrange("b s d -> (b s) d")

    def scratch(name, shape):
        return nc.dram_tensor(name, shape, F32, kind="Internal").ap()

    packed = scratch("packed_factors", (pairs, P, 8 * D))
    x1 = scratch("x1", (ntok, D))
    x1_sparse = scratch("x1_sparse", (ntok, D))
    y_rows = scratch("y_rows", (ntok, D))
    h_rows = scratch("h_rows", (ntok, D))
    qk_high = scratch("qk_high", (4 * P, ntok))
    qk_low = scratch("qk_low", (4 * P, ntok))
    v_aug = scratch("v_aug", (ntok, HEADS * 2 * HD))

    with ExitStack() as whole:
        ident = whole.enter_context(nc.sbuf_tensor("ident", [P, P], F32))
        stage_identity(nc, ident)
        with ExitStack() as ctx:
            zh = ctx.enter_context(nc.sbuf_tensor("z1_high", [P, KT, ntok], F32R))
            zl = ctx.enter_context(nc.sbuf_tensor("z1_low", [P, KT, ntok], F32R))
            stage_layernorm(nc, "ln1", x, zh, zl, None, ident, ntok)
            stage_factors(nc, u, v, ident, packed, pairs)
            stage_pairs(nc, x, x1, zh, zl, packed, ident, batches, seq, pairs)
        late = whole.enter_context(ExitStack())
        with ExitStack() as ctx:
            yh = ctx.enter_context(nc.sbuf_tensor("y_high", [P, KT, ntok], F32R))
            yl = ctx.enter_context(nc.sbuf_tensor("y_low", [P, KT, ntok], F32R))
            stage_layernorm(nc, "ln2", x1, yh, yl, y_rows, ident, ntok)
            stage_qkv(nc, yh, yl, wq, wk, wv, qk_high, qk_low, v_aug, ident, ntok)
            weights = ctx.enter_context(nc.sbuf_tensor("expert_weights", [P, ntok // P, EXPERTS], F32))
            moe = ctx.enter_context(nc.sbuf_tensor("moe", [P, ntok // P, D], F32))
            stage_router(nc, yh, yl, router, weights, ident, ntok)
            stage_experts(nc, yh, yl, ew1, ew2, ew3, weights, moe, ntok)
            stage_norm_add(nc, "moe_norm", moe, moe_w, [x1], x1_sparse, ntok)
        late = whole.enter_context(ExitStack())
        with ExitStack() as ctx:
            o_raw = ctx.enter_context(nc.sbuf_tensor("o_raw", [P, batches * (HEADS // 4), seq], F32))
            stage_attention(nc, qk_high, qk_low, v_aug, o_raw, ident, batches, seq)
            hh = late.enter_context(nc.sbuf_tensor("h_high", [P, KT, ntok], F32R, side="right"))
            hl = late.enter_context(nc.sbuf_tensor("h_low", [P, KT, ntok], F32R, side="right"))
            stage_attention_out(nc, o_raw, y_rows, wo, attn_w, hh, hl, h_rows, ident, batches, seq)
        ffn = whole.enter_context(nc.sbuf_tensor("ffn", [P, ntok // P, D], F32))
        stage_ffn(nc, hh, hl, w1, w2, w3, ffn, ntok)
        stage_norm_add(nc, "ff_norm", ffn, ff_w, [h_rows, x1_sparse], out, ntok)


_INS = ["L0_attn_qz", "L0_attn_ternary_factor_u", "L0_attn_ternary_factor_v", "L0_ffn_wq", "L0_ffn_wk", "L0_ffn_wv",
        "L0_ffn_wo", "L0_ffn_w1", "L0_ffn_w2", "L0_ffn_w3", "L0_ffn_attn_norm_w", "L0_ffn_ff_norm_w",
        "L0_ffn_moe_norm_w", "L0_ffn_router_w", "L0_ffn_ew1", "L0_ffn_ew2", "L0_ffn_ew3"]


def kernel(**inputs):
    import concourse.bacc as bacc
    from concourse.bass_utils import run_bass_kernel_spmd

    nc = bacc.Bacc("TRN2", target_bir_lowering=False, num_devices=1)
    arrays, args = {}, []
    for name in _INS:
        a = np.ascontiguousarray(inputs[name])
        arrays[name] = a
        args.append(nc.dram_tensor(name, a.shape, mybir.dt.from_np(a.dtype), kind="ExternalInput").ap())
    out = nc.dram_tensor("out", arrays["L0_attn_qz"].shape, F32, kind="ExternalOutput").ap()
    seq_preln(nc, *args, out)
    result = run_bass_kernel_spmd(nc, [arrays], core_ids=[0])
    return result.results[0]["out"]
```

```python
from contextlib import ExitStack

import numpy as np

import concourse.bass as bass
from concourse import mybir

F32 = mybir.dt.float32
F32R = mybir.dt.float32r
ALU = mybir.AluOpType
ACT = mybir.ActivationFunctionType
AX = mybir.AxisListType

P = 128
D = 256
KT = D // P
EPS = 1e-5
CHUNK = 512


def stage_identity(nc, ident):
    with ExitStack() as ctx:
        cleared = ctx.enter_context(nc.semaphore("ident_cleared"))
        block = ctx.enter_context(nc.Block())

        @block.gpsimd
        def _(pool):
            nc.gpsimd.memset(ident[:, :], 0.0).then_inc(cleared, 1)
            pool.wait_ge(cleared, 1)
            nc.gpsimd.affine_select(out=ident[:, :], in_=ident[:, :], compare_op=ALU.not_equal, fill=1.0, base=0,
                                    pattern=[[-1, P]], channel_multiplier=1)


def stage_layernorm(nc, name, src, zh, zl, z_keep, ident, ntok):
    tiles = ntok // P
    with ExitStack() as ctx:
        rows = ctx.enter_context(nc.sbuf_tensor(name + "_rows", [P, tiles, D], F32))
        stats = ctx.enter_context(nc.sbuf_tensor(name + "_stats", [P, tiles, 6], F32))
        mean_var = ctx.enter_context(nc.sbuf_tensor(name + "_mean_var", [P, tiles, 2], F32))
        var_eps = ctx.enter_context(nc.sbuf_tensor(name + "_var_eps", [P, tiles], F32))
        std = ctx.enter_context(nc.sbuf_tensor(name + "_std", [P, tiles], F32))
        rstd = ctx.enter_context(nc.sbuf_tensor(name + "_rstd", [P, tiles], F32))
        slots = 4 if z_keep is None else tiles
        z = ctx.enter_context(nc.sbuf_tensor(name + "_z", [P, slots, D], F32))
        turned = ctx.enter_context(nc.psum_tensor(name + "_turned", [P, 2, CHUNK], F32))
        parts = 4
        rows_in = [ctx.enter_context(nc.semaphore(f"{name}_rows_in{c}")) for c in range(parts)]
        stats_done = ctx.enter_context(nc.semaphore(name + "_stats_done"))
        std_done = ctx.enter_context(nc.semaphore(name + "_std_done"))
        z_done = ctx.enter_context(nc.semaphore(name + "_z_done"))
        z_kept = None if z_keep is None else ctx.enter_context(nc.semaphore(name + "_z_kept"))
        turned_done = ctx.enter_context(nc.semaphore(name + "_turned_done"))
        zh_done = ctx.enter_context(nc.semaphore(name + "_zh_done"))
        zl_done = ctx.enter_context(nc.semaphore(name + "_zl_done"))
        block = ctx.enter_context(nc.Block())
        src_t = src.rearrange("(t p) d -> p t d", p=P)
        per = tiles // parts

        @block.sync
        def _(sp):
            for c in range(parts):
                sp.dma_start(rows[:, c * per:(c + 1) * per, :],
                             src_t[:, c * per:(c + 1) * per, :]).then_inc(rows_in[c], 16)
            if z_keep is not None:
                keep_t = z_keep.rearrange("(t p) d -> p t d", p=P)
                for c in range(parts):
                    sp.wait_ge(z_done, (c + 1) * per)
                    sp.dma_start(keep_t[:, c * per:(c + 1) * per, :], z[:, c * per:(c + 1) * per, :]
                                 ).then_inc(z_kept, 16)
                sp.wait_ge(z_kept, 16 * parts)

        def z_slot(t):
            return z[:, t % slots, :]

        @block.vector
        def _(dve):
            for t in range(tiles):
                if t % per == 0:
                    dve.wait_ge(rows_in[t // per], 16)
                nc.vector.bn_stats(stats[:, t, :], rows[:, t, :]).then_inc(stats_done, 1)
            for t in range(tiles):
                dve.wait_ge(stats_done, t + 1)
                nc.vector.bn_aggr(mean_var[:, t, :], stats[:, t, :]).then_inc(stats_done, 1)
            dve.wait_ge(stats_done, 2 * tiles)
            nc.vector.tensor_scalar(var_eps[:, :], mean_var[:, :, 1], EPS, None, ALU.add).then_inc(stats_done, 1)
            dve.wait_ge(std_done, 1)
            nc.vector.reciprocal(rstd[:, :], std[:, :]).then_inc(std_done, 1)
            dve.wait_ge(std_done, 2)

            def low_part(g):
                dve.wait_ge(zh_done, g + 1)
                col = 2 * g * P
                nc.vector.tensor_tensor(zl[:, :, col:col + 2 * P],
                                        turned[:, g % 2, :].rearrange("p (k c) -> p k c", k=KT),
                                        zh[:, :, col:col + 2 * P].bitcast(F32),
                                        ALU.subtract).then_inc(zl_done, 1)

            for g in range(tiles // 2):
                for t in (2 * g, 2 * g + 1):
                    if z_keep is None and g >= 2:
                        dve.wait_ge(turned_done, g - 1)
                    nc.vector.tensor_scalar(z_slot(t), rows[:, t, :], mean_var[:, t, 0:1], rstd[:, t:t + 1],
                                            ALU.subtract, ALU.mult).then_inc(z_done, 1)
                if g >= 1:
                    low_part(g - 1)
            low_part(tiles // 2 - 1)

        @block.tensor
        def _(pe):
            for g in range(tiles // 2):
                pe.wait_ge(z_done, 2 * g + 2)
                if g >= 2:
                    pe.wait_ge(zl_done, g - 1)
                for j in range(2):
                    for k in range(KT):
                        last = nc.tensor.transpose(turned[:, g % 2, k * 2 * P + j * P:k * 2 * P + (j + 1) * P],
                                                   z_slot(2 * g + j)[:, k * P:(k + 1) * P], ident[:, :])
                last.then_inc(turned_done, 1)

        @block.scalar
        def _(act):
            act.wait_ge(stats_done, 2 * tiles + 1)
            nc.scalar.activation(std[:, :], var_eps[:, :], ACT.Sqrt).then_inc(std_done, 1)
            for g in range(tiles // 2):
                act.wait_ge(turned_done, g + 1)
                col = 2 * g * P
                nc.scalar.activation(zh[:, :, col:col + 2 * P],
                                     turned[:, g % 2, :].rearrange("p (k c) -> p k c", k=KT),
                                     ACT.Copy).then_inc(zh_done, 1)


def stage_factors(nc, u, v, ident, packed, pairs):
    with ExitStack() as ctx:
        nat = [ctx.enter_context(nc.sbuf_tensor(f"factor{i}", [P, pairs, D], F32)) for i in range(2)]
        rec = ctx.enter_context(nc.sbuf_tensor("factor_records", [P, pairs, 8, D], F32R))
        turned = ctx.enter_context(nc.psum_tensor("factor_turned", [P, 2, CHUNK], F32))
        factors_in = ctx.enter_context(nc.semaphore("factors_in"))
        nat_high = ctx.enter_context(nc.semaphore("nat_high"))
        nat_low = ctx.enter_context(nc.semaphore("nat_low"))
        turned_done = ctx.enter_context(nc.semaphore("factor_turned_done"))
        turned_high = ctx.enter_context(nc.semaphore("factor_turned_high"))
        turned_low = ctx.enter_context(nc.semaphore("factor_turned_low"))
        stored = ctx.enter_context(nc.semaphore("factors_stored"))
        block = ctx.enter_context(nc.Block())

        @block.sync
        def _(sp):
            for i, f in enumerate((u, v)):
                sp.dma_start(nat[i][:, :, :], f.rearrange("(c p) d -> p c d", p=P)).then_inc(factors_in, 16)
            for c in range(pairs):
                sp.wait_ge(nat_low, c + 1)
                sp.wait_ge(turned_low, c + 1)
                sp.dma_start(packed[c], rec[:, c, :, :].rearrange("p r d -> p (r d)").bitcast(F32)).then_inc(stored, 16)
            sp.wait_ge(stored, 16 * pairs)

        @block.tensor
        def _(pe):
            pe.wait_ge(factors_in, 32)
            for c in range(pairs):
                if c >= 2:
                    pe.wait_ge(turned_low, c - 1)
                for i in range(2):
                    for k in range(KT):
                        last = nc.tensor.transpose(turned[:, c % 2, i * D + k * P:i * D + (k + 1) * P],
                                                   nat[i][:, c, k * P:(k + 1) * P], ident[:, :])
                last.then_inc(turned_done, 1)

        @block.scalar
        def _(act):
            act.wait_ge(factors_in, 32)
            for c in range(pairs):
                for i in range(2):
                    last = nc.scalar.activation(rec[:, c, 4 + 2 * i, :], nat[i][:, c, :], ACT.Copy)
                    last.then_inc(nat_high, 1)
                act.wait_ge(turned_done, c + 1)
                nc.scalar.activation(rec[:, c, 0:3:2, :], turned[:, c % 2, :].rearrange("p (i d) -> p i d", i=2),
                                     ACT.Copy).then_inc(turned_high, 1)

        @block.vector
        def _(dve):
            dve.wait_ge(factors_in, 32)
            for c in range(pairs):
                dve.wait_ge(nat_high, 2 * c + 2)
                nc.vector.tensor_tensor(rec[:, c, 5, :], nat[0][:, c, :], rec[:, c, 4, :].bitcast(F32), ALU.subtract)
                nc.vector.tensor_tensor(rec[:, c, 7, :], nat[1][:, c, :], rec[:, c, 6, :].bitcast(F32),
                                        ALU.subtract).then_inc(nat_low, 1)
                dve.wait_ge(turned_high, c + 1)
                nc.vector.tensor_tensor(rec[:, c, 1:4:2, :], turned[:, c % 2, :].rearrange("p (i d) -> p i d", i=2),
                                        rec[:, c, 0:3:2, :].bitcast(F32), ALU.subtract).then_inc(turned_low, 1)


def stage_pairs(nc, x, x1, zh, zl, packed, ident, waited, batches, seq, pairs):
    SCALE = 0.03125
    R = 64
    STEPS = 32
    BLK = seq // P
    TURNS = batches * pairs
    JOBS = 12
    NEW = 8
    with ExitStack() as ctx:
        def sb(n, shape, dt):
            return ctx.enter_context(nc.sbuf_tensor(n, shape, dt))

        def sem(n):
            return ctx.enter_context(nc.semaphore(n))

        w = [sb(f"w{i}", [P, 8, D], F32R) for i in range(2)]
        proj = sb("proj", [P, 2, seq], F32)
        u_low = sb("u_low", [P, seq], F32R)
        u_stack = [sb(f"u_stack{i}", [P, 2, seq], F32R) for i in range(2)]
        v_high = [sb(f"v_high{i}", [P, 2, seq], F32R) for i in range(2)]
        v_low = [sb(f"v_low{i}", [P, 2, seq], F32R) for i in range(2)]
        nat = [sb(f"nat{i}", [P, 2, BLK, P], F32) for i in range(2)]
        probs = sb("probs", [P, 2, 2, CHUNK], F32)
        msg_high = sb("msg_high", [P, 2, seq], F32R)
        msg_low = sb("msg_low", [P, 2, seq], F32R)
        total = sb("total", [P, BLK, D], F32)
        f_ps = ctx.enter_context(nc.psum_tensor("f_ps", [P, 2, 2, CHUNK], F32))
        acc = ctx.enter_context(nc.psum_tensor("acc", [P, 2, CHUNK], F32))
        misc = ctx.enter_context(nc.psum_tensor("misc", [P, 2, CHUNK], F32))

        w_in = sem("w_in")
        x_in = sem("x_in")
        x1_out = sem("x1_out")
        f_ready = sem("f_ready")
        probs_ready = sem("probs_ready")
        acc_ready = sem("acc_ready")
        msg_high_ready = sem("msg_high_ready")
        msg_low_ready = sem("msg_low_ready")
        misc_ready = sem("misc_ready")
        misc_read = sem("misc_read")
        primed = sem("primed")
        split_high = sem("split_high")
        split_done = sem("split_done")
        u_low_moved = sem("u_low_moved")
        v_moved = sem("v_moved")
        block = ctx.enter_context(nc.Block())

        x_b = x.rearrange("(b t p) d -> b p t d", p=P, t=BLK)
        x1_b = x1.rearrange("(b t p) d -> b p t d", p=P, t=BLK)

        G_AT = {1: 0, 3: 1, 5: 2, 7: 3}
        P_AT = {11: 0, 13: 1, 15: 2, 17: 3}
        N_AT = {19: 0, 21: 1, 23: 2, 31: 3}

        @block.sync
        def _(sp):
            def load_w(slot, turn):
                sp.dma_start(w[slot][:, :, :].rearrange("p r d -> p (r d)").bitcast(F32),
                             packed[turn % pairs] if isinstance(turn, int) else
                             packed[bass.ds(turn % pairs, 1)].rearrange("o p n -> (o p) n")).then_inc(w_in, 16)

            def stacks(slot, turn):
                sp.wait_ge(split_done, turn * 2 + 1)
                sp.dma_start(u_stack[slot][R:P, 0, :].bitcast(F32), u_low[0:R, :].bitcast(F32)).then_inc(u_low_moved, 16)
                sp.dma_start(u_stack[slot][0:R, 1, :].bitcast(F32), u_low[R:P, :].bitcast(F32)).then_inc(u_low_moved, 16)
                sp.wait_ge(split_done, turn * 2 + 2)
                for part in (v_high, v_low):
                    sp.dma_start(part[slot][R:P, 0, :].bitcast(F32),
                                 part[slot][0:R, 0, :].bitcast(F32)).then_inc(v_moved, 16)
                    sp.dma_start(part[slot][0:R, 1, :].bitcast(F32),
                                 part[slot][R:P, 1, :].bitcast(F32)).then_inc(v_moved, 16)

            load_w(0, 0)
            load_w(1, 1)
            stacks(0, 0)
            with sp.Fori(0, TURNS, 2) as t0:
                for par in range(2):
                    turn = t0 + par
                    sp.wait_ge(misc_read, turn * JOBS + NEW + 4)
                    load_w(1 - par, turn + 1)
                    stacks(1 - par, turn + 1)
            sp.wait_ge(u_low_moved, 32 * (TURNS + 1))
            sp.wait_ge(v_moved, 64 * (TURNS + 1))

        @block.gpsimd
        def _(pool):
            nc.gpsimd.memset(msg_high[:, :, :].bitcast(F32), 0.0).then_inc(primed, 1)
            nc.gpsimd.memset(msg_low[:, :, :].bitcast(F32), 0.0).then_inc(msg_low_ready, 2)
            with pool.Fori(0, batches, 1) as b:
                pool.dma_start(total[:, :, :], x_b[bass.ds(b, 1)].rearrange("o p t d -> (o p) t d")).then_inc(x_in, 16)
                pool.wait_ge(misc_read, (b * pairs + pairs) * JOBS + NEW + 4)
                pool.sem_inc(waited, 1)
                pool.dma_start(x1_b[bass.ds(b, 1)].rearrange("o p t d -> (o p) t d"), total[:, :, :]).then_inc(x1_out, 16)
                pool.wait_ge(x1_out, b * 16 + 16)

        @block.tensor
        def _(pe):
            def f_step(par, s):
                kind, blk, chunk = s // 16, s % 16 // 2, s % 2
                rows = slice(blk * P, (blk + 1) * P)
                cols = slice(chunk * CHUNK, (chunk + 1) * CHUNK)
                for h in range(2):
                    for n, part in enumerate((v_high[par], v_low[par])):
                        lhs, rhs = u_stack[par][:, h, rows], part[:, h, cols]
                        if kind == 1:
                            lhs, rhs = part[:, h, rows], u_stack[par][:, h, cols]
                        last = nc.tensor.matmul(f_ps[:, s % 2, h, :], lhs, rhs, start=(n == 0), stop=(n == 1))
                last.then_inc(f_ready, 1)

            def msg_step(par, s, turn):
                kind, blk, chunk = s // 16, s % 16 // 2, s % 2
                pe.wait_ge(probs_ready, turn * STEPS + s + 1)
                if blk == 0:
                    pe.wait_ge(msg_low_ready, 2 + turn * 4 + (chunk - 1 if kind == 0 else chunk + 1))
                for h in range(2):
                    last = nc.tensor.matmul(acc[h * R:(h + 1) * R, chunk, :], nat[par][:, kind, blk, h * R:(h + 1) * R],
                                            probs[:, s % 2, h, :], start=(blk == 0), stop=(blk == BLK - 1))
                if blk == BLK - 1:
                    last.then_inc(acc_ready, 1)

            def g_job(slot, g, count):
                pe.wait_ge(misc_read, count - 1)
                for j in range(2):
                    tok = slice((2 * g + j) * P, (2 * g + j + 1) * P)
                    n = 0
                    for kind, f in ((0, 6), (1, 4)):
                        for lhs, rhs in ((msg_high, f), (msg_high, f + 1), (msg_low, f)):
                            last = nc.tensor.matmul(misc[:, g % 2, j * D:(j + 1) * D], lhs[:, kind, tok],
                                                    w[slot][:, rhs, :], start=(n == 0), stop=(n == 5))
                            n += 1
                last.then_inc(misc_ready, 1)

            def p_job(slot, p, turn, count):
                which, chunk = p // 2, p % 2
                if count is not None:
                    pe.wait_ge(misc_read, count - 1)
                n = 0
                for k in range(KT):
                    for a, z in ((0, zh), (0, zl), (1, zh)):
                        lhs = w[slot][:, 2 * which + a, k * P:(k + 1) * P]
                        if isinstance(turn, int):
                            rhs = z[:, k, chunk * CHUNK:(chunk + 1) * CHUNK]
                        else:
                            rhs = z[:, k, bass.ds((turn // pairs) % batches * seq + chunk * CHUNK, CHUNK)]
                        last = nc.tensor.matmul(misc[:, p % 2, :], lhs, rhs, start=(n == 0), stop=(n == 5))
                        n += 1
                last.then_inc(misc_ready, 1)

            def n_job(q, count):
                which, half = q // 2, q % 2
                pe.wait_ge(misc_read, count - 1)
                for j in range(4):
                    blk = 4 * half + j
                    last = nc.tensor.transpose(misc[:, q % 2, j * P:(j + 1) * P],
                                               proj[:, which, blk * P:(blk + 1) * P], ident[:, :])
                last.then_inc(misc_ready, 1)

            def new_jobs_first():
                for p in range(4):
                    p_job(0, p, 0, p if p >= 2 else None)
                for q in range(4):
                    if q == 0:
                        pe.wait_ge(misc_read, 4)
                    n_job(q, 4 + q)

            pe.wait_ge(w_in, 32)
            new_jobs_first()
            pe.wait_ge(primed, 1)
            pe.wait_ge(u_low_moved, 32)
            pe.wait_ge(v_moved, 64)
            f_step(0, 0)
            with pe.Fori(0, TURNS, 2) as t0:
                for par in range(2):
                    turn = t0 + par
                    base = turn * JOBS + NEW
                    for s in range(1, STEPS + 1):
                        if s < STEPS:
                            f_step(par, s)
                        else:
                            pe.wait_ge(u_low_moved, turn * 32 + 64)
                            pe.wait_ge(v_moved, turn * 64 + 128)
                            f_step(1 - par, 0)
                        if s == 1:
                            pe.wait_ge(misc_read, turn * JOBS + NEW)
                        msg_step(par, s - 1, turn)
                        if s in G_AT:
                            if s == 1:
                                pe.wait_ge(msg_low_ready, 2 + turn * 4)
                            g_job(1 - par, G_AT[s], base + G_AT[s])
                        if s in P_AT:
                            if P_AT[s] == 0:
                                pe.wait_ge(w_in, turn * 16 + 48)
                            p_job(1 - par, P_AT[s], turn + 1, base + 4 + P_AT[s])
                        if s in N_AT:
                            if N_AT[s] == 0:
                                pe.wait_ge(misc_read, base + 8)
                            n_job(N_AT[s], base + 8 + N_AT[s])
            pe.wait_ge(msg_low_ready, 2 + TURNS * 4)
            for g in range(4):
                g_job(1, g, TURNS * JOBS + NEW + g)

        @block.scalar
        def _(act):
            def msg_split(c, turn):
                act.wait_ge(acc_ready, turn * 4 + c + 1)
                kind, chunk = c // 2, c % 2
                nc.scalar.activation(msg_high[:, kind, chunk * CHUNK:(chunk + 1) * CHUNK], acc[:, chunk, :],
                                     ACT.Copy, scale=SCALE).then_inc(msg_high_ready, 1)

            def sigmoid(s, turn):
                act.wait_ge(f_ready, turn * STEPS + s + 1)
                nc.scalar.activation(probs[:, s % 2, :, :], f_ps[:, s % 2, :, :], ACT.Sigmoid).then_inc(probs_ready, 1)

            act.wait_ge(primed, 1)
            sigmoid(0, 0)
            with act.Fori(0, TURNS, 2) as t0:
                for par in range(2):
                    turn = t0 + par
                    for s in range(1, STEPS):
                        sigmoid(s, turn)
                        if s == 15:
                            act.wait_ge(misc_read, turn * JOBS + NEW + 4)
                            msg_split(0, turn)
                        if s == 16:
                            msg_split(1, turn)
                    msg_split(2, turn)
                    sigmoid(0, turn + 1)
                    msg_split(3, turn)

        @block.vector
        def _(dve):
            def low(c, turn):
                dve.wait_ge(msg_high_ready, turn * 4 + c + 1)
                kind, chunk = c // 2, c % 2
                cols = slice(chunk * CHUNK, (chunk + 1) * CHUNK)
                nc.vector.scalar_tensor_tensor(msg_low[:, kind, cols], acc[:, chunk, :], SCALE,
                                               msg_high[:, kind, cols].bitcast(F32), ALU.mult,
                                               ALU.subtract).then_inc(msg_low_ready, 1)

            def keep_proj(p, count):
                which, chunk = p // 2, p % 2
                dve.wait_ge(misc_ready, count + 1)
                nc.vector.tensor_scalar(proj[:, which, chunk * CHUNK:(chunk + 1) * CHUNK], misc[:, p % 2, :], SCALE,
                                        None, ALU.mult).then_inc(misc_read, 1)

            def split(slot, which, turn, count):
                dve.wait_ge(misc_read, count)
                high = (u_stack, v_high)[which][slot]
                if which == 0 and not isinstance(turn, int):
                    dve.wait_ge(u_low_moved, turn * 32)
                for h in range(2):
                    rows = slice(h * R, (h + 1) * R)
                    nc.vector.tensor_copy(high[rows, h, :], proj[rows, which, :]).then_inc(split_high, 1)
                dve.wait_ge(split_high, turn * 4 + 2 * which + 2)
                for h in range(2):
                    rows = slice(h * R, (h + 1) * R)
                    dst = u_low[rows, :] if which == 0 else v_low[slot][rows, h, :]
                    last = nc.vector.tensor_tensor(dst, proj[rows, which, :], high[rows, h, :].bitcast(F32),
                                                   ALU.subtract)
                last.then_inc(split_done, 1)

            def keep_nat(slot, q, count):
                which, half = q // 2, q % 2
                dve.wait_ge(misc_ready, count + 1)
                nc.vector.tensor_copy(nat[slot][:, which, 4 * half:4 * half + 4, :],
                                      misc[:, q % 2, :].rearrange("p (j r) -> p j r", j=4)).then_inc(misc_read, 1)

            def add_g(g, count):
                dve.wait_ge(misc_ready, count + 1)
                part = total[:, 2 * g:2 * g + 2, :]
                nc.vector.tensor_tensor(part, misc[:, g % 2, :].rearrange("p (j d) -> p j d", j=2), part,
                                        ALU.add).then_inc(misc_read, 1)

            for p in range(4):
                keep_proj(p, p)
                if p % 2 == 1:
                    split(0, p // 2, 0, p + 1)
            for q in range(4):
                keep_nat(0, q, 4 + q)
            dve.wait_ge(x_in, 16)
            with dve.Fori(0, TURNS, 2) as t0:
                for par in range(2):
                    turn = t0 + par
                    base = turn * JOBS + NEW
                    if par == 1:
                        dve.wait_ge(x_in, (turn + pairs - 1) // pairs * 16)
                    for g in range(4):
                        add_g(g, base + g)
                    keep_proj(0, base + 4)
                    keep_proj(1, base + 5)
                    split(1 - par, 0, turn + 1, base + 6)
                    low(0, turn)
                    keep_proj(2, base + 6)
                    low(1, turn)
                    keep_proj(3, base + 7)
                    split(1 - par, 1, turn + 1, base + 8)
                    for q in range(3):
                        keep_nat(1 - par, q, base + 8 + q)
                    low(2, turn)
                    keep_nat(1 - par, 3, base + 11)
                    low(3, turn)
            for g in range(4):
                add_g(g, TURNS * JOBS + NEW + g)


HEADS = 16
HD = 16
BIG = -1.0e37


def split_weights(nc, dve, act_or_none, src, high, low, sem, count):
    pass


def stage_qkv(nc, zh, zl, wq, wk, wv, qk_high, qk_low, v_aug, ident, ntok):
    CH = ntok // CHUNK
    with ExitStack() as ctx:
        def sb(n, shape, dt):
            return ctx.enter_context(nc.sbuf_tensor("qkv_" + n, shape, dt))

        def sem(n):
            return ctx.enter_context(nc.semaphore("qkv_" + n))

        raw = sb("raw", [P, 3, KT, D], F32)
        w_high = sb("w_high", [P, 3, KT, D], F32R)
        w_low = sb("w_low", [P, 3, KT, D], F32R)
        high = [sb(f"high{i}", [P, 4, CHUNK], F32R) for i in range(2)]
        low = [sb(f"low{i}", [P, 4, CHUNK], F32R) for i in range(2)]
        v_t = sb("v_t", [P, 2, CHUNK], F32)
        v_rows = [sb(f"v_rows{i}", [P, 4, HEADS, 2 * HD], F32) for i in range(2)]
        ps = ctx.enter_context(nc.psum_tensor("qkv_ps", [P, 6, CHUNK], F32))
        v_ps = ctx.enter_context(nc.psum_tensor("qkv_v_ps", [P, 2, CHUNK], F32))
        w_in, w_rounded, w_split, ones_set = sem("w_in"), sem("w_rounded"), sem("w_split"), sem("ones_set")
        proj_ready, high_ready, low_ready = sem("proj_ready"), sem("high_ready"), sem("low_ready")
        turned, v_ready, stored = sem("turned"), sem("v_ready"), sem("stored")
        block = ctx.enter_context(nc.Block())

        @block.sync
        def _(sp):
            sp.sem_inc(stored, 16)
            for i, w in enumerate((wq, wk, wv)):
                sp.dma_start(raw[:, i, :, :], w.rearrange("(k p) n -> p k n", p=P)).then_inc(w_in, 16)
            with sp.Fori(0, CH // 2, 1) as half:
                c0 = half * 2
                for par in range(2):
                    c = c0 + par
                    sp.wait_ge(low_ready, 1 + c * 4 + 4)
                    for dst, src in ((qk_high, high[par]), (qk_low, low[par])):
                        sp.dma_start(dst.rearrange("(j p) n -> p j n", p=P)[:, :, bass.ds(c * CHUNK, CHUNK)],
                                     src[:, :, :].bitcast(F32)).then_inc(stored, 16)
                    sp.wait_ge(v_ready, 1 + c * 2 + 2)
                    sp.dma_start(v_aug.rearrange("(t p) n -> p t n", p=P)[:, bass.ds(c * 4, 4), :],
                                 v_rows[par][:, :, :, :].rearrange("p t h e -> p t (h e)")).then_inc(stored, 16)
            sp.wait_ge(stored, 16 + 48 * CH)

        @block.gpsimd
        def _(pool):
            for i in range(2):
                nc.gpsimd.memset(v_rows[i][:, :, :, HD:], 1.0).then_inc(ones_set, 1)

        @block.tensor
        def _(pe):
            pe.sem_inc(turned, 1)
            pe.wait_ge(w_split, 3)
            with pe.Fori(0, CH, 1) as c:
                pe.wait_ge(high_ready, 1 + c * 6)
                pe.wait_ge(low_ready, 1 + c * 4)
                for j, (which, ct) in enumerate(((2, 0), (2, 1), (0, 0), (0, 1), (1, 0), (1, 1))):
                    n = 0
                    for k in range(KT):
                        for w, z in ((w_high, zh), (w_high, zl), (w_low, zh)):
                            last = nc.tensor.matmul(ps[:, j, :], w[:, which, k, ct * P:(ct + 1) * P],
                                                    z[:, k, bass.ds(c * CHUNK, CHUNK)], start=(n == 0), stop=(n == 5))
                            n += 1
                    last.then_inc(proj_ready, 1)
                pe.wait_ge(high_ready, 1 + c * 6 + 2)
                pe.wait_ge(v_ready, 1 + c * 2)
                for ct in range(2):
                    for j in range(4):
                        last = nc.tensor.transpose(v_ps[:, ct, j * P:(j + 1) * P], v_t[:, ct, j * P:(j + 1) * P],
                                                   ident[:, :])
                    last.then_inc(turned, 1)

        @block.scalar
        def _(act):
            act.sem_inc(high_ready, 1)
            act.wait_ge(w_in, 48)
            for i in range(3):
                nc.scalar.activation(w_high[:, i, :, :], raw[:, i, :, :], ACT.Copy).then_inc(w_rounded, 1)
            with act.Fori(0, CH // 2, 1) as half:
                c0 = half * 2
                for par in range(2):
                    c = c0 + par
                    act.wait_ge(turned, 1 + c * 2)
                    for j in range(2):
                        act.wait_ge(proj_ready, c * 6 + j + 1)
                        nc.scalar.activation(v_t[:, j, :], ps[:, j, :], ACT.Copy).then_inc(high_ready, 1)
                    act.wait_ge(stored, 16 + c0 * 48)
                    for j in range(4):
                        act.wait_ge(proj_ready, c * 6 + j + 3)
                        nc.scalar.activation(high[par][:, j, :], ps[:, j + 2, :], ACT.Copy,
                                             scale=(HD ** -0.5 if j < 2 else 1.0)).then_inc(high_ready, 1)

        @block.vector
        def _(dve):
            for counted in (low_ready, v_ready):
                dve.sem_inc(counted, 1)
            for i in range(3):
                dve.wait_ge(w_rounded, i + 1)
                nc.vector.tensor_tensor(w_low[:, i, :, :], raw[:, i, :, :], w_high[:, i, :, :].bitcast(F32),
                                        ALU.subtract).then_inc(w_split, 1)
            dve.wait_ge(ones_set, 2)
            with dve.Fori(0, CH // 2, 1) as half:
                c0 = half * 2
                for par in range(2):
                    c = c0 + par
                    dve.wait_ge(stored, 16 + c0 * 48)
                    for j in range(4):
                        dve.wait_ge(high_ready, 1 + c * 6 + j + 3)
                        nc.vector.scalar_tensor_tensor(low[par][:, j, :], ps[:, j + 2, :],
                                                       (HD ** -0.5 if j < 2 else 1.0), high[par][:, j, :].bitcast(F32),
                                                       ALU.mult, ALU.subtract).then_inc(low_ready, 1)
                    for ct in range(2):
                        dve.wait_ge(turned, 1 + c * 2 + ct + 1)
                        nc.vector.tensor_copy(v_rows[par][:, :, ct * 8:ct * 8 + 8, 0:HD],
                                              v_ps[:, ct, :].rearrange("p (t h e) -> p t h e", t=4, h=8)
                                              ).then_inc(v_ready, 1)


def stage_attention(nc, qk_high, qk_low, v_aug, o_raw, ident, waited, batches, seq):
    HQ = HEADS // 4
    TURNS = batches * HQ
    SLOTS = 4
    NB = seq // P
    GROUPS = [(kb, c) for c in range(2) for kb in range(4 * c + 4)]
    DIAG = [g for g, (kb, c) in enumerate(GROUPS) if kb // 4 == c]
    wide = sorted(((qb, c) for qb in range(NB) for c in range(qb // 4 + 1)), key=lambda u: u[1] * 4 - u[0])
    wide = sorted(wide, key=lambda u: -min(4, u[0] - u[1] * 4 + 1))
    UNITS = [(*u, h) for i in range(len(wide) // 2) for h in range(4) for u in (wide[i], wide[-1 - i])]
    NU = len(UNITS)
    NG = len(GROUPS)
    AHEAD = 2
    PER = NU // NG
    EARLY = 4
    with ExitStack() as ctx:
        def sb(n, shape, dt):
            return ctx.enter_context(nc.sbuf_tensor("att_" + n, shape, dt))

        def sem(n):
            return ctx.enter_context(nc.semaphore("att_" + n))

        k_stack = [sb(f"k_stack{i}", [P, 2, seq], F32R) for i in range(SLOTS)]
        q_stack = [sb(f"q_stack{i}", [P, 4, seq], F32R) for i in range(SLOTS)]
        v_win = [sb(f"v_win{i}", [P, NB, 4 * 2 * HD], F32) for i in range(SLOTS)]
        probs = sb("probs", [P, AHEAD + 1, 4, CHUNK], F32)
        mask = sb("mask", [P, CHUNK], F32)
        unused = sb("unused", [P, 3, CHUNK], mybir.dt.bfloat16)
        top = sb("top", [P, 2, 4, NB], F32)
        top2 = sb("top2", [P, 2, 4, NB // 2], F32)
        top_t = sb("top_t", [4 * NB, P], F32R)
        st = ctx.enter_context(nc.psum_tensor("att_st", [P, 2, 2, CHUNK], F32))
        s_ps = ctx.enter_context(nc.psum_tensor("att_s", [P, 3, CHUNK], F32))
        o_ps = ctx.enter_context(nc.psum_tensor("att_o", [P, CHUNK], F32))
        set_up, mask_set = [sem(f"set_up{i}") for i in range(SLOTS)], sem("mask_set")
        qk_in, v_in, top_in = ([sem(f"{n}{i}") for i in range(SLOTS)] for n in ("qk_in", "v_in", "top_in"))
        st_ready, exp_ready, sel_ready = sem("st_ready"), sem("exp_ready"), sem("sel_ready")
        s_ready, max_done, combined = sem("s_ready"), sem("max_done"), sem("combined")
        o_ready, o_kept = sem("o_ready"), sem("o_kept")
        block = ctx.enter_context(nc.Block())

        O_READY0, O_KEPT0 = 4, 2

        @block.sync
        def _(sp):
            def load(slot, turn):
                b, hq = turn // HQ, turn % HQ
                if isinstance(turn, int):
                    b = b % batches

                    def rows(d, base):
                        return d[base + hq * 64:base + hq * 64 + 64, b * seq:(b + 1) * seq]
                    v_src = v_aug[b * seq:(b + 1) * seq, hq * P:(hq + 1) * P]
                else:
                    b = b % batches
                    def rows(d, base):
                        return d[bass.ds(hq * 64 + base, 64), bass.ds(b * seq, seq)]
                    v_src = v_aug[bass.ds(b * seq, seq), bass.ds(hq * P, P)]
                for quad, kd, qd in ((0, qk_high, qk_high), (1, qk_low, qk_high), (2, qk_high, qk_low)):
                    at = 32 * quad
                    sp.dma_start(k_stack[slot][at:at + 32, :, :].bitcast(F32),
                                 rows(kd, D).rearrange("(pr r) n -> r pr n", r=32)).then_inc(qk_in[slot], 16)
                    for sub in range(2):
                        sp.dma_start(q_stack[slot][at + 16 * sub:at + 16 * sub + 16, sub:4:2, :].bitcast(F32),
                                     rows(qd, 0).rearrange("(pr s r) n -> s r pr n", s=2, r=16)[sub]
                                     ).then_inc(qk_in[slot], 16)
                sp.dma_start(v_win[slot][:, :, :], v_src.rearrange("(t p) n -> p t n", p=P)).then_inc(v_in[slot], 16)

            def tops(slot, turn):
                sp.wait_ge(max_done, turn * (NU + 1) + NU + 1)
                sp.dma_start(q_stack[slot][96:97, :, :].rearrange("o h (b q) -> o (h b) q", q=P).bitcast(F32),
                             top_t[:, :].bitcast(F32)).then_inc(top_in[slot], 16)

            for slot in range(2):
                sp.wait_ge(set_up[slot], 2)
                load(slot, slot)
            tops(0, 0)
            for slot in range(2, SLOTS):
                sp.wait_ge(set_up[slot], 2)
            with sp.Fori(0, TURNS // SLOTS, 1) as lap:
                for par in range(SLOTS):
                    turn = lap * SLOTS + par
                    sp.wait_ge(o_ready, O_READY0 + turn * 2 - 2)
                    load((par + 2) % SLOTS, turn + 2)
                    tops((par + 1) % SLOTS, turn + 1)
            for slot in range(SLOTS):
                loads = (TURNS + 2 - slot + SLOTS - 1) // SLOTS
                sp.wait_ge(qk_in[slot], 144 * loads)
                sp.wait_ge(v_in[slot], 16 * loads)
                sp.wait_ge(top_in[slot], 16 * ((TURNS + 1 - slot + SLOTS - 1) // SLOTS))

        @block.gpsimd
        def _(pool):
            nc.gpsimd.memset(mask[:, :], 0.0).then_inc(mask_set, 1)
            pool.wait_ge(mask_set, 1)
            nc.gpsimd.affine_select(out=mask[:, CHUNK - P:], in_=mask[:, CHUNK - P:], compare_op=ALU.is_ge, fill=BIG,
                                    base=0, pattern=[[-1, P]], channel_multiplier=1).then_inc(mask_set, 1)
            pool.wait_ge(mask_set, 2)
            for i in range(2, SLOTS):
                nc.gpsimd.memset(q_stack[i][:, :, :].bitcast(F32), 0.0).then_inc(set_up[i], 1)
                pool.wait_ge(set_up[i], 1)
                nc.gpsimd.memset(k_stack[i][96:97, :, :].bitcast(F32), 1.0).then_inc(set_up[i], 1)
                pool.wait_ge(set_up[i], 2)
            with pool.Fori(0, TURNS, 1) as turn:
                for g in DIAG:
                    kb = GROUPS[g][0]
                    pool.wait_ge(exp_ready, turn * (2 * NG) + 2 * g + 2)
                    pool.sem_inc(waited, 1)
                    part = probs[:, g % (AHEAD + 1), :, kb % 4 * P:kb % 4 * P + P]
                    nc.gpsimd.affine_select(out=part, in_=part, compare_op=ALU.is_ge, fill=0.0, base=0,
                                            pattern=[[0, 4], [1, P]], channel_multiplier=-1).then_inc(sel_ready, 1)

        @block.tensor
        def _(pe):
            def s_unit(slot, u, turn):
                qb, c, h = UNITS[u]
                n = CHUNK if qb // 4 > c else max(2, qb % 4 + 1) * P
                bank = (u + 1) % 3
                if u >= 3:
                    pe.wait_ge(max_done, turn * (NU + 1) + u - 2)
                elif u == 2 and not (isinstance(turn, int) and turn == 0):
                    pe.wait_ge(max_done, turn * (NU + 1))
                nc.tensor.matmul(s_ps[:, bank, 0:n], q_stack[slot][0:96, h, qb * P:(qb + 1) * P],
                                 k_stack[slot][0:96, h // 2, c * CHUNK:c * CHUNK + n],
                                 start=True, stop=True).then_inc(s_ready, 1)

            def top_unit(slot, turn):
                pe.wait_ge(combined, turn + 1)
                nc.tensor.transpose(s_ps[0:4 * NB, 0, 0:P],
                                    top[:, slot % 2, :, :].rearrange("p h b -> p (h b)"),
                                    ident[:, :]).then_inc(s_ready, 1)

            def st_unit(slot, g, pr, turn):
                kb, c = GROUPS[g]
                u = 2 * g + pr
                if not (isinstance(turn, int) and turn == 0 and u < 2):
                    pe.wait_ge(exp_ready, turn * (2 * NG) + u - 1)
                lo = min(kb % 4, 2) * P if kb // 4 == c else 0
                for h in range(2):
                    last = nc.tensor.matmul(st[:, u % 2, h, lo:CHUNK], k_stack[slot][0:97, pr, kb * P:(kb + 1) * P],
                                            q_stack[slot][0:97, 2 * pr + h, c * CHUNK + lo:(c + 1) * CHUNK],
                                            start=True, stop=True)
                last.then_inc(st_ready, 1)

            def pv(slot, g, turn):
                kb, c = GROUPS[g]
                if g in DIAG:
                    pe.wait_ge(sel_ready, turn * len(DIAG) + DIAG.index(g) + 1)
                else:
                    pe.wait_ge(exp_ready, turn * (2 * NG) + 2 * g + 2)
                if kb == 0:
                    pe.wait_ge(o_kept, O_KEPT0 + turn * 2 + c)
                lo = kb % 4 * P if kb // 4 == c else 0
                end = kb == 4 * c + 3
                for h in range(4):
                    last = nc.tensor.matmul(o_ps[32 * h:32 * h + 32, lo:CHUNK], v_win[slot][:, kb, 32 * h:32 * h + 32],
                                            probs[:, g % (AHEAD + 1), h, lo:CHUNK], start=(kb == 0), stop=end)
                if end:
                    last.then_inc(o_ready, 1)

            pe.sem_inc(o_ready, O_READY0)
            pe.wait_ge(qk_in[0], 144)
            for u in range(NU):
                s_unit(0, u, 0)
            top_unit(0, 0)
            pe.wait_ge(qk_in[1], 144)
            for u in range(PER * EARLY):
                s_unit(1, u, 1)
            pe.wait_ge(top_in[0], 16)
            for g in range(AHEAD):
                for pr in range(2):
                    st_unit(0, g, pr, 0)
            with pe.Fori(0, TURNS // SLOTS, 1) as lap:
                for par in range(SLOTS):
                    turn = lap * SLOTS + par
                    one, two = (par + 1) % SLOTS, (par + 2) % SLOTS
                    pe.wait_ge(v_in[par], lap * 16 + 16)
                    for g in range(NG):
                        if g < NG - EARLY:
                            todo = [(one, PER * (g + EARLY) + i, turn + 1) for i in range(PER)]
                        else:
                            todo = [(two, PER * (g + EARLY - NG) + i, turn + 2) for i in range(PER)]
                        first = g == NG - EARLY
                        if first:
                            pe.wait_ge(qk_in[two], (lap + (par + 2) // SLOTS) * 144 + 144)
                        ahead = (par, g + AHEAD, turn) if g + AHEAD < NG else (one, g + AHEAD - NG, turn + 1)
                        if g + AHEAD == NG:
                            pe.wait_ge(top_in[one], (lap + (par + 1) // SLOTS) * 16 + 16)
                        if not first:
                            s_unit(*todo[0])
                        st_unit(ahead[0], ahead[1], 0, ahead[2])
                        if not first:
                            s_unit(*todo[1])
                        st_unit(ahead[0], ahead[1], 1, ahead[2])
                        if first:
                            top_unit(one, turn + 1)
                            s_unit(*todo[0])
                            s_unit(*todo[1])
                        s_unit(*todo[2])
                        pv(par, g, turn)
                        s_unit(*todo[3])

        @block.scalar
        def _(act):
            def exps(g, turn):
                kb, c = GROUPS[g]
                lo = kb % 4 * P if kb // 4 == c else 0
                for pr in range(2):
                    u = 2 * g + pr
                    act.wait_ge(st_ready, turn * (2 * NG) + u + 1)
                    nc.scalar.activation(probs[:, g % (AHEAD + 1), 2 * pr:2 * pr + 2, lo:CHUNK], st[:, u % 2, :, lo:CHUNK],
                                         ACT.Exp).then_inc(exp_ready, 1)

            def keep(c, turn):
                act.wait_ge(o_ready, O_READY0 + turn * 2 + c + 1)
                nc.scalar.activation(o_raw[:, bass.ds(turn, 1), c * CHUNK:(c + 1) * CHUNK],
                                     o_ps[:, :].rearrange("p (o n) -> p o n", o=1), ACT.Copy).then_inc(o_kept, 1)

            act.sem_inc(o_kept, O_KEPT0)
            for g in range(AHEAD):
                exps(g, 0)
            with act.Fori(0, TURNS, 1) as turn:
                for g in range(NG):
                    if g + AHEAD < NG:
                        exps(g + AHEAD, turn)
                    else:
                        exps(g + AHEAD - NG, turn + 1)
                    if GROUPS[g] == (3, 0):
                        keep(0, turn)
                keep(1, turn)

        @block.vector
        def _(dve):
            def maxima(par, turn, units):
                for u in units:
                    qb, c, h = UNITS[u]
                    bank = (u + 1) % 3
                    dve.wait_ge(s_ready, turn * (NU + 1) + u + 1)
                    if qb // 4 == c:
                        dve.sem_inc(waited, 1)
                    n = CHUNK if qb // 4 > c else (qb % 4 + 1) * P
                    acc = top[:, par, h, qb:qb + 1] if c == 0 else top2[:, par, h, qb - 4:qb - 3]
                    if qb // 4 > c:
                        nc.vector.reduce_max(acc, s_ps[:, bank, 0:n], AX.X).then_inc(max_done, 1)
                    else:
                        nc.vector.tensor_tensor_reduce(out=unused[:, bank, 0:n], in0=s_ps[:, bank, 0:n],
                                                       in1=mask[:, CHUNK - n:], scale=1.0, scalar=BIG, op0=ALU.add,
                                                       op1=ALU.max, accum_out=acc).then_inc(max_done, 1)

            def negate(par, turn, before):
                dve.wait_ge(max_done, turn * (NU + 1) + NU)
                nc.vector.tensor_tensor(top[:, par, :, NB // 2:], top[:, par, :, NB // 2:], top2[:, par, :, :],
                                        ALU.max).then_inc(combined, 1)
                dve.wait_ge(s_ready, turn * (NU + 1) + NU + 1)
                if before is not None:
                    dve.wait_ge(*before)
                nc.vector.tensor_scalar(top_t[:, :], s_ps[0:4 * NB, 0, 0:P], -1.0, None,
                                        ALU.mult).then_inc(max_done, 1)

            for i in range(2):
                nc.vector.memset(q_stack[i][:, :, :].bitcast(F32), 0.0).then_inc(set_up[i], 1)
                nc.vector.memset(k_stack[i][96:97, :, :].bitcast(F32), 1.0).then_inc(set_up[i], 1)
            dve.wait_ge(mask_set, 2)
            maxima(0, 0, range(NU))
            negate(0, 0, None)
            maxima(1, 1, range(PER * EARLY))
            with dve.Fori(0, TURNS // SLOTS, 1) as lap:
                for par in range(SLOTS):
                    turn = lap * SLOTS + par
                    maxima((par + 1) % 2, turn + 1, range(PER * EARLY, NU))
                    negate((par + 1) % 2, turn + 1, (top_in[par], lap * 16 + 16))
                    maxima(par % 2, turn + 2, range(PER * EARLY))


EXPERTS = 8


def stage_router(nc, zh, zl, router, weights, ident, ntok):
    T = ntok // P
    CH = ntok // CHUNK
    E = EXPERTS
    with ExitStack() as ctx:
        def sb(n, shape, dt=F32):
            return ctx.enter_context(nc.sbuf_tensor("router_" + n, shape, dt))

        def sem(n):
            return ctx.enter_context(nc.semaphore("router_" + n))

        raw = sb("raw", [P, KT, E])
        w_high = sb("w_high", [P, KT, E], F32R)
        w_low = sb("w_low", [P, KT, E], F32R)
        logits_t = sb("logits_t", [E, ntok])
        top = sb("top", [P, T, 1])
        less = sb("less", [P, T, E])
        expo = sb("expo", [P, T, E])
        total = sb("total", [P, T, 1])
        share = sb("share", [P, T, 1])
        prob = sb("prob", [P, T, E])
        rank = sb("rank", [P, T, E])
        beats = sb("beats", [P, T, E])
        ps = ctx.enter_context(nc.psum_tensor("router_ps", [P, 2, CHUNK], F32))
        lg = ctx.enter_context(nc.psum_tensor("router_lg", [P, T, E], F32))
        w_in, logits_ready, kept = sem("w_in"), sem("logits_ready"), sem("kept")
        turned, step, less_ready, expo_ready = sem("turned"), sem("step"), sem("less_ready"), sem("expo_ready")
        block = ctx.enter_context(nc.Block())

        @block.sync
        def _(sp):
            sp.dma_start(raw[:, :, :], router.rearrange("(k p) e -> p k e", p=P)).then_inc(w_in, 16)

        @block.tensor
        def _(pe):
            pe.wait_ge(step, 2)
            for c in range(CH):
                if c >= 2:
                    pe.wait_ge(kept, c - 1)
                n = 0
                for k in range(KT):
                    for w, z in ((w_high, zh), (w_high, zl), (w_low, zh)):
                        last = nc.tensor.matmul(ps[0:E, c % 2, :], w[:, k, :], z[:, k, c * CHUNK:(c + 1) * CHUNK],
                                                start=(n == 0), stop=(n == 5))
                        n += 1
                last.then_inc(logits_ready, 1)
            pe.wait_ge(kept, CH)
            for t in range(T):
                last = nc.tensor.transpose(lg[:, t, :], logits_t[:, t * P:(t + 1) * P], ident[0:E, 0:E])
            last.then_inc(turned, 1)

        @block.scalar
        def _(act):
            for c in range(CH):
                act.wait_ge(logits_ready, c + 1)
                nc.scalar.activation(logits_t[:, c * CHUNK:(c + 1) * CHUNK], ps[0:E, c % 2, :],
                                     ACT.Copy).then_inc(kept, 1)
            act.wait_ge(less_ready, 1)
            nc.scalar.activation(expo[:, :, :], less[:, :, :], ACT.Exp).then_inc(expo_ready, 1)

        @block.vector
        def _(dve):
            count = [0]

            def link(ins):
                count[0] += 1
                ins.then_inc(step, 1)
                dve.wait_ge(step, count[0])

            def wide(ap):
                return ap.broadcast_to([P, T, E])

            dve.wait_ge(w_in, 16)
            link(nc.vector.tensor_copy(w_high[:, :, :], raw[:, :, :]))
            link(nc.vector.tensor_tensor(w_low[:, :, :], raw[:, :, :], w_high[:, :, :].bitcast(F32), ALU.subtract))
            dve.wait_ge(turned, 1)
            link(nc.vector.tensor_reduce(top[:, :, :].rearrange("p t o -> p (t o)"), lg[:, :, :], AX.X, ALU.max))
            nc.vector.tensor_tensor(less[:, :, :], lg[:, :, :], wide(top[:, :, :]), ALU.subtract).then_inc(less_ready, 1)
            link(nc.vector.memset(rank[:, :, :], 0.0))
            dve.wait_ge(expo_ready, 1)
            link(nc.vector.tensor_reduce(total[:, :, :].rearrange("p t o -> p (t o)"), expo[:, :, :], AX.X, ALU.add))
            link(nc.vector.reciprocal(share[:, :, :], total[:, :, :]))
            link(nc.vector.tensor_tensor(prob[:, :, :], expo[:, :, :], wide(share[:, :, :]), ALU.mult))
            for j in range(E):
                if j + 1 < E:
                    link(nc.vector.tensor_tensor(beats[:, :, j + 1:], prob[:, :, j:j + 1].broadcast_to([P, T, E - j - 1]),
                                                 prob[:, :, j + 1:], ALU.is_ge))
                link(nc.vector.tensor_tensor(beats[:, :, 0:j + 1], prob[:, :, j:j + 1].broadcast_to([P, T, j + 1]),
                                             prob[:, :, 0:j + 1], ALU.is_gt))
                link(nc.vector.tensor_tensor(rank[:, :, :], rank[:, :, :], beats[:, :, :], ALU.add))
            link(nc.vector.tensor_scalar(beats[:, :, :], rank[:, :, :], 2.0, None, ALU.is_lt))
            link(nc.vector.tensor_tensor(weights[:, :, :], prob[:, :, :], beats[:, :, :], ALU.mult))


def stage_experts(nc, zh, zl, ew1, ew2, ew3, weights, norm_w, x1, out, waited, ntok):
    TURN_CHUNKS = 2
    CH = ntok // CHUNK
    INNER = CH // TURN_CHUNKS
    TILES = CHUNK // P
    ROWS = TURN_CHUNKS * TILES
    LAST = (EXPERTS - 1) * INNER
    with ExitStack() as ctx:
        def sb(n, shape, dt=F32):
            return ctx.enter_context(nc.sbuf_tensor("moe_" + n, shape, dt))

        def sem(n):
            return ctx.enter_context(nc.semaphore("moe_" + n))

        raw = sb("raw", [P, 3, KT, D])
        w_high = [sb(f"w_high{i}", [P, 3, KT, D], F32R) for i in range(2)]
        w_low = [sb(f"w_low{i}", [P, 3, KT, D], F32R) for i in range(2)]
        silu = sb("silu", [P, 2, CHUNK])
        gate = sb("gate", [P, 2, CHUNK])
        g_high = sb("g_high", [P, 4, CHUNK], F32R)
        g_low = sb("g_low", [P, 4, CHUNK], F32R)
        moe = sb("sum", [P, ntok // P, D])
        w_row = sb("w_row", [P, D])
        x1_in = sb("x1_in", [P, ROWS, D])
        res = sb("res", [P, ROWS, D])
        squares = sb("squares", [P, ROWS, D])
        sums = sb("sums", [P, ROWS])
        ms = sb("ms", [P, ROWS])
        rms = sb("rms", [P, ROWS])
        inv = sb("inv", [P, ROWS])
        up = ctx.enter_context(nc.psum_tensor("moe_up", [P, 2, 2, CHUNK], F32))
        down = ctx.enter_context(nc.psum_tensor("moe_down", [P, 2, TILES, D], F32))
        raw_in, w_rounded, w_ready = sem("raw_in"), sem("w_rounded"), sem("w_ready")
        up_ready, silu_done, gate_done = sem("up_ready"), sem("silu_done"), sem("gate_done")
        high_done, low_done, down_ready, added = sem("high_done"), sem("low_done"), sem("down_ready"), sem("added")
        cleared = sem("cleared")
        row_in, rows_in, summed, ms_done, rms_done = sem("row_in"), sem("rows_in"), sem("summed"), sem("ms_done"), sem("rms_done")
        inv_done, scaled, finished, stored = (
            sem("inv_done"), sem("scaled"), sem("finished"), sem("stored"))
        block = ctx.enter_context(nc.Block())
        sources = (ew1, ew3, ew2)

        @block.sync
        def _(sp):
            def load(e):
                for i, w in enumerate(sources):
                    src = w[e] if isinstance(e, int) else w[bass.ds(e, 1)].rearrange("o d n -> (o d) n")
                    sp.dma_start(raw[:, i, :, :], src.rearrange("(k p) n -> p k n", p=P)).then_inc(raw_in, 16)

            sp.sem_inc(stored, 16)
            load(0)
            with sp.Fori(0, EXPERTS - 1, 1) as e:
                sp.wait_ge(w_ready, e + 1)
                load(e + 1)

            def rows(d, q):
                return d.rearrange("(t p) d -> p t d", p=P)[:, bass.ds(q * ROWS, ROWS), :]

            sp.dma_start(w_row[:, :], norm_w.rearrange("(o d) -> o d", o=1).broadcast_to([P, D])).then_inc(row_in, 16)
            sp.dma_start(x1_in[:, :, :], rows(x1, 0)).then_inc(rows_in, 16)
            with sp.Fori(0, INNER, 1) as q:
                sp.wait_ge(finished, (q + 1) * ROWS)
                sp.sem_inc(waited, 1)
                sp.dma_start(rows(out, q), res[:, :, :]).then_inc(stored, 16)
                sp.dma_start(x1_in[:, :, :], rows(x1, (q + 1) % INNER)).then_inc(rows_in, 16)
                sp.wait_ge(stored, 16 + q * 16 + 16)
                sp.sem_inc(waited, 1)
            sp.wait_ge(rows_in, 16 * (INNER + 1))

        @block.gpsimd
        def _(pool):
            def split(slot, e):
                pool.wait_ge(raw_in, e * 48 + 48)
                pool.sem_inc(waited, 1)
                nc.gpsimd.tensor_copy(w_high[slot][:, :, :, :], raw[:, :, :, :]).then_inc(w_rounded, 1)
                pool.wait_ge(w_rounded, e + 1)
                nc.gpsimd.tensor_tensor(w_low[slot][:, :, :, :], raw[:, :, :, :], w_high[slot][:, :, :, :].bitcast(F32),
                                        ALU.subtract).then_inc(w_ready, 1)

            split(0, 0)
            split(1, 1)
            with pool.Fori(0, EXPERTS // 2 - 1, 1) as half:
                for par in range(2):
                    pool.wait_ge(down_ready, (half * 2 + par + 1) * (2 * INNER))
                    split(par, half * 2 + par + 2)

        @block.tensor
        def _(pe):
            with pe.Fori(0, EXPERTS // 2, 1) as half:
                for par in range(2):
                    pe.wait_ge(w_ready, half * 2 + par + 1)
                    pe.sem_inc(waited, 1)
                    with pe.Fori(0, INNER, 1) as inner:
                        turn = (half * 2 + par) * INNER + inner
                        for j in range(4):
                            c, f = j // 2, j % 2
                            if j >= 2:
                                pe.wait_ge(gate_done, turn * 4 + j - 1)
                            for which in range(2):
                                n = 0
                                for k in range(KT):
                                    for w, z in ((w_high, zh), (w_high, zl), (w_low, zh)):
                                        last = nc.tensor.matmul(
                                            up[:, j % 2, which, :], w[par][:, which, k, f * P:(f + 1) * P],
                                            z[:, k, bass.ds(inner * (2 * CHUNK) + c * CHUNK, CHUNK)],
                                            start=(n == 0), stop=(n == 5))
                                        n += 1
                            last.then_inc(up_ready, 1)
                        for c in range(2):
                            pe.wait_ge(low_done, 1 + turn * 4 + 2 * c + 2)
                            if c == 0:
                                pe.wait_ge(added, 1 + turn * 8)
                            for i in range(TILES):
                                n = 0
                                for f in range(2):
                                    for g, w in ((g_high, w_high), (g_high, w_low), (g_low, w_high)):
                                        last = nc.tensor.matmul(down[:, c, i, :], g[:, 2 * c + f, i * P:(i + 1) * P],
                                                                w[par][:, 2, f, :], start=(n == 0), stop=(n == 5))
                                        n += 1
                            last.then_inc(down_ready, 1)

        @block.scalar
        def _(act):
            def high(j, turn):
                act.wait_ge(gate_done, turn * 4 + j + 1)
                nc.scalar.activation(g_high[:, j, :], gate[:, j % 2, :], ACT.Copy).then_inc(high_done, 1)

            def square_sums(turn):
                act.wait_ge(added, 1 + turn * ROWS)
                for i in range(ROWS):
                    nc.scalar.activation(squares[:, i, :].rearrange("p (o d) -> p o d", o=1),
                                         moe[:, bass.ds((turn - 1) % INNER * ROWS + i, 1), :], ACT.Square,
                                         accum_out=sums[:, i:i + 1]).then_inc(summed, 1)

            def root(turn):
                act.wait_ge(ms_done, turn - LAST)
                nc.scalar.activation(rms[:, :], ms[:, :], ACT.Sqrt).then_inc(rms_done, 1)

            def activate(turn, norm):
                for j in range(4):
                    act.wait_ge(up_ready, turn * 4 + j + 1)
                    nc.scalar.activation(silu[:, j % 2, :], up[:, j % 2, 0, :], ACT.Silu).then_inc(silu_done, 1)
                    if j >= 1:
                        high(j - 1, turn)
                    if norm and j == 1:
                        square_sums(turn)
                high(3, turn)
                if norm:
                    root(turn)

            with act.Fori(0, LAST + 1, 1) as turn:
                activate(turn, False)
            with act.Fori(LAST + 1, LAST + INNER, 1) as turn:
                activate(turn, True)
            square_sums(LAST + INNER)
            root(LAST + INNER)

        @block.vector
        def _(dve):
            def low(j, turn):
                dve.wait_ge(high_done, turn * 4 + j + 1)
                nc.vector.tensor_tensor(g_low[:, j, :], gate[:, j % 2, :], g_high[:, j, :].bitcast(F32),
                                        ALU.subtract).then_inc(low_done, 1)

            def gated(turn):
                for j in range(4):
                    dve.wait_ge(low_done, 1 + turn * 4 + max(j - 1, 0))
                    dve.wait_ge(silu_done, turn * 4 + j + 1)
                    nc.vector.tensor_tensor(gate[:, j % 2, :], up[:, j % 2, 1, :], silu[:, j % 2, :],
                                            ALU.mult).then_inc(gate_done, 1)
                    if j >= 1:
                        low(j - 1, turn)
                low(3, turn)

            def add(turn):
                dve.wait_ge(added, 1 + turn * ROWS)
                for c in range(2):
                    dve.wait_ge(down_ready, turn * 2 + c + 1)
                    for i in range(TILES):
                        tile = turn % INNER * ROWS + c * TILES + i
                        part = moe[:, bass.ds(tile, 1), :].rearrange("p o d -> p (o d)")
                        by = weights[:, bass.ds(tile, 1), bass.ds(turn // INNER, 1)].rearrange("p o e -> p (o e)")
                        nc.vector.scalar_tensor_tensor(part, down[:, c, i, :], by, part, ALU.mult,
                                                       ALU.add).then_inc(added, 1)

            def mean_squares(turn):
                dve.wait_ge(summed, (turn - LAST) * ROWS)
                nc.vector.tensor_scalar(ms[:, :], sums[:, :], 1.0 / D, EPS, ALU.mult, ALU.add).then_inc(ms_done, 1)

            def invert(turn):
                dve.wait_ge(rms_done, turn - LAST)
                nc.vector.reciprocal(inv[:, :], rms[:, :]).then_inc(inv_done, 1)

            def finish(turn):
                q = turn - LAST
                dve.wait_ge(rows_in, q * 16)
                dve.wait_ge(stored, 16 + q * 16 - 16)
                dve.wait_ge(inv_done, q)
                for i in range(ROWS):
                    tile = (turn - 1) % INNER * ROWS + i
                    nc.vector.scalar_tensor_tensor(res[:, i, :].rearrange("p (o d) -> p o d", o=1),
                                                   moe[:, bass.ds(tile, 1), :], inv[:, i:i + 1],
                                                   w_row[:, :].rearrange("p (o d) -> p o d", o=1),
                                                   ALU.mult, ALU.mult).then_inc(scaled, 1)
                for i in range(ROWS):
                    dve.wait_ge(scaled, (q - 1) * ROWS + i + 1)
                    nc.vector.tensor_tensor(res[:, i, :], res[:, i, :], x1_in[:, i, :], ALU.add).then_inc(finished, 1)

            for counted in (low_done, added):
                dve.sem_inc(counted, 1)
            nc.vector.memset(moe[:, :, :], 0.0).then_inc(cleared, 1)
            dve.wait_ge(cleared, 1)
            with dve.Fori(0, LAST + 1, 1) as turn:
                gated(turn)
                add(turn)
            dve.wait_ge(row_in, 16)
            with dve.Fori(LAST + 1, LAST + INNER, 1) as turn:
                gated(turn)
                mean_squares(turn)
                add(turn)
                invert(turn)
                finish(turn)
            mean_squares(LAST + INNER)
            invert(LAST + INNER)
            finish(LAST + INNER)


def stage_attention_out(nc, o_raw, z_rows, wo, norm_w, hh, hl, h_out, ident, batches, seq):
    ntok = batches * seq
    T = ntok // P
    HQ = HEADS // 4
    with ExitStack() as ctx:
        def sb(n, shape, dt=F32):
            return ctx.enter_context(nc.sbuf_tensor("ao_" + n, shape, dt))

        def sem(n):
            return ctx.enter_context(nc.semaphore("ao_" + n))

        raw = sb("raw", [P, KT, D])
        w_high = sb("w_high", [P, KT, D], F32R)
        w_low = sb("w_low", [P, KT, D], F32R)
        w_row = sb("w_row", [P, D])
        share = sb("share", [P, 2, HEADS, 1])
        o_rows = sb("o_rows", [P, 2, D])
        o_high = sb("o_high", [P, 2, KT, P], F32R)
        o_low = sb("o_low", [P, 2, KT, P], F32R)
        squares = sb("squares", [P, 2, D])
        sums = sb("sums", [P, 2, 1])
        ms = sb("ms", [P, 2, 1])
        rms = sb("rms", [P, 2, 1])
        inv = sb("inv", [P, 2, 1])
        scaled = sb("scaled", [P, 2, D])
        h = sb("h", [P, 4, D])
        t1 = ctx.enter_context(nc.psum_tensor("ao_t1", [P, 2, CHUNK], F32))
        t2 = ctx.enter_context(nc.psum_tensor("ao_t2", [P, 2, CHUNK], F32))
        prod = ctx.enter_context(nc.psum_tensor("ao_prod", [P, 2, CHUNK], F32))
        t3 = ctx.enter_context(nc.psum_tensor("ao_t3", [P, 2, CHUNK], F32))
        w_in, w_rounded, w_split = sem("w_in"), sem("w_rounded"), sem("w_split")
        t1_ready, share_done, rows_done, t2_ready = sem("t1_ready"), sem("share_done"), sem("rows_done"), sem("t2_ready")
        o_high_done, o_low_done, prod_ready = sem("o_high_done"), sem("o_low_done"), sem("prod_ready")
        sums_done, ms_done, rms_done, inv_done = sem("sums_done"), sem("ms_done"), sem("rms_done"), sem("inv_done")
        scaled_done, h_done, t3_ready = sem("scaled_done"), sem("h_done"), sem("t3_ready")
        h_high_done, h_low_done = sem("h_high_done"), sem("h_low_done")
        stored = [sem(f"stored{i}") for i in range(4)]
        z_in = [sem(f"z_in{i}") for i in range(2)]
        z = sb("z", [P, 2, 4, D])
        block = ctx.enter_context(nc.Block())

        @block.sync
        def _(sp):
            def load_z(c):
                sp.dma_start(z[:, c % 2, :, :], z_rows.rearrange("(t p) d -> p t d", p=P)[:, 4 * c:4 * c + 4, :]
                             ).then_inc(z_in[c % 2], 16)

            sp.dma_start(raw[:, :, :], wo.rearrange("(k p) n -> p k n", p=P)).then_inc(w_in, 16)
            sp.dma_start(w_row[:, :], norm_w.rearrange("(o d) -> o d", o=1).broadcast_to([P, D])).then_inc(w_in, 16)
            load_z(0)
            load_z(1)
            for t in range(T):
                sp.wait_ge(h_done, t + 1)
                if t % 4 == 3 and t + 4 < T - 1:
                    load_z(t // 4 + 2)
                sp.dma_start(h_out[t * P:(t + 1) * P, :], h[:, t % 4, :]).then_inc(stored[t % 4], 16)
            for i in range(4):
                sp.wait_ge(stored[i], 16 * (T // 4))

        @block.tensor
        def _(pe):
            def turn_heads(t):
                if t >= 2:
                    pe.wait_ge(rows_done, t - 1)
                at = t * P % seq
                for hq in range(HQ):
                    last = nc.tensor.transpose(t1[:, t % 2, hq * P:(hq + 1) * P],
                                               o_raw[:, t * P // seq * HQ + hq, at:at + P], ident[:, :])
                last.then_inc(t1_ready, 1)

            def turn_rows(t):
                pe.wait_ge(rows_done, t + 1)
                if t >= 2:
                    pe.wait_ge(o_low_done, t - 1)
                for k in range(KT):
                    last = nc.tensor.transpose(t2[:, t % 2, k * P:(k + 1) * P], o_rows[:, t % 2, k * P:(k + 1) * P],
                                               ident[:, :])
                last.then_inc(t2_ready, 1)

            def product(t):
                pe.wait_ge(o_low_done, t + 1)
                if t >= 2:
                    pe.wait_ge(scaled_done, t - 1)
                n = 0
                for k in range(KT):
                    for o, w in ((o_high, w_high), (o_high, w_low), (o_low, w_high)):
                        last = nc.tensor.matmul(prod[:, t % 2, 0:D], o[:, t % 2, k, :], w[:, k, :],
                                                start=(n == 0), stop=(n == 5))
                        n += 1
                last.then_inc(prod_ready, 1)

            def turn_h(t):
                pe.wait_ge(h_done, t + 1)
                if t >= 2:
                    pe.wait_ge(h_low_done, t - 1)
                for k in range(KT):
                    last = nc.tensor.transpose(t3[:, t % 2, k * P:(k + 1) * P], h[:, t % 4, k * P:(k + 1) * P],
                                               ident[:, :])
                last.then_inc(t3_ready, 1)

            pe.wait_ge(w_split, 1)
            for t in range(T + 3):
                if t < T:
                    turn_heads(t)
                if 0 <= t - 1 < T:
                    turn_rows(t - 1)
                if 0 <= t - 2 < T:
                    product(t - 2)
                if 0 <= t - 3 < T:
                    turn_h(t - 3)

        @block.scalar
        def _(act):
            act.wait_ge(w_in, 32)
            nc.scalar.activation(w_high[:, :, :], raw[:, :, :], ACT.Copy).then_inc(w_rounded, 1)
            for t in range(T + 3):
                if 0 <= t - 1 < T:
                    u = t - 1
                    act.wait_ge(t2_ready, u + 1)
                    if u >= 2:
                        act.wait_ge(prod_ready, u - 1)
                    nc.scalar.activation(o_high[:, u % 2, :, :], t2[:, u % 2, 0:D].rearrange("p (k c) -> p k c", k=KT),
                                         ACT.Copy).then_inc(o_high_done, 1)
                if 0 <= t - 2 < T:
                    u = t - 2
                    act.wait_ge(prod_ready, u + 1)
                    if u >= 2:
                        act.wait_ge(ms_done, u - 1)
                        act.wait_ge(sums_done, u - 1)
                    nc.scalar.activation(squares[:, u % 2, :], prod[:, u % 2, 0:D], ACT.Square,
                                         accum_out=sums[:, u % 2, :]).then_inc(sums_done, 1)
                    act.wait_ge(ms_done, u + 1)
                    if u >= 2:
                        act.wait_ge(inv_done, u - 1)
                    nc.scalar.activation(rms[:, u % 2, :], ms[:, u % 2, :], ACT.Sqrt).then_inc(rms_done, 1)
                if 0 <= t - 3 < T:
                    u = t - 3
                    act.wait_ge(t3_ready, u + 1)
                    nc.scalar.activation(hh[:, :, u * P:(u + 1) * P],
                                         t3[:, u % 2, 0:D].rearrange("p (k c) -> p k c", k=KT),
                                         ACT.Copy).then_inc(h_high_done, 1)

        @block.vector
        def _(dve):
            dve.wait_ge(w_rounded, 1)
            nc.vector.tensor_tensor(w_low[:, :, :], raw[:, :, :], w_high[:, :, :].bitcast(F32),
                                    ALU.subtract).then_inc(w_split, 1)
            for t in range(T + 3):
                if t < T:
                    dve.wait_ge(t1_ready, t + 1)
                    heads = t1[:, t % 2, :].rearrange("p (h e) -> p h e", e=2 * HD)
                    nc.vector.reciprocal(share[:, t % 2, :, :], heads[:, :, HD:HD + 1]).then_inc(share_done, 1)
                    dve.wait_ge(share_done, t + 1)
                    if t >= 2:
                        dve.wait_ge(t2_ready, t - 1)
                    nc.vector.tensor_tensor(o_rows[:, t % 2, :].rearrange("p (h e) -> p h e", e=HD), heads[:, :, 0:HD],
                                            share[:, t % 2, :, :].broadcast_to([P, HEADS, HD]),
                                            ALU.mult).then_inc(rows_done, 1)
                if 0 <= t - 1 < T:
                    u = t - 1
                    dve.wait_ge(o_high_done, u + 1)
                    nc.vector.tensor_tensor(o_low[:, u % 2, :, :], t2[:, u % 2, 0:D].rearrange("p (k c) -> p k c", k=KT),
                                            o_high[:, u % 2, :, :].bitcast(F32), ALU.subtract).then_inc(o_low_done, 1)
                if 0 <= t - 2 < T:
                    u = t - 2
                    dve.wait_ge(sums_done, u + 1)
                    nc.vector.tensor_scalar(ms[:, u % 2, :], sums[:, u % 2, :], 1.0 / D, EPS, ALU.mult,
                                            ALU.add).then_inc(ms_done, 1)
                    dve.wait_ge(rms_done, u + 1)
                    nc.vector.reciprocal(inv[:, u % 2, :], rms[:, u % 2, :]).then_inc(inv_done, 1)
                    dve.wait_ge(inv_done, u + 1)
                    nc.vector.scalar_tensor_tensor(scaled[:, u % 2, :], prod[:, u % 2, 0:D], inv[:, u % 2, :],
                                                   w_row[:, :], ALU.mult, ALU.mult).then_inc(scaled_done, 1)
                    dve.wait_ge(scaled_done, u + 1)
                    if u >= 4:
                        dve.wait_ge(stored[u % 4], 16 * (u // 4))
                        dve.wait_ge(t3_ready, u - 3)
                    if u % 4 == 0:
                        dve.wait_ge(z_in[u // 4 % 2], 16 * (u // 8 + 1))
                    nc.vector.tensor_tensor(h[:, u % 4, :], scaled[:, u % 2, :], z[:, u // 4 % 2, u % 4, :], ALU.add).then_inc(h_done, 1)
                if 0 <= t - 3 < T:
                    u = t - 3
                    dve.wait_ge(h_high_done, u + 1)
                    nc.vector.tensor_tensor(hl[:, :, u * P:(u + 1) * P],
                                            t3[:, u % 2, 0:D].rearrange("p (k c) -> p k c", k=KT),
                                            hh[:, :, u * P:(u + 1) * P].bitcast(F32), ALU.subtract).then_inc(h_low_done, 1)


def stage_ffn(nc, hh, hl, w1, w2, w3, norm_w, extras, out, waited, ntok):
    CH = ntok // CHUNK
    FT = w1.shape[1] // P
    TILES = CHUNK // P
    AHEAD = 2
    with ExitStack() as ctx:
        def sb(n, shape, dt=F32):
            return ctx.enter_context(nc.sbuf_tensor("ffn_" + n, shape, dt))

        def sem(n):
            return ctx.enter_context(nc.semaphore("ffn_" + n))

        SIZE = KT * FT * P
        raw = sb("raw", [P, 3, SIZE])
        w_high = sb("w_high", [P, 3, SIZE], F32R)
        w_low = sb("w_low", [P, 3, SIZE], F32R)
        silu = sb("silu", [P, 2, CHUNK])
        gate = sb("gate", [P, 2, CHUNK])
        g_high = sb("g_high", [P, 4, CHUNK], F32R)
        g_low = sb("g_low", [P, 4, CHUNK], F32R)
        w_row = sb("w_row", [P, D])
        extra_in = sb("extra_in", [P, len(extras), TILES, D])
        kept = sb("kept", [P, TILES, D])
        squares = sb("squares", [P, TILES, D])
        sums = sb("sums", [P, TILES])
        ms = sb("ms", [P, TILES])
        rms = sb("rms", [P, TILES])
        inv = sb("inv", [P, TILES])
        res = sb("res", [P, TILES, D])
        up = ctx.enter_context(nc.psum_tensor("ffn_up", [P, 2, 2, CHUNK], F32))
        down = ctx.enter_context(nc.psum_tensor("ffn_down", [P, TILES, CHUNK], F32))
        w_in = [sem(f"w_in{i}") for i in range(3)]
        w_rounded, w_ready, row_in = sem("w_rounded"), sem("w_ready"), sem("row_in")
        up_ready, silu_done, gate_done = sem("up_ready"), sem("silu_done"), sem("gate_done")
        high_done, low_done, down_ready, down_kept = (
            sem("high_done"), sem("low_done"), sem("down_ready"), sem("down_kept"))
        extras_in, summed, ms_done, rms_done, inv_done = (
            sem("extras_in"), sem("summed"), sem("ms_done"), sem("rms_done"), sem("inv_done"))
        adding, finished, stored = sem("adding"), sem("finished"), sem("stored")
        block = ctx.enter_context(nc.Block())
        out_t = out.rearrange("(t p) d -> p t d", p=P)

        @block.sync
        def _(sp):
            def load_extras(c):
                for i, x in enumerate(extras):
                    sp.dma_start(extra_in[:, i, :, :],
                                 x.rearrange("(t p) d -> p t d", p=P)[:, bass.ds(c * TILES, TILES), :]
                                 ).then_inc(extras_in, 16)

            for i, w in enumerate((w1, w3, w2)):
                sp.dma_start(raw[:, i, :].rearrange("p (k n) -> p k n", n=w.shape[1]),
                             w.rearrange("(k p) n -> p k n", p=P)).then_inc(w_in[i], 16)
            sp.dma_start(w_row[:, :], norm_w.rearrange("(o d) -> o d", o=1).broadcast_to([P, D])).then_inc(row_in, 16)
            load_extras(0)
            with sp.Fori(0, CH, 1) as c:
                sp.wait_ge(finished, (c + 1) * TILES)
                sp.sem_inc(waited, 1)
                sp.dma_start(out_t[:, bass.ds(c * TILES, TILES), :], res[:, :, :]).then_inc(stored, 16)
                load_extras((c + 1) % CH)
                sp.wait_ge(stored, c * 16 + 16)
                sp.sem_inc(waited, 1)
            sp.wait_ge(extras_in, 16 * len(extras) * (CH + 1))

        @block.tensor
        def _(pe):
            def up_job(c, f):
                if f >= FT:
                    c, f = c + 1, f - FT
                n = c * FT + f
                if not (isinstance(c, int) and n < 2):
                    pe.wait_ge(gate_done, n - 1)
                for which in range(2):
                    m = 0
                    for k in range(KT):
                        at = k * FT * P + f * P
                        for w, z in ((w_high, hh), (w_high, hl), (w_low, hh)):
                            last = nc.tensor.matmul(up[:, f % 2, which, :], w[:, which, at:at + P],
                                                    z[:, k, bass.ds(c % CH * CHUNK, CHUNK)],
                                                    start=(m == 0), stop=(m == 5))
                            m += 1
                last.then_inc(up_ready, 1)

            def down_job(c, f):
                pe.wait_ge(low_done, c * FT + f + 1)
                if f == 0 and not isinstance(c, int):
                    pe.wait_ge(down_kept, c)
                for i in range(TILES):
                    for n, (g, w) in enumerate(((g_high, w_high), (g_high, w_low), (g_low, w_high))):
                        last = nc.tensor.matmul(down[:, i, 0:D], g[:, f % 4, i * P:(i + 1) * P],
                                                w[:, 2, f * D:(f + 1) * D], start=(f == 0 and n == 0),
                                                stop=(f == FT - 1 and n == 2))
                if f == FT - 1:
                    last.then_inc(down_ready, 1)

            def chunk(c):
                for f in range(FT):
                    up_job(c, f + AHEAD)
                    down_job(c, f)

            pe.wait_ge(w_ready, 2)
            for f in range(AHEAD):
                up_job(0, f)
            pe.wait_ge(w_ready, 3)
            chunk(0)
            with pe.Fori(1, CH, 1) as c:
                chunk(c)

        @block.scalar
        def _(act):
            def activate(c, f):
                n = c * FT + f
                act.wait_ge(up_ready, n + 1)
                nc.scalar.activation(silu[:, f % 2, :], up[:, f % 2, 0, :], ACT.Silu).then_inc(silu_done, 1)

            def high(c, f):
                n = c * FT + f
                act.wait_ge(gate_done, n + 1)
                nc.scalar.activation(g_high[:, f % 4, :], gate[:, f % 2, :], ACT.Copy).then_inc(high_done, 1)

            def square_sums(c):
                act.wait_ge(down_kept, c)
                for i in range(TILES):
                    nc.scalar.activation(squares[:, i, :], kept[:, i, :], ACT.Square,
                                         accum_out=sums[:, i:i + 1]).then_inc(summed, 1)

            def root(c):
                act.wait_ge(ms_done, c)
                nc.scalar.activation(rms[:, :], ms[:, :], ACT.Sqrt).then_inc(rms_done, 1)

            def chunk(c):
                for f in range(FT):
                    activate(c, f + AHEAD)
                    high(c, f + AHEAD - 1)
                    if not isinstance(c, int):
                        if f == 0:
                            square_sums(c)
                        if f == 2:
                            root(c)

            for i in range(3):
                act.wait_ge(w_in[i], 16)
                nc.scalar.activation(w_high[:, i, :], raw[:, i, :], ACT.Copy).then_inc(w_rounded, 1)
            for f in range(AHEAD):
                activate(0, f)
                if f >= 1:
                    high(0, f - 1)
            chunk(0)
            with act.Fori(1, CH, 1) as c:
                chunk(c)
            square_sums(CH)
            root(CH)

        @block.vector
        def _(dve):
            def gated(c, f):
                n = c * FT + f
                if not (isinstance(c, int) and n < 2):
                    dve.wait_ge(low_done, n - 1)
                dve.wait_ge(silu_done, n + 1)
                nc.vector.tensor_tensor(gate[:, f % 2, :], up[:, f % 2, 1, :], silu[:, f % 2, :],
                                        ALU.mult).then_inc(gate_done, 1)

            def low(c, f):
                dve.wait_ge(high_done, c * FT + f + 1)
                nc.vector.tensor_tensor(g_low[:, f % 4, :], gate[:, f % 2, :], g_high[:, f % 4, :].bitcast(F32),
                                        ALU.subtract).then_inc(low_done, 1)

            def keep(c):
                dve.wait_ge(down_ready, c)
                nc.vector.tensor_copy(kept[:, :, :], down[:, :, 0:D]).then_inc(down_kept, 1)

            def mean_squares(c):
                dve.wait_ge(summed, c * TILES)
                nc.vector.tensor_scalar(ms[:, :], sums[:, :], 1.0 / D, EPS, ALU.mult, ALU.add).then_inc(ms_done, 1)

            def invert(c):
                dve.wait_ge(rms_done, c)
                nc.vector.reciprocal(inv[:, :], rms[:, :]).then_inc(inv_done, 1)
                dve.wait_ge(extras_in, c * (16 * len(extras)))
                if not (isinstance(c, int) and c == 1):
                    dve.wait_ge(stored, (c - 1) * 16 if isinstance(c, int) else c * 16 - 16)
                dve.wait_ge(inv_done, c)

            def finish(c, i):
                nc.vector.scalar_tensor_tensor(res[:, i, :], kept[:, i, :], inv[:, i:i + 1],
                                               w_row[:, :], ALU.mult, ALU.mult).then_inc(adding, 1)
                for n in range(len(extras)):
                    dve.wait_ge(adding, (c - 1) * (TILES * len(extras)) + i * len(extras) + n + 1)
                    last = nc.vector.tensor_tensor(res[:, i, :], res[:, i, :], extra_in[:, n, i, :], ALU.add)
                    last.then_inc(adding if n + 1 < len(extras) else finished, 1)

            def chunk(c):
                if not isinstance(c, int):
                    keep(c)
                for f in range(FT):
                    gated(c, f + AHEAD)
                    low(c, f + AHEAD - 1)
                    if not isinstance(c, int):
                        if f == 1:
                            mean_squares(c)
                        if f == 3:
                            invert(c)
                        if f >= FT - TILES:
                            finish(c, f - (FT - TILES))

            for i in range(3):
                dve.wait_ge(w_rounded, i + 1)
                nc.vector.tensor_tensor(w_low[:, i, :], raw[:, i, :], w_high[:, i, :].bitcast(F32),
                                        ALU.subtract).then_inc(w_ready, 1)
            dve.wait_ge(row_in, 16)
            for f in range(AHEAD):
                gated(0, f)
                if f >= 1:
                    low(0, f - 1)
            chunk(0)
            with dve.Fori(1, CH, 1) as c:
                chunk(c)
            keep(CH)
            mean_squares(CH)
            invert(CH)
            for i in range(TILES):
                finish(CH, i)


def seq_preln(nc, x, u, v, wq, wk, wv, wo, w1, w2, w3, attn_w, ff_w, moe_w, router, ew1, ew2, ew3, out):
    batches, seq, _ = x.shape
    ntok = batches * seq
    pairs = u.shape[0] // P
    x = x.rearrange("b s d -> (b s) d")
    out = out.rearrange("b s d -> (b s) d")

    def scratch(name, shape):
        return nc.dram_tensor(name, shape, F32, kind="Internal").ap()

    packed = scratch("packed_factors", (pairs, P, 8 * D))
    x1 = scratch("x1", (ntok, D))
    x1_sparse = scratch("x1_sparse", (ntok, D))
    y_rows = scratch("y_rows", (ntok, D))
    h_rows = scratch("h_rows", (ntok, D))
    qk_high = scratch("qk_high", (4 * P, ntok))
    qk_low = scratch("qk_low", (4 * P, ntok))
    v_aug = scratch("v_aug", (ntok, HEADS * 2 * HD))

    with ExitStack() as whole:
        ident = whole.enter_context(nc.sbuf_tensor("ident", [P, P], F32))
        waited = whole.enter_context(nc.semaphore("waited"))
        stage_identity(nc, ident)
        with ExitStack() as ctx:
            zh = ctx.enter_context(nc.sbuf_tensor("z1_high", [P, KT, ntok], F32R))
            zl = ctx.enter_context(nc.sbuf_tensor("z1_low", [P, KT, ntok], F32R))
            stage_layernorm(nc, "ln1", x, zh, zl, None, ident, ntok)
            stage_factors(nc, u, v, ident, packed, pairs)
            stage_pairs(nc, x, x1, zh, zl, packed, ident, waited, batches, seq, pairs)
        late = whole.enter_context(ExitStack())
        with ExitStack() as ctx:
            yh = ctx.enter_context(nc.sbuf_tensor("y_high", [P, KT, ntok], F32R))
            yl = ctx.enter_context(nc.sbuf_tensor("y_low", [P, KT, ntok], F32R))
            stage_layernorm(nc, "ln2", x1, yh, yl, y_rows, ident, ntok)
            stage_qkv(nc, yh, yl, wq, wk, wv, qk_high, qk_low, v_aug, ident, ntok)
            weights = ctx.enter_context(nc.sbuf_tensor("expert_weights", [P, ntok // P, EXPERTS], F32))
            stage_router(nc, yh, yl, router, weights, ident, ntok)
            stage_experts(nc, yh, yl, ew1, ew2, ew3, weights, moe_w, x1, x1_sparse, waited, ntok)
        late = whole.enter_context(ExitStack())
        with ExitStack() as ctx:
            o_raw = ctx.enter_context(nc.sbuf_tensor("o_raw", [P, batches * (HEADS // 4), seq], F32))
            stage_attention(nc, qk_high, qk_low, v_aug, o_raw, ident, waited, batches, seq)
            hh = late.enter_context(nc.sbuf_tensor("h_high", [P, KT, ntok], F32R, side="right"))
            hl = late.enter_context(nc.sbuf_tensor("h_low", [P, KT, ntok], F32R, side="right"))
            stage_attention_out(nc, o_raw, y_rows, wo, attn_w, hh, hl, h_rows, ident, batches, seq)
        stage_ffn(nc, hh, hl, w1, w2, w3, ff_w, [h_rows, x1_sparse], out, waited, ntok)


_INS = ["L0_attn_qz", "L0_attn_ternary_factor_u", "L0_attn_ternary_factor_v", "L0_ffn_wq", "L0_ffn_wk", "L0_ffn_wv",
        "L0_ffn_wo", "L0_ffn_w1", "L0_ffn_w2", "L0_ffn_w3", "L0_ffn_attn_norm_w", "L0_ffn_ff_norm_w",
        "L0_ffn_moe_norm_w", "L0_ffn_router_w", "L0_ffn_ew1", "L0_ffn_ew2", "L0_ffn_ew3"]


def kernel(**inputs):
    import concourse.bacc as bacc
    from concourse.bass_utils import run_bass_kernel_spmd

    nc = bacc.Bacc("TRN2", target_bir_lowering=False, num_devices=1)
    arrays, args = {}, []
    for name in _INS:
        a = np.ascontiguousarray(inputs[name])
        arrays[name] = a
        args.append(nc.dram_tensor(name, a.shape, mybir.dt.from_np(a.dtype), kind="ExternalInput").ap())
    out = nc.dram_tensor("out", arrays["L0_attn_qz"].shape, F32, kind="ExternalOutput").ap()
    seq_preln(nc, *args, out)
    result = run_bass_kernel_spmd(nc, [arrays], core_ids=[0])
    return result.results[0]["out"]
```

```python
from contextlib import ExitStack

import numpy as np

import concourse.bass as bass
from concourse import mybir

F32 = mybir.dt.float32
F32R = mybir.dt.float32r
ALU = mybir.AluOpType
ACT = mybir.ActivationFunctionType
AX = mybir.AxisListType

P = 128
D = 256
KT = D // P
EPS = 1e-5
CHUNK = 512


def stage_identity(nc, ident):
    with ExitStack() as ctx:
        cleared = ctx.enter_context(nc.semaphore("ident_cleared"))
        block = ctx.enter_context(nc.Block())

        @block.gpsimd
        def _(pool):
            nc.gpsimd.memset(ident[:, :], 0.0).then_inc(cleared, 1)
            pool.wait_ge(cleared, 1)
            nc.gpsimd.affine_select(out=ident[:, :], in_=ident[:, :], compare_op=ALU.not_equal, fill=1.0, base=0,
                                    pattern=[[-1, P]], channel_multiplier=1)


def start_early(sp, early):
    for dst, src, loaded in early:
        sp.dma_start(dst, src).then_inc(loaded, 16)


def stage_layernorm(nc, name, src, zh, zl, z_keep, ident, early, ntok):
    tiles = ntok // P
    PARTS = 8
    per = tiles // PARTS
    groups = per // 2
    BANKS = 4
    with ExitStack() as ctx:
        def sb(n, shape):
            return ctx.enter_context(nc.sbuf_tensor(name + "_" + n, shape, F32))

        def sem(n):
            return ctx.enter_context(nc.semaphore(name + "_" + n))

        rows = sb("rows", [P, tiles, D])
        stats = sb("stats", [P, tiles, 6])
        mean_var = sb("mean_var", [P, tiles, 2])
        var_eps = sb("var_eps", [P, tiles])
        std = sb("std", [P, tiles])
        rstd = sb("rstd", [P, tiles])
        shift = sb("shift", [P, tiles])
        slots = 8 if z_keep is None else tiles
        z = sb("z", [P, slots, D])
        turned = ctx.enter_context(nc.psum_tensor(name + "_turned", [P, BANKS, CHUNK], F32))
        rows_in = [sem(f"rows_in{i}") for i in range(2)]
        stats_done, vars_done = sem("stats_done"), sem("vars_done")
        std_done, rstd_done = sem("std_done"), sem("rstd_done")
        z_done, turned_done, zh_done, zl_done = sem("z_done"), sem("turned_done"), sem("zh_done"), sem("zl_done")
        z_kept = None if z_keep is None else sem("z_kept")
        block = ctx.enter_context(nc.Block())
        src_t = src.rearrange("(t p) d -> p t d", p=P)

        @block.sync
        def _(sp):
            for c in range(PARTS):
                if c >= 2:
                    sp.wait_ge(vars_done, c - 1)
                sp.dma_start(rows[:, c * per:(c + 1) * per, :],
                             src_t[:, c * per:(c + 1) * per, :]).then_inc(rows_in[c % 2], 16)
            start_early(sp, early)
            if z_keep is not None:
                keep_t = z_keep.rearrange("(t p) d -> p t d", p=P)
                for c in range(PARTS):
                    sp.wait_ge(z_done, (c + 1) * per)
                    sp.dma_start(keep_t[:, c * per:(c + 1) * per, :], z[:, c * per:(c + 1) * per, :]
                                 ).then_inc(z_kept, 16)
                sp.wait_ge(z_kept, 16 * PARTS)

        @block.vector
        def _(dve):
            def statistics(c):
                part = slice(c * per, (c + 1) * per)
                dve.wait_ge(rows_in[c % 2], 16 * (c // 2 + 1))
                for t in range(c * per, (c + 1) * per):
                    nc.vector.bn_stats(stats[:, t, :], rows[:, t, :]).then_inc(stats_done, 1)
                for t in range(c * per, (c + 1) * per):
                    dve.wait_ge(stats_done, c * (2 * per) + t - c * per + 1)
                    nc.vector.bn_aggr(mean_var[:, t, :], stats[:, t, :]).then_inc(stats_done, 1)
                dve.wait_ge(stats_done, (c + 1) * 2 * per)
                nc.vector.tensor_scalar(var_eps[:, part], mean_var[:, part, 1], EPS, None, ALU.add).then_inc(vars_done, 1)

            def scales(c):
                part = slice(c * per, (c + 1) * per)
                dve.wait_ge(std_done, c + 1)
                nc.vector.reciprocal(rstd[:, part], std[:, part]).then_inc(rstd_done, 1)
                dve.wait_ge(rstd_done, 2 * c + 1)
                nc.vector.scalar_tensor_tensor(shift[:, part], mean_var[:, part, 0], -1.0, rstd[:, part], ALU.mult,
                                               ALU.mult).then_inc(rstd_done, 1)

            def low_part(g):
                dve.wait_ge(zh_done, g + 1)
                col = 2 * g * P
                nc.vector.tensor_tensor(zl[:, :, col:col + 2 * P],
                                        turned[:, g % BANKS, :].rearrange("p (k c) -> p k c", k=KT),
                                        zh[:, :, col:col + 2 * P].bitcast(F32),
                                        ALU.subtract).then_inc(zl_done, 1)

            statistics(0)
            scales(0)
            statistics(1)
            scales(1)
            for c in range(PARTS):
                if c + 2 < PARTS:
                    statistics(c + 2)
                for i in range(groups):
                    low_part(c * groups + i)
                    if i == 0 and c + 2 < PARTS:
                        scales(c + 2)

        @block.tensor
        def _(pe):
            for g in range(tiles // 2):
                pe.wait_ge(z_done, 2 * g + 2)
                if g >= BANKS:
                    pe.wait_ge(zl_done, g - BANKS + 1)
                for j in range(2):
                    for k in range(KT):
                        last = nc.tensor.transpose(turned[:, g % BANKS, k * 2 * P + j * P:k * 2 * P + (j + 1) * P],
                                                   z[:, (2 * g + j) % slots, k * P:(k + 1) * P], ident[:, :])
                last.then_inc(turned_done, 1)

        @block.scalar
        def _(act):
            def root(c):
                part = slice(c * per, (c + 1) * per)
                act.wait_ge(vars_done, c + 1)
                nc.scalar.activation(std[:, part], var_eps[:, part], ACT.Sqrt).then_inc(std_done, 1)

            def normalize(g):
                if slots < tiles and 2 * g >= slots:
                    act.wait_ge(turned_done, g - slots // 2 + 1)
                for t in (2 * g, 2 * g + 1):
                    nc.scalar.activation(z[:, t % slots, :], rows[:, t, :], ACT.Identity, bias=shift[:, t:t + 1],
                                         scale=rstd[:, t:t + 1]).then_inc(z_done, 1)

            def high_part(g):
                act.wait_ge(turned_done, g + 1)
                col = 2 * g * P
                nc.scalar.activation(zh[:, :, col:col + 2 * P],
                                     turned[:, g % BANKS, :].rearrange("p (k c) -> p k c", k=KT),
                                     ACT.Copy).then_inc(zh_done, 1)

            root(0)
            root(1)
            for c in range(PARTS):
                act.wait_ge(rstd_done, 2 * c + 2)
                for i in range(groups):
                    g = c * groups + i
                    normalize(g)
                    if g >= 1:
                        high_part(g - 1)
                    if i == groups - 1 and c + 2 < PARTS:
                        root(c + 2)
            high_part(tiles // 2 - 1)


def stage_factors(nc, nat, factors_in, ident, packed, pairs):
    with ExitStack() as ctx:
        rec = ctx.enter_context(nc.sbuf_tensor("factor_records", [P, pairs, 8, D], F32R))
        turned = ctx.enter_context(nc.psum_tensor("factor_turned", [P, 2, CHUNK], F32))
        nat_high = ctx.enter_context(nc.semaphore("nat_high"))
        nat_low = ctx.enter_context(nc.semaphore("nat_low"))
        turned_done = ctx.enter_context(nc.semaphore("factor_turned_done"))
        turned_high = ctx.enter_context(nc.semaphore("factor_turned_high"))
        turned_low = ctx.enter_context(nc.semaphore("factor_turned_low"))
        stored = ctx.enter_context(nc.semaphore("factors_stored"))
        block = ctx.enter_context(nc.Block())

        @block.sync
        def _(sp):
            for c in range(pairs):
                sp.wait_ge(nat_low, c + 1)
                sp.wait_ge(turned_low, c + 1)
                sp.dma_start(packed[c], rec[:, c, :, :].rearrange("p r d -> p (r d)").bitcast(F32)).then_inc(stored, 16)
            sp.wait_ge(stored, 16 * pairs)

        @block.tensor
        def _(pe):
            pe.wait_ge(factors_in, 32)
            for c in range(pairs):
                if c >= 2:
                    pe.wait_ge(turned_low, c - 1)
                for i in range(2):
                    for k in range(KT):
                        last = nc.tensor.transpose(turned[:, c % 2, i * D + k * P:i * D + (k + 1) * P],
                                                   nat[i][:, c, k * P:(k + 1) * P], ident[:, :])
                last.then_inc(turned_done, 1)

        @block.scalar
        def _(act):
            act.wait_ge(factors_in, 32)
            for c in range(pairs):
                for i in range(2):
                    last = nc.scalar.activation(rec[:, c, 4 + 2 * i, :], nat[i][:, c, :], ACT.Copy)
                    last.then_inc(nat_high, 1)
                act.wait_ge(turned_done, c + 1)
                nc.scalar.activation(rec[:, c, 0:3:2, :], turned[:, c % 2, :].rearrange("p (i d) -> p i d", i=2),
                                     ACT.Copy).then_inc(turned_high, 1)

        @block.vector
        def _(dve):
            dve.wait_ge(factors_in, 32)
            for c in range(pairs):
                dve.wait_ge(nat_high, 2 * c + 2)
                nc.vector.tensor_tensor(rec[:, c, 5, :], nat[0][:, c, :], rec[:, c, 4, :].bitcast(F32), ALU.subtract)
                nc.vector.tensor_tensor(rec[:, c, 7, :], nat[1][:, c, :], rec[:, c, 6, :].bitcast(F32),
                                        ALU.subtract).then_inc(nat_low, 1)
                dve.wait_ge(turned_high, c + 1)
                nc.vector.tensor_tensor(rec[:, c, 1:4:2, :], turned[:, c % 2, :].rearrange("p (i d) -> p i d", i=2),
                                        rec[:, c, 0:3:2, :].bitcast(F32), ALU.subtract).then_inc(turned_low, 1)


def stage_pairs(nc, x, x1, zh, zl, packed, ident, waited, batches, seq, pairs):
    SCALE = 0.03125
    R = 64
    STEPS = 32
    BLK = seq // P
    TURNS = batches * pairs
    JOBS = 12
    NEW = 8
    with ExitStack() as ctx:
        def sb(n, shape, dt):
            return ctx.enter_context(nc.sbuf_tensor(n, shape, dt))

        def sem(n):
            return ctx.enter_context(nc.semaphore(n))

        w = [sb(f"w{i}", [P, 8, D], F32R) for i in range(2)]
        proj = sb("proj", [P, 2, seq], F32)
        u_low = sb("u_low", [P, seq], F32R)
        u_stack = [sb(f"u_stack{i}", [P, 2, seq], F32R) for i in range(2)]
        v_high = [sb(f"v_high{i}", [P, 2, seq], F32R) for i in range(2)]
        v_low = [sb(f"v_low{i}", [P, 2, seq], F32R) for i in range(2)]
        nat = [sb(f"nat{i}", [P, 2, BLK, P], F32) for i in range(2)]
        probs = sb("probs", [P, 2, 2, CHUNK], F32)
        msg_high = sb("msg_high", [P, 2, seq], F32R)
        msg_low = sb("msg_low", [P, 2, seq], F32R)
        total = sb("total", [P, BLK, D], F32)
        f_ps = ctx.enter_context(nc.psum_tensor("f_ps", [P, 2, 2, CHUNK], F32))
        acc = ctx.enter_context(nc.psum_tensor("acc", [P, 2, CHUNK], F32))
        misc = ctx.enter_context(nc.psum_tensor("misc", [P, 2, CHUNK], F32))

        w_in = sem("w_in")
        x_in = sem("x_in")
        x1_out = sem("x1_out")
        f_ready = sem("f_ready")
        probs_ready = sem("probs_ready")
        acc_ready = sem("acc_ready")
        msg_high_ready = sem("msg_high_ready")
        msg_low_ready = sem("msg_low_ready")
        misc_ready = sem("misc_ready")
        misc_read = sem("misc_read")
        primed = sem("primed")
        split_high = sem("split_high")
        split_done = sem("split_done")
        u_low_moved = sem("u_low_moved")
        v_moved = sem("v_moved")
        block = ctx.enter_context(nc.Block())

        x_b = x.rearrange("(b t p) d -> b p t d", p=P, t=BLK)
        x1_b = x1.rearrange("(b t p) d -> b p t d", p=P, t=BLK)

        G_AT = {1: 0, 3: 1, 5: 2, 7: 3}
        P_AT = {11: 0, 13: 1, 15: 2, 17: 3}
        N_AT = {19: 0, 21: 1, 23: 2, 31: 3}

        @block.sync
        def _(sp):
            def load_w(slot, turn):
                sp.dma_start(w[slot][:, :, :].rearrange("p r d -> p (r d)").bitcast(F32),
                             packed[turn % pairs] if isinstance(turn, int) else
                             packed[bass.ds(turn % pairs, 1)].rearrange("o p n -> (o p) n")).then_inc(w_in, 16)

            def stacks(slot, turn):
                sp.wait_ge(split_done, turn * 2 + 1)
                sp.dma_start(u_stack[slot][R:P, 0, :].bitcast(F32), u_low[0:R, :].bitcast(F32)).then_inc(u_low_moved, 16)
                sp.dma_start(u_stack[slot][0:R, 1, :].bitcast(F32), u_low[R:P, :].bitcast(F32)).then_inc(u_low_moved, 16)
                sp.wait_ge(split_done, turn * 2 + 2)
                for part in (v_high, v_low):
                    sp.dma_start(part[slot][R:P, 0, :].bitcast(F32),
                                 part[slot][0:R, 0, :].bitcast(F32)).then_inc(v_moved, 16)
                    sp.dma_start(part[slot][0:R, 1, :].bitcast(F32),
                                 part[slot][R:P, 1, :].bitcast(F32)).then_inc(v_moved, 16)

            load_w(0, 0)
            load_w(1, 1)
            stacks(0, 0)
            with sp.Fori(0, TURNS, 2) as t0:
                for par in range(2):
                    turn = t0 + par
                    sp.wait_ge(misc_read, turn * JOBS + NEW + 4)
                    load_w(1 - par, turn + 1)
                    stacks(1 - par, turn + 1)
            sp.wait_ge(u_low_moved, 32 * (TURNS + 1))
            sp.wait_ge(v_moved, 64 * (TURNS + 1))

        @block.gpsimd
        def _(pool):
            nc.gpsimd.memset(msg_high[:, :, :].bitcast(F32), 0.0).then_inc(primed, 1)
            nc.gpsimd.memset(msg_low[:, :, :].bitcast(F32), 0.0).then_inc(msg_low_ready, 2)
            with pool.Fori(0, batches, 1) as b:
                pool.dma_start(total[:, :, :], x_b[bass.ds(b, 1)].rearrange("o p t d -> (o p) t d")).then_inc(x_in, 16)
                pool.wait_ge(misc_read, (b * pairs + pairs) * JOBS + NEW + 4)
                pool.sem_inc(waited, 1)
                pool.dma_start(x1_b[bass.ds(b, 1)].rearrange("o p t d -> (o p) t d"), total[:, :, :]).then_inc(x1_out, 16)
                pool.wait_ge(x1_out, b * 16 + 16)

        @block.tensor
        def _(pe):
            def f_step(par, s):
                kind, blk, chunk = s // 16, s % 16 // 2, s % 2
                rows = slice(blk * P, (blk + 1) * P)
                cols = slice(chunk * CHUNK, (chunk + 1) * CHUNK)
                for h in range(2):
                    for n, part in enumerate((v_high[par], v_low[par])):
                        lhs, rhs = u_stack[par][:, h, rows], part[:, h, cols]
                        if kind == 1:
                            lhs, rhs = part[:, h, rows], u_stack[par][:, h, cols]
                        last = nc.tensor.matmul(f_ps[:, s % 2, h, :], lhs, rhs, start=(n == 0), stop=(n == 1))
                last.then_inc(f_ready, 1)

            def msg_step(par, s, turn):
                kind, blk, chunk = s // 16, s % 16 // 2, s % 2
                pe.wait_ge(probs_ready, turn * STEPS + s + 1)
                if blk == 0:
                    pe.wait_ge(msg_low_ready, 2 + turn * 4 + (chunk - 1 if kind == 0 else chunk + 1))
                for h in range(2):
                    last = nc.tensor.matmul(acc[h * R:(h + 1) * R, chunk, :], nat[par][:, kind, blk, h * R:(h + 1) * R],
                                            probs[:, s % 2, h, :], start=(blk == 0), stop=(blk == BLK - 1))
                if blk == BLK - 1:
                    last.then_inc(acc_ready, 1)

            def g_job(slot, g, count):
                pe.wait_ge(misc_read, count - 1)
                for j in range(2):
                    tok = slice((2 * g + j) * P, (2 * g + j + 1) * P)
                    n = 0
                    for kind, f in ((0, 6), (1, 4)):
                        for lhs, rhs in ((msg_high, f), (msg_high, f + 1), (msg_low, f)):
                            last = nc.tensor.matmul(misc[:, g % 2, j * D:(j + 1) * D], lhs[:, kind, tok],
                                                    w[slot][:, rhs, :], start=(n == 0), stop=(n == 5))
                            n += 1
                last.then_inc(misc_ready, 1)

            def p_job(slot, p, turn, count):
                which, chunk = p // 2, p % 2
                if count is not None:
                    pe.wait_ge(misc_read, count - 1)
                n = 0
                for k in range(KT):
                    for a, z in ((0, zh), (0, zl), (1, zh)):
                        lhs = w[slot][:, 2 * which + a, k * P:(k + 1) * P]
                        if isinstance(turn, int):
                            rhs = z[:, k, chunk * CHUNK:(chunk + 1) * CHUNK]
                        else:
                            rhs = z[:, k, bass.ds((turn // pairs) % batches * seq + chunk * CHUNK, CHUNK)]
                        last = nc.tensor.matmul(misc[:, p % 2, :], lhs, rhs, start=(n == 0), stop=(n == 5))
                        n += 1
                last.then_inc(misc_ready, 1)

            def n_job(q, count):
                which, half = q // 2, q % 2
                pe.wait_ge(misc_read, count - 1)
                for j in range(4):
                    blk = 4 * half + j
                    last = nc.tensor.transpose(misc[:, q % 2, j * P:(j + 1) * P],
                                               proj[:, which, blk * P:(blk + 1) * P], ident[:, :])
                last.then_inc(misc_ready, 1)

            def new_jobs_first():
                for p in range(4):
                    p_job(0, p, 0, p if p >= 2 else None)
                for q in range(4):
                    if q == 0:
                        pe.wait_ge(misc_read, 4)
                    n_job(q, 4 + q)

            pe.wait_ge(w_in, 32)
            new_jobs_first()
            pe.wait_ge(primed, 1)
            pe.wait_ge(u_low_moved, 32)
            pe.wait_ge(v_moved, 64)
            f_step(0, 0)
            with pe.Fori(0, TURNS, 2) as t0:
                for par in range(2):
                    turn = t0 + par
                    base = turn * JOBS + NEW
                    for s in range(1, STEPS + 1):
                        if s < STEPS:
                            f_step(par, s)
                        else:
                            pe.wait_ge(u_low_moved, turn * 32 + 64)
                            pe.wait_ge(v_moved, turn * 64 + 128)
                            f_step(1 - par, 0)
                        if s == 1:
                            pe.wait_ge(misc_read, turn * JOBS + NEW)
                        msg_step(par, s - 1, turn)
                        if s in G_AT:
                            if s == 1:
                                pe.wait_ge(msg_low_ready, 2 + turn * 4)
                            g_job(1 - par, G_AT[s], base + G_AT[s])
                        if s in P_AT:
                            if P_AT[s] == 0:
                                pe.wait_ge(w_in, turn * 16 + 48)
                            p_job(1 - par, P_AT[s], turn + 1, base + 4 + P_AT[s])
                        if s in N_AT:
                            if N_AT[s] == 0:
                                pe.wait_ge(misc_read, base + 8)
                            n_job(N_AT[s], base + 8 + N_AT[s])
            pe.wait_ge(msg_low_ready, 2 + TURNS * 4)
            for g in range(4):
                g_job(1, g, TURNS * JOBS + NEW + g)

        @block.scalar
        def _(act):
            def msg_split(c, turn):
                act.wait_ge(acc_ready, turn * 4 + c + 1)
                kind, chunk = c // 2, c % 2
                nc.scalar.activation(msg_high[:, kind, chunk * CHUNK:(chunk + 1) * CHUNK], acc[:, chunk, :],
                                     ACT.Copy, scale=SCALE).then_inc(msg_high_ready, 1)

            def sigmoid(s, turn):
                act.wait_ge(f_ready, turn * STEPS + s + 1)
                nc.scalar.activation(probs[:, s % 2, :, :], f_ps[:, s % 2, :, :], ACT.Sigmoid).then_inc(probs_ready, 1)

            act.wait_ge(primed, 1)
            sigmoid(0, 0)
            with act.Fori(0, TURNS, 2) as t0:
                for par in range(2):
                    turn = t0 + par
                    for s in range(1, STEPS):
                        sigmoid(s, turn)
                        if s == 15:
                            act.wait_ge(misc_read, turn * JOBS + NEW + 4)
                            msg_split(0, turn)
                        if s == 16:
                            msg_split(1, turn)
                    msg_split(2, turn)
                    sigmoid(0, turn + 1)
                    msg_split(3, turn)

        @block.vector
        def _(dve):
            def low(c, turn):
                dve.wait_ge(msg_high_ready, turn * 4 + c + 1)
                kind, chunk = c // 2, c % 2
                cols = slice(chunk * CHUNK, (chunk + 1) * CHUNK)
                nc.vector.scalar_tensor_tensor(msg_low[:, kind, cols], acc[:, chunk, :], SCALE,
                                               msg_high[:, kind, cols].bitcast(F32), ALU.mult,
                                               ALU.subtract).then_inc(msg_low_ready, 1)

            def keep_proj(p, count):
                which, chunk = p // 2, p % 2
                dve.wait_ge(misc_ready, count + 1)
                nc.vector.tensor_scalar(proj[:, which, chunk * CHUNK:(chunk + 1) * CHUNK], misc[:, p % 2, :], SCALE,
                                        None, ALU.mult).then_inc(misc_read, 1)

            def split(slot, which, turn, count):
                dve.wait_ge(misc_read, count)
                high = (u_stack, v_high)[which][slot]
                if which == 0 and not isinstance(turn, int):
                    dve.wait_ge(u_low_moved, turn * 32)
                for h in range(2):
                    rows = slice(h * R, (h + 1) * R)
                    nc.vector.tensor_copy(high[rows, h, :], proj[rows, which, :]).then_inc(split_high, 1)
                dve.wait_ge(split_high, turn * 4 + 2 * which + 2)
                for h in range(2):
                    rows = slice(h * R, (h + 1) * R)
                    dst = u_low[rows, :] if which == 0 else v_low[slot][rows, h, :]
                    last = nc.vector.tensor_tensor(dst, proj[rows, which, :], high[rows, h, :].bitcast(F32),
                                                   ALU.subtract)
                last.then_inc(split_done, 1)

            def keep_nat(slot, q, count):
                which, half = q // 2, q % 2
                dve.wait_ge(misc_ready, count + 1)
                nc.vector.tensor_copy(nat[slot][:, which, 4 * half:4 * half + 4, :],
                                      misc[:, q % 2, :].rearrange("p (j r) -> p j r", j=4)).then_inc(misc_read, 1)

            def add_g(g, count):
                dve.wait_ge(misc_ready, count + 1)
                part = total[:, 2 * g:2 * g + 2, :]
                nc.vector.tensor_tensor(part, misc[:, g % 2, :].rearrange("p (j d) -> p j d", j=2), part,
                                        ALU.add).then_inc(misc_read, 1)

            for p in range(4):
                keep_proj(p, p)
                if p % 2 == 1:
                    split(0, p // 2, 0, p + 1)
            for q in range(4):
                keep_nat(0, q, 4 + q)
            dve.wait_ge(x_in, 16)
            with dve.Fori(0, TURNS, 2) as t0:
                for par in range(2):
                    turn = t0 + par
                    base = turn * JOBS + NEW
                    if par == 1:
                        dve.wait_ge(x_in, (turn + pairs - 1) // pairs * 16)
                    for g in range(4):
                        add_g(g, base + g)
                    keep_proj(0, base + 4)
                    keep_proj(1, base + 5)
                    split(1 - par, 0, turn + 1, base + 6)
                    low(0, turn)
                    keep_proj(2, base + 6)
                    low(1, turn)
                    keep_proj(3, base + 7)
                    split(1 - par, 1, turn + 1, base + 8)
                    for q in range(3):
                        keep_nat(1 - par, q, base + 8 + q)
                    low(2, turn)
                    keep_nat(1 - par, 3, base + 11)
                    low(3, turn)
            for g in range(4):
                add_g(g, TURNS * JOBS + NEW + g)


HEADS = 16
HD = 16
BIG = -1.0e37


def stage_qkv(nc, held, zh, zl, raw, w_in, early, ew, waited, qk_high, qk_low, v_aug, ident, ntok):
    CH = ntok // CHUNK
    HIGH0, LOW0 = 6, 4
    with ExitStack() as ctx:
        def sb(n, shape, dt):
            return held.enter_context(nc.sbuf_tensor("qkv_" + n, shape, dt))

        def sem(n):
            return ctx.enter_context(nc.semaphore("qkv_" + n))

        w_high = sb("w_high", [P, 3, KT, D], F32R)
        w_low = sb("w_low", [P, 3, KT, D], F32R)
        high = [sb(f"high{i}", [P, 4, CHUNK], F32R) for i in range(2)]
        low = [sb(f"low{i}", [P, 4, CHUNK], F32R) for i in range(2)]
        v_t = sb("v_t", [P, 2, CHUNK], F32)
        v_rows = [sb(f"v_rows{i}", [P, 4, HEADS, 2 * HD], F32) for i in range(2)]
        ps = ctx.enter_context(nc.psum_tensor("qkv_ps", [P, 6, CHUNK], F32))
        v_ps = ctx.enter_context(nc.psum_tensor("qkv_v_ps", [P, 2, CHUNK], F32))
        w_rounded, w_split, ones_set = sem("w_rounded"), sem("w_split"), sem("ones_set")
        proj_ready, high_ready, low_ready = sem("proj_ready"), sem("high_ready"), sem("low_ready")
        turned, v_ready = sem("turned"), sem("v_ready")
        stored = held.enter_context(nc.semaphore("qkv_stored"))
        block = ctx.enter_context(nc.Block())

        @block.sync
        def _(sp):
            sp.sem_inc(stored, 16)
            start_early(sp, early)
            ew.load(sp, 0)
            sp.wait_ge(ew.ready, 1)
            ew.load(sp, 1)
            with sp.Fori(0, CH // 2, 1) as half:
                c0 = half * 2
                for par in range(2):
                    c = c0 + par
                    sp.wait_ge(low_ready, LOW0 + c * 4 + 4)
                    for dst, src in ((qk_high, high[par]), (qk_low, low[par])):
                        sp.dma_start(dst.rearrange("(j p) n -> p j n", p=P)[:, :, bass.ds(c * CHUNK, CHUNK)],
                                     src[:, :, :].bitcast(F32)).then_inc(stored, 16)
                    sp.wait_ge(v_ready, 1 + c * 2 + 2)
                    sp.dma_start(v_aug.rearrange("(t p) n -> p t n", p=P)[:, bass.ds(c * 4, 4), :],
                                 v_rows[par][:, :, :, :].rearrange("p t h e -> p t (h e)")).then_inc(stored, 16)

        @block.gpsimd
        def _(pool):
            for i in range(2):
                nc.gpsimd.memset(v_rows[i][:, :, :, HD:], 1.0).then_inc(ones_set, 1)
            pool.wait_ge(ones_set, 2)
            ew.split(pool, 0, 0, waited)
            pool.wait_ge(ew.ready, 1)
            ew.split(pool, 1, 1, waited)

        @block.tensor
        def _(pe):
            pe.sem_inc(turned, 1)
            pe.wait_ge(w_split, 3)
            with pe.Fori(0, CH, 1) as c:
                for j, (which, ct) in enumerate(((2, 0), (2, 1), (0, 0), (0, 1), (1, 0), (1, 1))):
                    if j < 2:
                        pe.wait_ge(high_ready, HIGH0 + c * 6 - 6 + j + 1)
                    else:
                        pe.wait_ge(low_ready, LOW0 + c * 4 - 4 + j - 1)
                    n = 0
                    for k in range(KT):
                        for w, z in ((w_high, zh), (w_high, zl), (w_low, zh)):
                            last = nc.tensor.matmul(ps[:, j, :], w[:, which, k, ct * P:(ct + 1) * P],
                                                    z[:, k, bass.ds(c * CHUNK, CHUNK)], start=(n == 0), stop=(n == 5))
                            n += 1
                    last.then_inc(proj_ready, 1)
                pe.wait_ge(high_ready, HIGH0 + c * 6 + 2)
                pe.wait_ge(v_ready, 1 + c * 2)
                for ct in range(2):
                    for j in range(4):
                        last = nc.tensor.transpose(v_ps[:, ct, j * P:(j + 1) * P], v_t[:, ct, j * P:(j + 1) * P],
                                                   ident[:, :])
                    last.then_inc(turned, 1)

        @block.scalar
        def _(act):
            act.sem_inc(high_ready, HIGH0)
            act.wait_ge(w_in, 48)
            for i in range(3):
                nc.scalar.activation(w_high[:, i, :, :], raw[:, i, :, :], ACT.Copy).then_inc(w_rounded, 1)
            with act.Fori(0, CH // 2, 1) as half:
                c0 = half * 2
                for par in range(2):
                    c = c0 + par
                    act.wait_ge(turned, 1 + c * 2)
                    for j in range(2):
                        act.wait_ge(proj_ready, c * 6 + j + 1)
                        nc.scalar.activation(v_t[:, j, :], ps[:, j, :], ACT.Copy).then_inc(high_ready, 1)
                    act.wait_ge(stored, 16 + c0 * 48)
                    for j in range(4):
                        act.wait_ge(proj_ready, c * 6 + j + 3)
                        nc.scalar.activation(high[par][:, j, :], ps[:, j + 2, :], ACT.Copy,
                                             scale=(HD ** -0.5 if j < 2 else 1.0)).then_inc(high_ready, 1)

        @block.vector
        def _(dve):
            dve.sem_inc(low_ready, LOW0)
            dve.sem_inc(v_ready, 1)
            for i in range(3):
                dve.wait_ge(w_rounded, i + 1)
                nc.vector.tensor_tensor(w_low[:, i, :, :], raw[:, i, :, :], w_high[:, i, :, :].bitcast(F32),
                                        ALU.subtract).then_inc(w_split, 1)
            dve.wait_ge(ones_set, 2)
            with dve.Fori(0, CH // 2, 1) as half:
                c0 = half * 2
                for par in range(2):
                    c = c0 + par
                    dve.wait_ge(stored, 16 + c0 * 48)
                    for j in range(4):
                        dve.wait_ge(high_ready, HIGH0 + c * 6 + j + 3)
                        nc.vector.scalar_tensor_tensor(low[par][:, j, :], ps[:, j + 2, :],
                                                       (HD ** -0.5 if j < 2 else 1.0), high[par][:, j, :].bitcast(F32),
                                                       ALU.mult, ALU.subtract).then_inc(low_ready, 1)
                    for ct in range(2):
                        dve.wait_ge(turned, 1 + c * 2 + ct + 1)
                        nc.vector.tensor_copy(v_rows[par][:, :, ct * 8:ct * 8 + 8, 0:HD],
                                              v_ps[:, ct, :].rearrange("p (t h e) -> p t h e", t=4, h=8)
                                              ).then_inc(v_ready, 1)
    return stored, 16 + 48 * CH


def stage_attention(nc, qk_high, qk_low, v_aug, o_raw, ident, waited, batches, seq):
    HQ = HEADS // 4
    TURNS = batches * HQ
    SLOTS = 4
    NB = seq // P
    GROUPS = [(kb, c) for c in range(2) for kb in range(4 * c + 4)]
    DIAG = [g for g, (kb, c) in enumerate(GROUPS) if kb // 4 == c]
    wide = sorted(((qb, c) for qb in range(NB) for c in range(qb // 4 + 1)), key=lambda u: u[1] * 4 - u[0])
    wide = sorted(wide, key=lambda u: -min(4, u[0] - u[1] * 4 + 1))
    UNITS = [(*u, h) for i in range(len(wide) // 2) for h in range(4) for u in (wide[i], wide[-1 - i])]
    NU = len(UNITS)
    NG = len(GROUPS)
    AHEAD = 2
    PER = NU // NG
    EARLY = 5
    with ExitStack() as ctx:
        def sb(n, shape, dt):
            return ctx.enter_context(nc.sbuf_tensor("att_" + n, shape, dt))

        def sem(n):
            return ctx.enter_context(nc.semaphore("att_" + n))

        k_stack = [sb(f"k_stack{i}", [P, 2, seq], F32R) for i in range(SLOTS)]
        q_stack = [sb(f"q_stack{i}", [P, 4, seq], F32R) for i in range(SLOTS)]
        v_win = [sb(f"v_win{i}", [P, NB, 4 * 2 * HD], F32) for i in range(SLOTS)]
        probs = sb("probs", [P, AHEAD + 1, 4, CHUNK], F32)
        mask = sb("mask", [P, CHUNK], F32)
        unused = sb("unused", [P, 3, CHUNK], mybir.dt.bfloat16)
        top = sb("top", [P, 2, 4, NB], F32)
        top2 = sb("top2", [P, 2, 4, NB // 2], F32)
        top_t = sb("top_t", [4 * NB, P], F32R)
        st = ctx.enter_context(nc.psum_tensor("att_st", [P, 2, 2, CHUNK], F32))
        s_ps = ctx.enter_context(nc.psum_tensor("att_s", [P, 3, CHUNK], F32))
        o_ps = ctx.enter_context(nc.psum_tensor("att_o", [P, CHUNK], F32))
        set_up, mask_set = [sem(f"set_up{i}") for i in range(SLOTS)], sem("mask_set")
        qk_in, v_in, top_in = ([sem(f"{n}{i}") for i in range(SLOTS)] for n in ("qk_in", "v_in", "top_in"))
        st_ready, exp_ready, sel_ready = sem("st_ready"), sem("exp_ready"), sem("sel_ready")
        s_ready, max_done, combined = sem("s_ready"), sem("max_done"), sem("combined")
        o_ready, o_kept = sem("o_ready"), sem("o_kept")
        block = ctx.enter_context(nc.Block())

        O_READY0, O_KEPT0 = 4, 2

        @block.sync
        def _(sp):
            def load(slot, turn):
                b, hq = turn // HQ, turn % HQ
                if isinstance(turn, int):
                    b = b % batches

                    def rows(d, base):
                        return d[base + hq * 64:base + hq * 64 + 64, b * seq:(b + 1) * seq]
                    v_src = v_aug[b * seq:(b + 1) * seq, hq * P:(hq + 1) * P]
                else:
                    b = b % batches
                    def rows(d, base):
                        return d[bass.ds(hq * 64 + base, 64), bass.ds(b * seq, seq)]
                    v_src = v_aug[bass.ds(b * seq, seq), bass.ds(hq * P, P)]
                for quad, kd, qd in ((0, qk_high, qk_high), (1, qk_low, qk_high), (2, qk_high, qk_low)):
                    at = 32 * quad
                    sp.dma_start(k_stack[slot][at:at + 32, :, :].bitcast(F32),
                                 rows(kd, D).rearrange("(pr r) n -> r pr n", r=32)).then_inc(qk_in[slot], 16)
                    for sub in range(2):
                        sp.dma_start(q_stack[slot][at + 16 * sub:at + 16 * sub + 16, sub:4:2, :].bitcast(F32),
                                     rows(qd, 0).rearrange("(pr s r) n -> s r pr n", s=2, r=16)[sub]
                                     ).then_inc(qk_in[slot], 16)
                sp.dma_start(v_win[slot][:, :, :], v_src.rearrange("(t p) n -> p t n", p=P)).then_inc(v_in[slot], 16)

            def tops(slot, turn):
                sp.wait_ge(max_done, turn * (NU + 1) + NU + 1)
                sp.dma_start(q_stack[slot][96:97, :, :].rearrange("o h (b q) -> o (h b) q", q=P).bitcast(F32),
                             top_t[:, :].bitcast(F32)).then_inc(top_in[slot], 16)

            for slot in range(2):
                sp.wait_ge(set_up[slot], 2)
                load(slot, slot)
            tops(0, 0)
            for slot in range(2, SLOTS):
                sp.wait_ge(set_up[slot], 2)
            with sp.Fori(0, TURNS // SLOTS, 1) as lap:
                for par in range(SLOTS):
                    turn = lap * SLOTS + par
                    sp.wait_ge(o_ready, O_READY0 + turn * 2 - 2)
                    load((par + 2) % SLOTS, turn + 2)
                    tops((par + 1) % SLOTS, turn + 1)
            for slot in range(SLOTS):
                loads = (TURNS + 2 - slot + SLOTS - 1) // SLOTS
                sp.wait_ge(qk_in[slot], 144 * loads)
                sp.wait_ge(v_in[slot], 16 * loads)
                sp.wait_ge(top_in[slot], 16 * ((TURNS + 1 - slot + SLOTS - 1) // SLOTS))

        @block.gpsimd
        def _(pool):
            nc.gpsimd.memset(mask[:, :], 0.0).then_inc(mask_set, 1)
            pool.wait_ge(mask_set, 1)
            nc.gpsimd.affine_select(out=mask[:, CHUNK - P:], in_=mask[:, CHUNK - P:], compare_op=ALU.is_ge, fill=BIG,
                                    base=0, pattern=[[-1, P]], channel_multiplier=1).then_inc(mask_set, 1)
            pool.wait_ge(mask_set, 2)
            for i in range(2, SLOTS):
                nc.gpsimd.memset(q_stack[i][:, :, :].bitcast(F32), 0.0).then_inc(set_up[i], 1)
                pool.wait_ge(set_up[i], 1)
                nc.gpsimd.memset(k_stack[i][96:97, :, :].bitcast(F32), 1.0).then_inc(set_up[i], 1)
                pool.wait_ge(set_up[i], 2)
            with pool.Fori(0, TURNS, 1) as turn:
                for g in DIAG:
                    kb = GROUPS[g][0]
                    pool.wait_ge(exp_ready, turn * (2 * NG) + 2 * g + 2)
                    pool.sem_inc(waited, 1)
                    part = probs[:, g % (AHEAD + 1), :, kb % 4 * P:kb % 4 * P + P]
                    nc.gpsimd.affine_select(out=part, in_=part, compare_op=ALU.is_ge, fill=0.0, base=0,
                                            pattern=[[0, 4], [1, P]], channel_multiplier=-1).then_inc(sel_ready, 1)

        @block.tensor
        def _(pe):
            def s_unit(slot, u, turn):
                qb, c, h = UNITS[u]
                n = CHUNK if qb // 4 > c else max(2, qb % 4 + 1) * P
                bank = (u + 1) % 3
                if u >= 3:
                    pe.wait_ge(max_done, turn * (NU + 1) + u - 2)
                elif u == 2 and not (isinstance(turn, int) and turn == 0):
                    pe.wait_ge(max_done, turn * (NU + 1))
                nc.tensor.matmul(s_ps[:, bank, 0:n], q_stack[slot][0:96, h, qb * P:(qb + 1) * P],
                                 k_stack[slot][0:96, h // 2, c * CHUNK:c * CHUNK + n],
                                 start=True, stop=True).then_inc(s_ready, 1)

            def top_unit(slot, turn):
                pe.wait_ge(combined, turn + 1)
                nc.tensor.transpose(s_ps[0:4 * NB, 0, 0:P],
                                    top[:, slot % 2, :, :].rearrange("p h b -> p (h b)"),
                                    ident[:, :]).then_inc(s_ready, 1)

            def st_unit(slot, g, pr, turn):
                kb, c = GROUPS[g]
                u = 2 * g + pr
                if not (isinstance(turn, int) and turn == 0 and u < 2):
                    pe.wait_ge(exp_ready, turn * (2 * NG) + u - 1)
                lo = min(kb % 4, 2) * P if kb // 4 == c else 0
                for h in range(2):
                    last = nc.tensor.matmul(st[:, u % 2, h, lo:CHUNK], k_stack[slot][0:97, pr, kb * P:(kb + 1) * P],
                                            q_stack[slot][0:97, 2 * pr + h, c * CHUNK + lo:(c + 1) * CHUNK],
                                            start=True, stop=True)
                last.then_inc(st_ready, 1)

            def pv(slot, g, turn):
                kb, c = GROUPS[g]
                if g in DIAG:
                    pe.wait_ge(sel_ready, turn * len(DIAG) + DIAG.index(g) + 1)
                else:
                    pe.wait_ge(exp_ready, turn * (2 * NG) + 2 * g + 2)
                if kb == 0:
                    pe.wait_ge(o_kept, O_KEPT0 + turn * 2 + c)
                lo = kb % 4 * P if kb // 4 == c else 0
                end = kb == 4 * c + 3
                for h in range(4):
                    last = nc.tensor.matmul(o_ps[32 * h:32 * h + 32, lo:CHUNK], v_win[slot][:, kb, 32 * h:32 * h + 32],
                                            probs[:, g % (AHEAD + 1), h, lo:CHUNK], start=(kb == 0), stop=end)
                if end:
                    last.then_inc(o_ready, 1)

            pe.sem_inc(o_ready, O_READY0)
            pe.wait_ge(qk_in[0], 144)
            for u in range(NU):
                s_unit(0, u, 0)
            top_unit(0, 0)
            pe.wait_ge(qk_in[1], 144)
            for u in range(PER * EARLY):
                s_unit(1, u, 1)
            pe.wait_ge(top_in[0], 16)
            for g in range(AHEAD):
                for pr in range(2):
                    st_unit(0, g, pr, 0)
            with pe.Fori(0, TURNS // SLOTS, 1) as lap:
                for par in range(SLOTS):
                    turn = lap * SLOTS + par
                    one, two = (par + 1) % SLOTS, (par + 2) % SLOTS
                    pe.wait_ge(v_in[par], lap * 16 + 16)
                    for g in range(NG):
                        if g < NG - EARLY:
                            todo = [(one, PER * (g + EARLY) + i, turn + 1) for i in range(PER)]
                        else:
                            todo = [(two, PER * (g + EARLY - NG) + i, turn + 2) for i in range(PER)]
                        first = g == NG - EARLY
                        if first:
                            pe.wait_ge(qk_in[two], (lap + (par + 2) // SLOTS) * 144 + 144)
                        ahead = (par, g + AHEAD, turn) if g + AHEAD < NG else (one, g + AHEAD - NG, turn + 1)
                        if g + AHEAD == NG:
                            pe.wait_ge(top_in[one], (lap + (par + 1) // SLOTS) * 16 + 16)
                        if not first:
                            s_unit(*todo[0])
                        st_unit(ahead[0], ahead[1], 0, ahead[2])
                        if not first:
                            s_unit(*todo[1])
                        st_unit(ahead[0], ahead[1], 1, ahead[2])
                        if first:
                            top_unit(one, turn + 1)
                            s_unit(*todo[0])
                            s_unit(*todo[1])
                        s_unit(*todo[2])
                        pv(par, g, turn)
                        s_unit(*todo[3])

        @block.scalar
        def _(act):
            def exps(g, turn):
                kb, c = GROUPS[g]
                lo = kb % 4 * P if kb // 4 == c else 0
                for pr in range(2):
                    u = 2 * g + pr
                    act.wait_ge(st_ready, turn * (2 * NG) + u + 1)
                    nc.scalar.activation(probs[:, g % (AHEAD + 1), 2 * pr:2 * pr + 2, lo:CHUNK], st[:, u % 2, :, lo:CHUNK],
                                         ACT.Exp).then_inc(exp_ready, 1)

            def keep(c, turn):
                act.wait_ge(o_ready, O_READY0 + turn * 2 + c + 1)
                nc.scalar.activation(o_raw[:, bass.ds(turn, 1), c * CHUNK:(c + 1) * CHUNK],
                                     o_ps[:, :].rearrange("p (o n) -> p o n", o=1), ACT.Copy).then_inc(o_kept, 1)

            act.sem_inc(o_kept, O_KEPT0)
            for g in range(AHEAD):
                exps(g, 0)
            with act.Fori(0, TURNS, 1) as turn:
                for g in range(NG):
                    if g + AHEAD < NG:
                        exps(g + AHEAD, turn)
                    else:
                        exps(g + AHEAD - NG, turn + 1)
                    if GROUPS[g] == (3, 0):
                        keep(0, turn)
                keep(1, turn)

        @block.vector
        def _(dve):
            def maxima(par, turn, units):
                for u in units:
                    qb, c, h = UNITS[u]
                    bank = (u + 1) % 3
                    dve.wait_ge(s_ready, turn * (NU + 1) + u + 1)
                    if qb // 4 == c:
                        dve.sem_inc(waited, 1)
                    n = CHUNK if qb // 4 > c else (qb % 4 + 1) * P
                    acc = top[:, par, h, qb:qb + 1] if c == 0 else top2[:, par, h, qb - 4:qb - 3]
                    if qb // 4 > c:
                        nc.vector.reduce_max(acc, s_ps[:, bank, 0:n], AX.X).then_inc(max_done, 1)
                    else:
                        nc.vector.tensor_tensor_reduce(out=unused[:, bank, 0:n], in0=s_ps[:, bank, 0:n],
                                                       in1=mask[:, CHUNK - n:], scale=1.0, scalar=BIG, op0=ALU.add,
                                                       op1=ALU.max, accum_out=acc).then_inc(max_done, 1)

            def negate(par, turn, before):
                dve.wait_ge(max_done, turn * (NU + 1) + NU)
                nc.vector.tensor_tensor(top[:, par, :, NB // 2:], top[:, par, :, NB // 2:], top2[:, par, :, :],
                                        ALU.max).then_inc(combined, 1)
                dve.wait_ge(s_ready, turn * (NU + 1) + NU + 1)
                if before is not None:
                    dve.wait_ge(*before)
                nc.vector.tensor_scalar(top_t[:, :], s_ps[0:4 * NB, 0, 0:P], -1.0, None,
                                        ALU.mult).then_inc(max_done, 1)

            for i in range(2):
                nc.vector.memset(q_stack[i][:, :, :].bitcast(F32), 0.0).then_inc(set_up[i], 1)
                nc.vector.memset(k_stack[i][96:97, :, :].bitcast(F32), 1.0).then_inc(set_up[i], 1)
            dve.wait_ge(mask_set, 2)
            maxima(0, 0, range(NU))
            negate(0, 0, None)
            maxima(1, 1, range(PER * EARLY))
            with dve.Fori(0, TURNS // SLOTS, 1) as lap:
                for par in range(SLOTS):
                    turn = lap * SLOTS + par
                    maxima((par + 1) % 2, turn + 1, range(PER * EARLY, NU))
                    negate((par + 1) % 2, turn + 1, (top_in[par], lap * 16 + 16))
                    maxima(par % 2, turn + 2, range(PER * EARLY))


EXPERTS = 8


class ExpertWeights:

    def __init__(self, nc, ctx, ew1, ew2, ew3):
        self.nc = nc
        self.sources = (ew1, ew3, ew2)
        self.raw = ctx.enter_context(nc.sbuf_tensor("moe_raw", [P, 3, KT, D], F32))
        self.high = [ctx.enter_context(nc.sbuf_tensor(f"moe_w_high{i}", [P, 3, KT, D], F32R)) for i in range(2)]
        self.low = [ctx.enter_context(nc.sbuf_tensor(f"moe_w_low{i}", [P, 3, KT, D], F32R)) for i in range(2)]
        self.raw_in, self.rounded, self.ready = (
            ctx.enter_context(nc.semaphore("moe_" + n)) for n in ("raw_in", "w_rounded", "w_ready"))

    def load(self, sp, e):
        for i, w in enumerate(self.sources):
            src = w[e] if isinstance(e, int) else w[bass.ds(e, 1)].rearrange("o d n -> (o d) n")
            sp.dma_start(self.raw[:, i, :, :], src.rearrange("(k p) n -> p k n", p=P)).then_inc(self.raw_in, 16)

    def split(self, pool, slot, e, waited):
        pool.wait_ge(self.raw_in, e * 48 + 48)
        pool.sem_inc(waited, 1)
        high, low = self.high[slot], self.low[slot]
        self.nc.gpsimd.tensor_copy(high[:, :, :, :], self.raw[:, :, :, :]).then_inc(self.rounded, 1)
        pool.wait_ge(self.rounded, e + 1)
        self.nc.gpsimd.tensor_tensor(low[:, :, :, :], self.raw[:, :, :, :], high[:, :, :, :].bitcast(F32),
                                     ALU.subtract).then_inc(self.ready, 1)


def stage_router(nc, zh, zl, raw, w_in, weights, ident, before, ntok):
    T = ntok // P
    CH = ntok // CHUNK
    E = EXPERTS
    with ExitStack() as ctx:
        def sb(n, shape, dt=F32):
            return ctx.enter_context(nc.sbuf_tensor("router_" + n, shape, dt))

        def sem(n):
            return ctx.enter_context(nc.semaphore("router_" + n))

        w_high = sb("w_high", [P, KT, E], F32R)
        w_low = sb("w_low", [P, KT, E], F32R)
        logits_t = sb("logits_t", [E, ntok])
        top = sb("top", [P, T, 1])
        less = sb("less", [P, T, E])
        expo = sb("expo", [P, T, E])
        total = sb("total", [P, T, 1])
        share = sb("share", [P, T, 1])
        prob = sb("prob", [P, T, E])
        rank = sb("rank", [P, T, E])
        beats = sb("beats", [P, T, E])
        ps = ctx.enter_context(nc.psum_tensor("router_ps", [P, 2, CHUNK], F32))
        lg = ctx.enter_context(nc.psum_tensor("router_lg", [P, T, E], F32))
        logits_ready, kept = sem("logits_ready"), sem("kept")
        turned, step, less_ready, expo_ready = sem("turned"), sem("step"), sem("less_ready"), sem("expo_ready")
        block = ctx.enter_context(nc.Block())

        @block.sync
        def _(sp):
            sp.wait_ge(*before)

        @block.tensor
        def _(pe):
            pe.wait_ge(step, 2)
            for c in range(CH):
                if c >= 2:
                    pe.wait_ge(kept, c - 1)
                n = 0
                for k in range(KT):
                    for w, z in ((w_high, zh), (w_high, zl), (w_low, zh)):
                        last = nc.tensor.matmul(ps[0:E, c % 2, :], w[:, k, :], z[:, k, c * CHUNK:(c + 1) * CHUNK],
                                                start=(n == 0), stop=(n == 5))
                        n += 1
                last.then_inc(logits_ready, 1)
            pe.wait_ge(kept, CH)
            for t in range(T):
                last = nc.tensor.transpose(lg[:, t, :], logits_t[:, t * P:(t + 1) * P], ident[0:E, 0:E])
            last.then_inc(turned, 1)

        @block.scalar
        def _(act):
            for c in range(CH):
                act.wait_ge(logits_ready, c + 1)
                nc.scalar.activation(logits_t[:, c * CHUNK:(c + 1) * CHUNK], ps[0:E, c % 2, :],
                                     ACT.Copy).then_inc(kept, 1)
            act.wait_ge(less_ready, 1)
            nc.scalar.activation(expo[:, :, :], less[:, :, :], ACT.Exp).then_inc(expo_ready, 1)

        @block.vector
        def _(dve):
            count = [0]

            def link(ins):
                count[0] += 1
                ins.then_inc(step, 1)
                dve.wait_ge(step, count[0])

            def wide(ap):
                return ap.broadcast_to([P, T, E])

            dve.wait_ge(w_in, 16)
            link(nc.vector.tensor_copy(w_high[:, :, :], raw[:, :, :]))
            link(nc.vector.tensor_tensor(w_low[:, :, :], raw[:, :, :], w_high[:, :, :].bitcast(F32), ALU.subtract))
            dve.wait_ge(turned, 1)
            link(nc.vector.tensor_reduce(top[:, :, :].rearrange("p t o -> p (t o)"), lg[:, :, :], AX.X, ALU.max))
            nc.vector.tensor_tensor(less[:, :, :], lg[:, :, :], wide(top[:, :, :]), ALU.subtract).then_inc(less_ready, 1)
            link(nc.vector.memset(rank[:, :, :], 0.0))
            dve.wait_ge(expo_ready, 1)
            link(nc.vector.tensor_reduce(total[:, :, :].rearrange("p t o -> p (t o)"), expo[:, :, :], AX.X, ALU.add))
            link(nc.vector.reciprocal(share[:, :, :], total[:, :, :]))
            link(nc.vector.tensor_tensor(prob[:, :, :], expo[:, :, :], wide(share[:, :, :]), ALU.mult))
            for j in range(E):
                if j + 1 < E:
                    link(nc.vector.tensor_tensor(beats[:, :, j + 1:], prob[:, :, j:j + 1].broadcast_to([P, T, E - j - 1]),
                                                 prob[:, :, j + 1:], ALU.is_ge))
                link(nc.vector.tensor_tensor(beats[:, :, 0:j + 1], prob[:, :, j:j + 1].broadcast_to([P, T, j + 1]),
                                             prob[:, :, 0:j + 1], ALU.is_gt))
                link(nc.vector.tensor_tensor(rank[:, :, :], rank[:, :, :], beats[:, :, :], ALU.add))
            link(nc.vector.tensor_scalar(beats[:, :, :], rank[:, :, :], 2.0, None, ALU.is_lt))
            link(nc.vector.tensor_tensor(weights[:, :, :], prob[:, :, :], beats[:, :, :], ALU.mult))


def stage_experts(nc, zh, zl, ew, weights, norm_w, x1, out, waited, ntok):
    TURN_CHUNKS = 2
    CH = ntok // CHUNK
    INNER = CH // TURN_CHUNKS
    TILES = CHUNK // P
    ROWS = TURN_CHUNKS * TILES
    LAST = (EXPERTS - 1) * INNER
    with ExitStack() as ctx:
        def sb(n, shape, dt=F32):
            return ctx.enter_context(nc.sbuf_tensor("moe_" + n, shape, dt))

        def sem(n):
            return ctx.enter_context(nc.semaphore("moe_" + n))

        w_high, w_low = ew.high, ew.low
        silu = sb("silu", [P, 2, CHUNK])
        gate = sb("gate", [P, 2, CHUNK])
        g_high = sb("g_high", [P, 4, CHUNK], F32R)
        g_low = sb("g_low", [P, 4, CHUNK], F32R)
        moe = sb("sum", [P, ntok // P, D])
        w_row = sb("w_row", [P, D])
        x1_in = sb("x1_in", [P, ROWS, D])
        res = sb("res", [P, ROWS, D])
        squares = sb("squares", [P, ROWS, D])
        sums = sb("sums", [P, ROWS])
        ms = sb("ms", [P, ROWS])
        rms = sb("rms", [P, ROWS])
        inv = sb("inv", [P, ROWS])
        up = ctx.enter_context(nc.psum_tensor("moe_up", [P, 2, 2, CHUNK], F32))
        down = ctx.enter_context(nc.psum_tensor("moe_down", [P, 2, TILES, D], F32))
        up_ready, silu_done, gate_done = sem("up_ready"), sem("silu_done"), sem("gate_done")
        high_done, low_done, down_ready, added = sem("high_done"), sem("low_done"), sem("down_ready"), sem("added")
        cleared = sem("cleared")
        row_in, rows_in, summed, ms_done, rms_done = (
            sem("row_in"), sem("rows_in"), sem("summed"), sem("ms_done"), sem("rms_done"))
        inv_done, scaled, finished, stored = (
            sem("inv_done"), sem("scaled"), sem("finished"), sem("stored"))
        block = ctx.enter_context(nc.Block())

        @block.sync
        def _(sp):
            sp.sem_inc(stored, 16)
            with sp.Fori(1, EXPERTS - 1, 1) as e:
                sp.wait_ge(ew.ready, e + 1)
                ew.load(sp, e + 1)

            def rows(d, q):
                return d.rearrange("(t p) d -> p t d", p=P)[:, bass.ds(q * ROWS, ROWS), :]

            sp.dma_start(w_row[:, :], norm_w.rearrange("(o d) -> o d", o=1).broadcast_to([P, D])).then_inc(row_in, 16)
            sp.dma_start(x1_in[:, :, :], rows(x1, 0)).then_inc(rows_in, 16)
            with sp.Fori(0, INNER - 1, 1) as q:
                sp.wait_ge(finished, (q + 1) * ROWS)
                sp.sem_inc(waited, 1)
                sp.dma_start(rows(out, q), res[:, :, :]).then_inc(stored, 16)
                sp.dma_start(x1_in[:, :, :], rows(x1, q + 1)).then_inc(rows_in, 16)
                sp.wait_ge(stored, 16 + q * 16 + 16)
                sp.sem_inc(waited, 1)
            for i in range(TURN_CHUNKS):
                sp.wait_ge(finished, (INNER - 1) * ROWS + (i + 1) * TILES)
                part = slice(i * TILES, (i + 1) * TILES)
                sp.dma_start(rows(out, INNER - 1)[:, part, :], res[:, part, :]).then_inc(stored, 16)
            sp.wait_ge(stored, 16 * (INNER + TURN_CHUNKS))

        @block.gpsimd
        def _(pool):
            with pool.Fori(0, EXPERTS // 2 - 1, 1) as half:
                for par in range(2):
                    pool.wait_ge(down_ready, (half * 2 + par + 1) * (2 * INNER))
                    ew.split(pool, par, half * 2 + par + 2, waited)

        @block.tensor
        def _(pe):
            with pe.Fori(0, EXPERTS // 2, 1) as half:
                for par in range(2):
                    pe.wait_ge(ew.ready, half * 2 + par + 1)
                    pe.sem_inc(waited, 1)
                    with pe.Fori(0, INNER, 1) as inner:
                        turn = (half * 2 + par) * INNER + inner
                        for j in range(4):
                            c, f = j // 2, j % 2
                            if j >= 2:
                                pe.wait_ge(gate_done, turn * 4 + j - 1)
                            for which in range(2):
                                n = 0
                                for k in range(KT):
                                    for w, z in ((w_high, zh), (w_high, zl), (w_low, zh)):
                                        last = nc.tensor.matmul(
                                            up[:, j % 2, which, :], w[par][:, which, k, f * P:(f + 1) * P],
                                            z[:, k, bass.ds(inner * (2 * CHUNK) + c * CHUNK, CHUNK)],
                                            start=(n == 0), stop=(n == 5))
                                        n += 1
                            last.then_inc(up_ready, 1)
                        for c in range(2):
                            pe.wait_ge(low_done, 1 + turn * 4 + 2 * c + 2)
                            if c == 0:
                                pe.wait_ge(added, 1 + turn * 8)
                            for i in range(TILES):
                                n = 0
                                for f in range(2):
                                    for g, w in ((g_high, w_high), (g_high, w_low), (g_low, w_high)):
                                        last = nc.tensor.matmul(down[:, c, i, :], g[:, 2 * c + f, i * P:(i + 1) * P],
                                                                w[par][:, 2, f, :], start=(n == 0), stop=(n == 5))
                                        n += 1
                            last.then_inc(down_ready, 1)

        @block.scalar
        def _(act):
            def high(j, turn):
                act.wait_ge(gate_done, turn * 4 + j + 1)
                nc.scalar.activation(g_high[:, j, :], gate[:, j % 2, :], ACT.Copy).then_inc(high_done, 1)

            def square_sums(turn):
                for i in range(ROWS):
                    act.wait_ge(added, 1 + turn * ROWS - ROWS + i + 1)
                    nc.scalar.activation(squares[:, i, :].rearrange("p (o d) -> p o d", o=1),
                                         moe[:, bass.ds((turn - 1) % INNER * ROWS + i, 1), :], ACT.Square,
                                         accum_out=sums[:, i:i + 1]).then_inc(summed, 1)

            def root(turn):
                act.wait_ge(ms_done, turn - LAST)
                nc.scalar.activation(rms[:, :], ms[:, :], ACT.Sqrt).then_inc(rms_done, 1)

            def activate(turn, norm):
                for j in range(4):
                    act.wait_ge(up_ready, turn * 4 + j + 1)
                    nc.scalar.activation(silu[:, j % 2, :], up[:, j % 2, 0, :], ACT.Silu).then_inc(silu_done, 1)
                    if j >= 1:
                        high(j - 1, turn)
                    if norm and j == 1:
                        square_sums(turn)
                high(3, turn)
                if norm:
                    root(turn)

            with act.Fori(0, LAST + 1, 1) as turn:
                activate(turn, False)
            with act.Fori(LAST + 1, LAST + INNER, 1) as turn:
                activate(turn, True)
            square_sums(LAST + INNER)
            root(LAST + INNER)

        @block.vector
        def _(dve):
            def low(j, turn):
                dve.wait_ge(high_done, turn * 4 + j + 1)
                nc.vector.tensor_tensor(g_low[:, j, :], gate[:, j % 2, :], g_high[:, j, :].bitcast(F32),
                                        ALU.subtract).then_inc(low_done, 1)

            def gated(turn):
                for j in range(4):
                    dve.wait_ge(low_done, 1 + turn * 4 + max(j - 1, 0))
                    dve.wait_ge(silu_done, turn * 4 + j + 1)
                    nc.vector.tensor_tensor(gate[:, j % 2, :], up[:, j % 2, 1, :], silu[:, j % 2, :],
                                            ALU.mult).then_inc(gate_done, 1)
                    if j >= 1:
                        low(j - 1, turn)
                low(3, turn)

            def add(turn):
                dve.wait_ge(added, 1 + turn * ROWS)
                for c in range(2):
                    dve.wait_ge(down_ready, turn * 2 + c + 1)
                    for i in range(TILES):
                        tile = turn % INNER * ROWS + c * TILES + i
                        part = moe[:, bass.ds(tile, 1), :].rearrange("p o d -> p (o d)")
                        by = weights[:, bass.ds(tile, 1), bass.ds(turn // INNER, 1)].rearrange("p o e -> p (o e)")
                        nc.vector.scalar_tensor_tensor(part, down[:, c, i, :], by, part, ALU.mult,
                                                       ALU.add).then_inc(added, 1)

            def mean_squares(turn):
                dve.wait_ge(summed, (turn - LAST) * ROWS)
                nc.vector.tensor_scalar(ms[:, :], sums[:, :], 1.0 / D, EPS, ALU.mult, ALU.add).then_inc(ms_done, 1)

            def invert(turn):
                dve.wait_ge(rms_done, turn - LAST)
                nc.vector.reciprocal(inv[:, :], rms[:, :]).then_inc(inv_done, 1)

            def finish(turn):
                q = turn - LAST
                dve.wait_ge(rows_in, q * 16)
                dve.wait_ge(stored, 16 + q * 16 - 16)
                dve.wait_ge(inv_done, q)
                for i in range(ROWS):
                    tile = (turn - 1) % INNER * ROWS + i
                    nc.vector.scalar_tensor_tensor(res[:, i, :].rearrange("p (o d) -> p o d", o=1),
                                                   moe[:, bass.ds(tile, 1), :], inv[:, i:i + 1],
                                                   w_row[:, :].rearrange("p (o d) -> p o d", o=1),
                                                   ALU.mult, ALU.mult).then_inc(scaled, 1)
                for i in range(ROWS):
                    dve.wait_ge(scaled, (q - 1) * ROWS + i + 1)
                    nc.vector.tensor_tensor(res[:, i, :], res[:, i, :], x1_in[:, i, :], ALU.add).then_inc(finished, 1)

            for counted in (low_done, added):
                dve.sem_inc(counted, 1)
            nc.vector.memset(moe[:, :, :], 0.0).then_inc(cleared, 1)
            dve.wait_ge(cleared, 1)
            with dve.Fori(0, LAST + 1, 1) as turn:
                gated(turn)
                add(turn)
            dve.wait_ge(row_in, 16)
            with dve.Fori(LAST + 1, LAST + INNER, 1) as turn:
                gated(turn)
                mean_squares(turn)
                add(turn)
                invert(turn)
                finish(turn)
            mean_squares(LAST + INNER)
            invert(LAST + INNER)
            finish(LAST + INNER)


def stage_attention_out(nc, o_raw, z_rows, wo, norm_w, hh, hl, h_out, fw, ident, batches, seq):
    ntok = batches * seq
    T = ntok // P
    HQ = HEADS // 4
    with ExitStack() as ctx:
        def sb(n, shape, dt=F32):
            return ctx.enter_context(nc.sbuf_tensor("ao_" + n, shape, dt))

        def sem(n):
            return ctx.enter_context(nc.semaphore("ao_" + n))

        raw = sb("raw", [P, KT, D])
        w_high = sb("w_high", [P, KT, D], F32R)
        w_low = sb("w_low", [P, KT, D], F32R)
        w_row = sb("w_row", [P, D])
        share = sb("share", [P, 2, HEADS, 1])
        o_rows = sb("o_rows", [P, 2, D])
        o_high = sb("o_high", [P, 2, KT, P], F32R)
        o_low = sb("o_low", [P, 2, KT, P], F32R)
        squares = sb("squares", [P, 2, D])
        sums = sb("sums", [P, 4, 1])
        ms = sb("ms", [P, 4, 1])
        rms = sb("rms", [P, 4, 1])
        inv = sb("inv", [P, 4, 1])
        scaled = sb("scaled", [P, 2, D])
        h = sb("h", [P, 4, D])
        t1 = ctx.enter_context(nc.psum_tensor("ao_t1", [P, 2, CHUNK], F32))
        t2 = ctx.enter_context(nc.psum_tensor("ao_t2", [P, 1, CHUNK], F32))
        prod = ctx.enter_context(nc.psum_tensor("ao_prod", [P, 3, CHUNK], F32))
        t3 = ctx.enter_context(nc.psum_tensor("ao_t3", [P, 2, CHUNK], F32))
        w_in, w_rounded, w_split = sem("w_in"), sem("w_rounded"), sem("w_split")
        t1_ready, share_done, rows_done, t2_ready = sem("t1_ready"), sem("share_done"), sem("rows_done"), sem("t2_ready")
        o_high_done, o_low_done, prod_ready = sem("o_high_done"), sem("o_low_done"), sem("prod_ready")
        sums_done, ms_done, rms_done, inv_done = sem("sums_done"), sem("ms_done"), sem("rms_done"), sem("inv_done")
        scaled_done, h_done, t3_ready = sem("scaled_done"), sem("h_done"), sem("t3_ready")
        h_high_done, h_low_done = sem("h_high_done"), sem("h_low_done")
        stored = [sem(f"stored{i}") for i in range(4)]
        z_in = [sem(f"z_in{i}") for i in range(2)]
        z = sb("z", [P, 2, 4, D])
        block = ctx.enter_context(nc.Block())

        @block.sync
        def _(sp):
            def load_z(c):
                sp.dma_start(z[:, c % 2, :, :], z_rows.rearrange("(t p) d -> p t d", p=P)[:, 4 * c:4 * c + 4, :]
                             ).then_inc(z_in[c % 2], 16)

            sp.dma_start(raw[:, :, :], wo.rearrange("(k p) n -> p k n", p=P)).then_inc(w_in, 16)
            sp.dma_start(w_row[:, :], norm_w.rearrange("(o d) -> o d", o=1).broadcast_to([P, D])).then_inc(w_in, 16)
            load_z(0)
            load_z(1)
            fw.load(sp)
            for t in range(T):
                sp.wait_ge(h_done, t + 1)
                if t % 4 == 3 and t + 4 < T - 1:
                    load_z(t // 4 + 2)
                sp.dma_start(h_out[t * P:(t + 1) * P, :], h[:, t % 4, :]).then_inc(stored[t % 4], 16)
            for i in range(4):
                sp.wait_ge(stored[i], 16 * (T // 4))

        @block.tensor
        def _(pe):
            def turn_heads(t):
                if t >= 2:
                    pe.wait_ge(rows_done, t - 1)
                at = t * P % seq
                for hq in range(HQ):
                    last = nc.tensor.transpose(t1[:, t % 2, hq * P:(hq + 1) * P],
                                               o_raw[:, t * P // seq * HQ + hq, at:at + P], ident[:, :])
                last.then_inc(t1_ready, 1)

            def turn_rows(t):
                pe.wait_ge(rows_done, t + 1)
                if t >= 1:
                    pe.wait_ge(o_low_done, t)
                for k in range(KT):
                    last = nc.tensor.transpose(t2[:, 0, k * P:(k + 1) * P], o_rows[:, t % 2, k * P:(k + 1) * P],
                                               ident[:, :])
                last.then_inc(t2_ready, 1)

            def product(t):
                pe.wait_ge(o_low_done, t + 1)
                if t >= 3:
                    pe.wait_ge(scaled_done, t - 2)
                n = 0
                for k in range(KT):
                    for o, w in ((o_high, w_high), (o_high, w_low), (o_low, w_high)):
                        last = nc.tensor.matmul(prod[:, t % 3, 0:D], o[:, t % 2, k, :], w[:, k, :],
                                                start=(n == 0), stop=(n == 5))
                        n += 1
                last.then_inc(prod_ready, 1)

            def turn_h(t):
                pe.wait_ge(h_done, t + 1)
                if t >= 2:
                    pe.wait_ge(h_low_done, t - 1)
                for k in range(KT):
                    last = nc.tensor.transpose(t3[:, t % 2, k * P:(k + 1) * P], h[:, t % 4, k * P:(k + 1) * P],
                                               ident[:, :])
                last.then_inc(t3_ready, 1)

            pe.wait_ge(w_split, 1)
            for t in range(T + 5):
                if t < T:
                    turn_heads(t)
                if 0 <= t - 1 < T:
                    turn_rows(t - 1)
                if 0 <= t - 2 < T:
                    product(t - 2)
                if 0 <= t - 4 < T:
                    turn_h(t - 4)

        @block.scalar
        def _(act):
            act.wait_ge(w_in, 32)
            nc.scalar.activation(w_high[:, :, :], raw[:, :, :], ACT.Copy).then_inc(w_rounded, 1)
            for t in range(T + 5):
                if 0 <= t - 1 < T:
                    u = t - 1
                    act.wait_ge(t2_ready, u + 1)
                    if u >= 2:
                        act.wait_ge(prod_ready, u - 1)
                    nc.scalar.activation(o_high[:, u % 2, :, :], t2[:, 0, 0:D].rearrange("p (k c) -> p k c", k=KT),
                                         ACT.Copy).then_inc(o_high_done, 1)
                if 0 <= t - 2 < T:
                    u = t - 2
                    act.wait_ge(prod_ready, u + 1)
                    if u >= 2:
                        act.wait_ge(sums_done, u - 1)
                    nc.scalar.activation(squares[:, u % 2, :], prod[:, u % 3, 0:D], ACT.Square,
                                         accum_out=sums[:, u % 4, :]).then_inc(sums_done, 1)
                if 0 <= t - 3 < T:
                    u = t - 3
                    act.wait_ge(ms_done, u + 1)
                    nc.scalar.activation(rms[:, u % 4, :], ms[:, u % 4, :], ACT.Sqrt).then_inc(rms_done, 1)
                if 0 <= t - 4 < T:
                    u = t - 4
                    act.wait_ge(t3_ready, u + 1)
                    nc.scalar.activation(hh[:, :, u * P:(u + 1) * P],
                                         t3[:, u % 2, 0:D].rearrange("p (k c) -> p k c", k=KT),
                                         ACT.Copy).then_inc(h_high_done, 1)

        @block.gpsimd
        def _(pool):
            for u in range(T):
                pool.wait_ge(scaled_done, u + 1)
                if u >= 4:
                    pool.wait_ge(stored[u % 4], 16 * (u // 4))
                    pool.wait_ge(t3_ready, u - 3)
                if u % 4 == 0:
                    pool.wait_ge(z_in[u // 4 % 2], 16 * (u // 8 + 1))
                if u >= 1:
                    pool.wait_ge(h_done, u)
                nc.gpsimd.tensor_tensor(h[:, u % 4, :], scaled[:, u % 2, :], z[:, u // 4 % 2, u % 4, :],
                                        ALU.add).then_inc(h_done, 1)

        @block.vector
        def _(dve):
            dve.wait_ge(w_rounded, 1)
            nc.vector.tensor_tensor(w_low[:, :, :], raw[:, :, :], w_high[:, :, :].bitcast(F32),
                                    ALU.subtract).then_inc(w_split, 1)
            for t in range(T + 5):
                if t < T:
                    dve.wait_ge(t1_ready, t + 1)
                    heads = t1[:, t % 2, :].rearrange("p (h e) -> p h e", e=2 * HD)
                    nc.vector.reciprocal(share[:, t % 2, :, :], heads[:, :, HD:HD + 1]).then_inc(share_done, 1)
                    dve.wait_ge(share_done, t + 1)
                    if t >= 2:
                        dve.wait_ge(t2_ready, t - 1)
                    nc.vector.tensor_tensor(o_rows[:, t % 2, :].rearrange("p (h e) -> p h e", e=HD), heads[:, :, 0:HD],
                                            share[:, t % 2, :, :].broadcast_to([P, HEADS, HD]),
                                            ALU.mult).then_inc(rows_done, 1)
                if 0 <= t - 1 < T:
                    u = t - 1
                    dve.wait_ge(o_high_done, u + 1)
                    nc.vector.tensor_tensor(o_low[:, u % 2, :, :], t2[:, 0, 0:D].rearrange("p (k c) -> p k c", k=KT),
                                            o_high[:, u % 2, :, :].bitcast(F32), ALU.subtract).then_inc(o_low_done, 1)
                if 0 <= t - 2 < T:
                    u = t - 2
                    dve.wait_ge(sums_done, u + 1)
                    nc.vector.tensor_scalar(ms[:, u % 4, :], sums[:, u % 4, :], 1.0 / D, EPS, ALU.mult,
                                            ALU.add).then_inc(ms_done, 1)
                if 0 <= t - 3 < T:
                    u = t - 3
                    dve.wait_ge(rms_done, u + 1)
                    nc.vector.reciprocal(inv[:, u % 4, :], rms[:, u % 4, :]).then_inc(inv_done, 1)
                    dve.wait_ge(inv_done, u + 1)
                    if u >= 2:
                        dve.wait_ge(h_done, u - 1)
                    nc.vector.scalar_tensor_tensor(scaled[:, u % 2, :], prod[:, u % 3, 0:D], inv[:, u % 4, :],
                                                   w_row[:, :], ALU.mult, ALU.mult).then_inc(scaled_done, 1)
                if 0 <= t - 4 < T:
                    u = t - 4
                    dve.wait_ge(h_high_done, u + 1)
                    nc.vector.tensor_tensor(hl[:, :, u * P:(u + 1) * P],
                                            t3[:, u % 2, 0:D].rearrange("p (k c) -> p k c", k=KT),
                                            hh[:, :, u * P:(u + 1) * P].bitcast(F32), ALU.subtract).then_inc(h_low_done, 1)


class FfnWeights:

    def __init__(self, nc, ctx, w1, w2, w3):
        self.sources = (w1, w3, w2)
        self.tiles = w1.shape[1] // P
        self.raw = ctx.enter_context(nc.sbuf_tensor("ffn_raw", [P, 3, KT * self.tiles * P], F32, side="right"))
        self.loaded = [ctx.enter_context(nc.semaphore(f"ffn_w_in{i}")) for i in range(3)]

    def load(self, sp):
        for i, w in enumerate(self.sources):
            sp.dma_start(self.raw[:, i, :].rearrange("p (k n) -> p k n", n=w.shape[1]),
                         w.rearrange("(k p) n -> p k n", p=P)).then_inc(self.loaded[i], 16)


def stage_ffn(nc, hh, hl, fw, norm_w, extras, out, waited, ntok):
    CH = ntok // CHUNK
    FT = fw.tiles
    TILES = CHUNK // P
    AHEAD = 2
    with ExitStack() as ctx:
        def sb(n, shape, dt=F32):
            return ctx.enter_context(nc.sbuf_tensor("ffn_" + n, shape, dt))

        def sem(n):
            return ctx.enter_context(nc.semaphore("ffn_" + n))

        SIZE = KT * FT * P
        raw, w_in = fw.raw, fw.loaded
        w_high = sb("w_high", [P, 3, SIZE], F32R)
        w_low = sb("w_low", [P, 3, SIZE], F32R)
        silu = sb("silu", [P, 2, CHUNK])
        gate = sb("gate", [P, 2, CHUNK])
        g_high = sb("g_high", [P, 4, CHUNK], F32R)
        g_low = sb("g_low", [P, 4, CHUNK], F32R)
        w_row = sb("w_row", [P, D])
        extra_in = sb("extra_in", [P, len(extras), TILES, D])
        kept = sb("kept", [P, TILES, D])
        squares = sb("squares", [P, TILES, D])
        sums = sb("sums", [P, TILES])
        ms = sb("ms", [P, TILES])
        rms = sb("rms", [P, TILES])
        inv = sb("inv", [P, TILES])
        res = sb("res", [P, TILES, D])
        up = ctx.enter_context(nc.psum_tensor("ffn_up", [P, 2, 2, CHUNK], F32))
        down = ctx.enter_context(nc.psum_tensor("ffn_down", [P, TILES, CHUNK], F32))
        w_rounded, w_ready, row_in = sem("w_rounded"), sem("w_ready"), sem("row_in")
        up_ready, silu_done, gate_done = sem("up_ready"), sem("silu_done"), sem("gate_done")
        high_done, low_done, down_ready, down_kept = (
            sem("high_done"), sem("low_done"), sem("down_ready"), sem("down_kept"))
        extras_in, summed, ms_done, rms_done, inv_done = (
            sem("extras_in"), sem("summed"), sem("ms_done"), sem("rms_done"), sem("inv_done"))
        adding, finished, stored = sem("adding"), sem("finished"), sem("stored")
        block = ctx.enter_context(nc.Block())
        out_t = out.rearrange("(t p) d -> p t d", p=P)

        @block.sync
        def _(sp):
            def load_extras(c):
                for i, x in enumerate(extras):
                    sp.dma_start(extra_in[:, i, :, :],
                                 x.rearrange("(t p) d -> p t d", p=P)[:, bass.ds(c * TILES, TILES), :]
                                 ).then_inc(extras_in, 16)

            sp.dma_start(w_row[:, :], norm_w.rearrange("(o d) -> o d", o=1).broadcast_to([P, D])).then_inc(row_in, 16)
            load_extras(0)
            with sp.Fori(0, CH - 1, 1) as c:
                sp.wait_ge(finished, (c + 1) * TILES)
                sp.sem_inc(waited, 1)
                sp.dma_start(out_t[:, bass.ds(c * TILES, TILES), :], res[:, :, :]).then_inc(stored, 16)
                load_extras(c + 1)
                sp.wait_ge(stored, c * 16 + 16)
                sp.sem_inc(waited, 1)
            for i in range(TILES):
                sp.wait_ge(finished, (CH - 1) * TILES + i + 1)
                sp.dma_start(out_t[:, (CH - 1) * TILES + i, :], res[:, i, :]).then_inc(stored, 16)
            sp.wait_ge(stored, 16 * (CH - 1 + TILES))

        @block.tensor
        def _(pe):
            def up_job(c, f):
                if f >= FT:
                    c, f = c + 1, f - FT
                n = c * FT + f
                if not (isinstance(c, int) and n < 2):
                    pe.wait_ge(gate_done, n - 1)
                for which in range(2):
                    m = 0
                    for k in range(KT):
                        at = k * FT * P + f * P
                        for w, z in ((w_high, hh), (w_high, hl), (w_low, hh)):
                            last = nc.tensor.matmul(up[:, f % 2, which, :], w[:, which, at:at + P],
                                                    z[:, k, bass.ds(c % CH * CHUNK, CHUNK)],
                                                    start=(m == 0), stop=(m == 5))
                            m += 1
                last.then_inc(up_ready, 1)

            def down_job(c, f):
                pe.wait_ge(low_done, c * FT + f + 1)
                if f == 0 and not isinstance(c, int):
                    pe.wait_ge(down_kept, c)
                for i in range(TILES):
                    for n, (g, w) in enumerate(((g_high, w_high), (g_high, w_low), (g_low, w_high))):
                        last = nc.tensor.matmul(down[:, i, 0:D], g[:, f % 4, i * P:(i + 1) * P],
                                                w[:, 2, f * D:(f + 1) * D], start=(f == 0 and n == 0),
                                                stop=(f == FT - 1 and n == 2))
                if f == FT - 1:
                    last.then_inc(down_ready, 1)

            def chunk(c):
                for f in range(FT):
                    up_job(c, f + AHEAD)
                    down_job(c, f)

            pe.wait_ge(w_ready, 2)
            for f in range(AHEAD):
                up_job(0, f)
            pe.wait_ge(w_ready, 3)
            chunk(0)
            with pe.Fori(1, CH, 1) as c:
                chunk(c)

        @block.scalar
        def _(act):
            def activate(c, f):
                n = c * FT + f
                act.wait_ge(up_ready, n + 1)
                nc.scalar.activation(silu[:, f % 2, :], up[:, f % 2, 0, :], ACT.Silu).then_inc(silu_done, 1)

            def high(c, f):
                n = c * FT + f
                act.wait_ge(gate_done, n + 1)
                nc.scalar.activation(g_high[:, f % 4, :], gate[:, f % 2, :], ACT.Copy).then_inc(high_done, 1)

            def square_sums(c):
                act.wait_ge(down_kept, c)
                for i in range(TILES):
                    nc.scalar.activation(squares[:, i, :], kept[:, i, :], ACT.Square,
                                         accum_out=sums[:, i:i + 1]).then_inc(summed, 1)

            def root(c):
                act.wait_ge(ms_done, c)
                nc.scalar.activation(rms[:, :], ms[:, :], ACT.Sqrt).then_inc(rms_done, 1)

            def chunk(c):
                for f in range(FT):
                    activate(c, f + AHEAD)
                    high(c, f + AHEAD - 1)
                    if not isinstance(c, int):
                        if f == 0:
                            square_sums(c)
                        if f == 2:
                            root(c)

            for i in range(3):
                act.wait_ge(w_in[i], 16)
                nc.scalar.activation(w_high[:, i, :], raw[:, i, :], ACT.Copy).then_inc(w_rounded, 1)
            for f in range(AHEAD):
                activate(0, f)
                if f >= 1:
                    high(0, f - 1)
            chunk(0)
            with act.Fori(1, CH, 1) as c:
                chunk(c)
            square_sums(CH)
            root(CH)

        @block.vector
        def _(dve):
            def gated(c, f):
                n = c * FT + f
                if not (isinstance(c, int) and n < 2):
                    dve.wait_ge(low_done, n - 1)
                dve.wait_ge(silu_done, n + 1)
                nc.vector.tensor_tensor(gate[:, f % 2, :], up[:, f % 2, 1, :], silu[:, f % 2, :],
                                        ALU.mult).then_inc(gate_done, 1)

            def low(c, f):
                dve.wait_ge(high_done, c * FT + f + 1)
                nc.vector.tensor_tensor(g_low[:, f % 4, :], gate[:, f % 2, :], g_high[:, f % 4, :].bitcast(F32),
                                        ALU.subtract).then_inc(low_done, 1)

            def keep(c):
                dve.wait_ge(down_ready, c)
                nc.vector.tensor_copy(kept[:, :, :], down[:, :, 0:D]).then_inc(down_kept, 1)

            def mean_squares(c):
                dve.wait_ge(summed, c * TILES)
                nc.vector.tensor_scalar(ms[:, :], sums[:, :], 1.0 / D, EPS, ALU.mult, ALU.add).then_inc(ms_done, 1)

            def invert(c):
                dve.wait_ge(rms_done, c)
                nc.vector.reciprocal(inv[:, :], rms[:, :]).then_inc(inv_done, 1)
                dve.wait_ge(extras_in, c * (16 * len(extras)))
                if not (isinstance(c, int) and c == 1):
                    dve.wait_ge(stored, (c - 1) * 16 if isinstance(c, int) else c * 16 - 16)
                dve.wait_ge(inv_done, c)

            def finish(c, i):
                nc.vector.scalar_tensor_tensor(res[:, i, :], kept[:, i, :], inv[:, i:i + 1],
                                               w_row[:, :], ALU.mult, ALU.mult).then_inc(adding, 1)
                for n in range(len(extras)):
                    dve.wait_ge(adding, (c - 1) * (TILES * len(extras)) + i * len(extras) + n + 1)
                    last = nc.vector.tensor_tensor(res[:, i, :], res[:, i, :], extra_in[:, n, i, :], ALU.add)
                    last.then_inc(adding if n + 1 < len(extras) else finished, 1)

            def chunk(c):
                if not isinstance(c, int):
                    keep(c)
                for f in range(FT):
                    gated(c, f + AHEAD)
                    low(c, f + AHEAD - 1)
                    if not isinstance(c, int):
                        if f == 1:
                            mean_squares(c)
                        if f == 3:
                            invert(c)
                        if f >= FT - TILES:
                            finish(c, f - (FT - TILES))

            for i in range(3):
                dve.wait_ge(w_rounded, i + 1)
                nc.vector.tensor_tensor(w_low[:, i, :], raw[:, i, :], w_high[:, i, :].bitcast(F32),
                                        ALU.subtract).then_inc(w_ready, 1)
            dve.wait_ge(row_in, 16)
            for f in range(AHEAD):
                gated(0, f)
                if f >= 1:
                    low(0, f - 1)
            chunk(0)
            with dve.Fori(1, CH, 1) as c:
                chunk(c)
            keep(CH)
            mean_squares(CH)
            invert(CH)
            for i in range(TILES):
                finish(CH, i)


def seq_preln(nc, x, u, v, wq, wk, wv, wo, w1, w2, w3, attn_w, ff_w, moe_w, router, ew1, ew2, ew3, out):
    batches, seq, _ = x.shape
    ntok = batches * seq
    pairs = u.shape[0] // P
    x = x.rearrange("b s d -> (b s) d")
    out = out.rearrange("b s d -> (b s) d")

    def scratch(name, shape):
        return nc.dram_tensor(name, shape, F32, kind="Internal").ap()

    packed = scratch("packed_factors", (pairs, P, 8 * D))
    x1 = scratch("x1", (ntok, D))
    x1_sparse = scratch("x1_sparse", (ntok, D))
    y_rows = scratch("y_rows", (ntok, D))
    h_rows = scratch("h_rows", (ntok, D))
    qk_high = scratch("qk_high", (4 * P, ntok))
    qk_low = scratch("qk_low", (4 * P, ntok))
    v_aug = scratch("v_aug", (ntok, HEADS * 2 * HD))

    with ExitStack() as whole:
        ident = whole.enter_context(nc.sbuf_tensor("ident", [P, P], F32))
        waited = whole.enter_context(nc.semaphore("waited"))
        stage_identity(nc, ident)
        with ExitStack() as ctx:
            zh = ctx.enter_context(nc.sbuf_tensor("z1_high", [P, KT, ntok], F32R))
            zl = ctx.enter_context(nc.sbuf_tensor("z1_low", [P, KT, ntok], F32R))
            with ExitStack() as inner:
                nat = [inner.enter_context(nc.sbuf_tensor(f"factor{i}", [P, pairs, D], F32)) for i in range(2)]
                factors_in = inner.enter_context(nc.semaphore("factors_in"))
                early = [(nat[i][:, :, :], f.rearrange("(c p) d -> p c d", p=P), factors_in)
                         for i, f in enumerate((u, v))]
                stage_layernorm(nc, "ln1", x, zh, zl, None, ident, early, ntok)
                stage_factors(nc, nat, factors_in, ident, packed, pairs)
            stage_pairs(nc, x, x1, zh, zl, packed, ident, waited, batches, seq, pairs)
        late = whole.enter_context(ExitStack())
        with ExitStack() as ctx:
            yh = ctx.enter_context(nc.sbuf_tensor("y_high", [P, KT, ntok], F32R))
            yl = ctx.enter_context(nc.sbuf_tensor("y_low", [P, KT, ntok], F32R))
            weights = ctx.enter_context(nc.sbuf_tensor("expert_weights", [P, ntok // P, EXPERTS], F32))
            ew = ExpertWeights(nc, ctx, ew1, ew2, ew3)
            with ExitStack() as held:
                qkv_raw = held.enter_context(nc.sbuf_tensor("qkv_raw", [P, 3, KT, D], F32))
                router_raw = held.enter_context(nc.sbuf_tensor("router_raw", [P, KT, EXPERTS], F32))
                qkv_in, router_in = (held.enter_context(nc.semaphore(n)) for n in ("qkv_in", "router_in"))
                early = [(qkv_raw[:, i, :, :], w.rearrange("(k p) n -> p k n", p=P), qkv_in)
                         for i, w in enumerate((wq, wk, wv))]
                stage_layernorm(nc, "ln2", x1, yh, yl, y_rows, ident, early, ntok)
                early = [(router_raw[:, :, :], router.rearrange("(k p) e -> p k e", p=P), router_in)]
                qkv_stores = stage_qkv(nc, held, yh, yl, qkv_raw, qkv_in, early, ew, waited, qk_high, qk_low, v_aug,
                                       ident, ntok)
                stage_router(nc, yh, yl, router_raw, router_in, weights, ident, qkv_stores, ntok)
            stage_experts(nc, yh, yl, ew, weights, moe_w, x1, x1_sparse, waited, ntok)
        late = whole.enter_context(ExitStack())
        with ExitStack() as ctx:
            o_raw = ctx.enter_context(nc.sbuf_tensor("o_raw", [P, batches * (HEADS // 4), seq], F32))
            stage_attention(nc, qk_high, qk_low, v_aug, o_raw, ident, waited, batches, seq)
            hh = late.enter_context(nc.sbuf_tensor("h_high", [P, KT, ntok], F32R, side="right"))
            hl = late.enter_context(nc.sbuf_tensor("h_low", [P, KT, ntok], F32R, side="right"))
            fw = FfnWeights(nc, late, w1, w2, w3)
            stage_attention_out(nc, o_raw, y_rows, wo, attn_w, hh, hl, h_rows, fw, ident, batches, seq)
        stage_ffn(nc, hh, hl, fw, ff_w, [h_rows, x1_sparse], out, waited, ntok)


_INS = ["L0_attn_qz", "L0_attn_ternary_factor_u", "L0_attn_ternary_factor_v", "L0_ffn_wq", "L0_ffn_wk", "L0_ffn_wv",
        "L0_ffn_wo", "L0_ffn_w1", "L0_ffn_w2", "L0_ffn_w3", "L0_ffn_attn_norm_w", "L0_ffn_ff_norm_w",
        "L0_ffn_moe_norm_w", "L0_ffn_router_w", "L0_ffn_ew1", "L0_ffn_ew2", "L0_ffn_ew3"]


def kernel(**inputs):
    import concourse.bacc as bacc
    from concourse.bass_utils import run_bass_kernel_spmd

    nc = bacc.Bacc("TRN2", target_bir_lowering=False, num_devices=1)
    arrays, args = {}, []
    for name in _INS:
        a = np.ascontiguousarray(inputs[name])
        arrays[name] = a
        args.append(nc.dram_tensor(name, a.shape, mybir.dt.from_np(a.dtype), kind="ExternalInput").ap())
    out = nc.dram_tensor("out", arrays["L0_attn_qz"].shape, F32, kind="ExternalOutput").ap()
    seq_preln(nc, *args, out)
    result = run_bass_kernel_spmd(nc, [arrays], core_ids=[0])
    return result.results[0]["out"]
```
